# Optimizing a Trainium2 kernel written in Bass

```python
import numpy as np
import jax
import jax.numpy as jnp

def _softmax(x, axis=-1):
    return jax.nn.softmax(x, axis=axis)

def _gelu(x):
    return jax.nn.gelu(x, approximate=True)

def _silu(x):
    return jax.nn.silu(x)

def _sigmoid(x):
    return jax.nn.sigmoid(x)

def _layernorm(x, axis=-1, eps=1e-05):
    m = jnp.mean(x, axis=axis, keepdims=True)
    v = jnp.var(x, axis=axis, keepdims=True)
    return (x - m) / jnp.sqrt(v + eps)

def _scatter_add(tgt, idx, src, axis=0):
    return tgt.at[idx].add(src)

def _segment_sum(src, seg, n):
    return jax.ops.segment_sum(src, seg, n)
kernel_name = 'mk_adaln_d1_jaxref_r4_25defa'

def setup_inputs(seed: int=0):
    np.random.seed(seed)
    _w = jnp.asarray

    def _L0_attn_setup():
        import jax, jax.numpy as jnp
        import numpy as np
        B, S, D = (2, 512, 256)
        H = 16
        HD = D // H
        WINDOW = 128
        SCALE = HD ** (-0.5)

        def _local_mask(seq_len):
            idx = jnp.arange(seq_len)
            band = jnp.abs(idx[:, None] - idx[None, :]) <= WINDOW // 2
            return jnp.where(band, 0.0, -jnp.inf).astype(jnp.float32)
        key = jax.random.key(seed)
        ks = jax.random.split(key, 5)
        x = jax.random.normal(ks[0], (B, S, D), dtype=jnp.float32)
        w_qkv = jax.random.normal(ks[1], (D, 3 * D), dtype=jnp.float32) * D ** (-0.5)
        b_qkv = jax.random.normal(ks[2], (3 * D,), dtype=jnp.float32) * 0.02
        w_out = jax.random.normal(ks[3], (D, D), dtype=jnp.float32) * D ** (-0.5)
        b_out = jax.random.normal(ks[4], (D,), dtype=jnp.float32) * 0.02
        return {'x': x, 'w_qkv': w_qkv, 'b_qkv': b_qkv, 'w_out': w_out, 'b_out': b_out}
    _L0_attn_in = _L0_attn_setup()

    def _L0_ffn_setup():
        import jax, jax.numpy as jnp
        import numpy as np
        B, S, H, I = (2, 512, 256, 128)
        E, K, G, TG = (64, 8, 8, 4)
        SCALE = 2.5
        CAP = 256
        key = jax.random.key(seed)
        ks = jax.random.split(key, 6)
        hidden_states = jax.random.normal(ks[0], (B, S, H), jnp.float32)
        gate_w = jax.random.normal(ks[1], (E, H), jnp.float32) * 0.02
        gate_bias = jax.random.normal(ks[2], (E,), jnp.float32) * 0.02
        w_gate = jax.random.normal(ks[3], (E, H, I), jnp.float32) * (1.0 / np.sqrt(H))
        w_up = jax.random.normal(ks[4], (E, H, I), jnp.float32) * (1.0 / np.sqrt(H))
        w_down = jax.random.normal(ks[5], (E, I, H), jnp.float32) * (1.0 / np.sqrt(I))
        return {'hidden_states': hidden_states, 'gate_w': gate_w, 'gate_bias': gate_bias, 'w_gate': w_gate, 'w_up': w_up, 'w_down': w_down}
    _L0_ffn_in = _L0_ffn_setup()
    _L0_c = _w((lambda *s: np.random.randn(*s).astype(np.float32) * 0.05)(8, 256))
    _L0_wmod = _w((lambda *s: np.random.randn(*s).astype(np.float32) * 0.05)(256, 6 * 256) * 256 ** (-0.5))
    _d = {'L0_attn_x': _L0_attn_in['x'], 'L0_attn_w_qkv': _L0_attn_in['w_qkv'], 'L0_attn_b_qkv': _L0_attn_in['b_qkv'], 'L0_attn_w_out': _L0_attn_in['w_out'], 'L0_attn_b_out': _L0_attn_in['b_out'], 'L0_ffn_gate_w': _L0_ffn_in['gate_w'], 'L0_ffn_gate_bias': _L0_ffn_in['gate_bias'], 'L0_ffn_w_gate': _L0_ffn_in['w_gate'], 'L0_ffn_w_up': _L0_ffn_in['w_up'], 'L0_ffn_w_down': _L0_ffn_in['w_down'], 'L0_c': _L0_c, 'L0_wmod': _L0_wmod}
    _x0 = _d['L0_attn_x']
    _d['L0_attn_x'] = jax.random.normal(jax.random.fold_in(jax.random.key(seed), 1), (8, 512, 256), dtype=_x0.dtype)
    del _x0
    return _d

def reference(L0_attn_x, L0_attn_w_qkv, L0_attn_b_qkv, L0_attn_w_out, L0_attn_b_out, L0_ffn_gate_w, L0_ffn_gate_bias, L0_ffn_w_gate, L0_ffn_w_up, L0_ffn_w_down, L0_c, L0_wmod):

    def _L0_attn_ref(x, w_qkv, b_qkv, w_out, b_out):
        import jax, jax.numpy as jnp
        import numpy as np
        B, S, D = (2, 512, 256)
        H = 16
        HD = D // H
        WINDOW = 128
        SCALE = HD ** (-0.5)

        def _local_mask(seq_len):
            idx = jnp.arange(seq_len)
            band = jnp.abs(idx[:, None] - idx[None, :]) <= WINDOW // 2
            return jnp.where(band, 0.0, -jnp.inf).astype(jnp.float32)
        b, s, _ = x.shape
        qkv = x @ w_qkv + b_qkv
        qkv = qkv.reshape(b, s, 3, H, HD).transpose(2, 0, 3, 1, 4)
        q, k, v = (qkv[0], qkv[1], qkv[2])
        mask = _local_mask(s)
        scores = jnp.einsum('bhqd,bhkd->bhqk', q, k) * SCALE + mask
        attn = jax.nn.softmax(scores, axis=-1)
        out = jnp.einsum('bhqk,bhkd->bhqd', attn, v)
        out = out.transpose(0, 2, 1, 3).reshape(b, s, D)
        return out @ w_out + b_out

    def _L0_ffn_ref(hidden_states, gate_w, gate_bias, w_gate, w_up, w_down):
        import jax, jax.numpy as jnp
        import numpy as np
        B, S, H, I = (2, 512, 256, 128)
        E, K, G, TG = (64, 8, 8, 4)
        SCALE = 2.5
        CAP = 256
        b, s, h = hidden_states.shape
        x = hidden_states.reshape(-1, h)
        n = x.shape[0]
        logits = x.astype(jnp.float32) @ gate_w.astype(jnp.float32).T
        scores = jax.nn.sigmoid(logits)
        sfc = scores + gate_bias[None, :]
        group_scores = jax.lax.top_k(sfc.reshape(n, G, E // G), 2)[0].sum(-1)
        gidx = jax.lax.top_k(group_scores, TG)[1]
        gmask = jnp.zeros((n, G), bool).at[jnp.arange(n)[:, None], gidx].set(True)
        smask = jnp.repeat(gmask, E // G, axis=1)
        tmp = jnp.where(smask, sfc, -jnp.inf)
        topk_idx = jax.lax.top_k(tmp, K)[1]
        topk_w = jnp.take_along_axis(scores, topk_idx, axis=1)
        topk_w = topk_w / (topk_w.sum(-1, keepdims=True) + 1e-20)
        topk_w = topk_w * SCALE
        e = topk_idx.reshape(-1)
        token = jnp.repeat(jnp.arange(n), K)
        oh = jax.nn.one_hot(e, E, dtype=jnp.int32)
        pos = jnp.take_along_axis(jnp.cumsum(oh, 0) - 1, e[:, None], 1)[:, 0]
        valid = pos < CAP
        pos_c = jnp.where(valid, pos, CAP)
        buf = jnp.zeros((E, CAP + 1, h), x.dtype).at[e, pos_c].set(x[token])[:, :CAP]
        g = jnp.einsum('ech,ehi->eci', buf, w_gate)
        u = jnp.einsum('ech,ehi->eci', buf, w_up)
        y = jnp.einsum('eci,eih->ech', jax.nn.silu(g) * u, w_down)
        y_slots = y[e, jnp.minimum(pos, CAP - 1)]
        w_slot = topk_w.reshape(-1) * valid.astype(topk_w.dtype)
        out = jnp.zeros((n, h), jnp.float32).at[token].add(y_slots * w_slot[:, None])
        return out.reshape(b, s, h)
    x = L0_attn_x
    mod = (_silu(L0_c) @ L0_wmod).reshape(L0_c.shape[0], 6, 1, -1)
    sa, ca, ga, sb, cb, gb = (mod[:, 0], mod[:, 1], mod[:, 2], mod[:, 3], mod[:, 4], mod[:, 5])
    ga = (2 * (ga >= 0) - 1) * jnp.maximum(jnp.abs(ga), 0.25)
    gb = (2 * (gb >= 0) - 1) * jnp.maximum(jnp.abs(gb), 0.25)
    h = _layernorm(x, axis=-1) * (1 + ca) + sa
    x = x + ga * _L0_attn_ref(h, L0_attn_w_qkv, L0_attn_b_qkv, L0_attn_w_out, L0_attn_b_out)
    h = _layernorm(x, axis=-1) * (1 + cb) + sb
    x = x + gb * _L0_ffn_ref(h, L0_ffn_gate_w, L0_ffn_gate_bias, L0_ffn_w_gate, L0_ffn_w_up, L0_ffn_w_down)
    return x

_drawn_inputs = setup_inputs


def setup_inputs(seed=0):
    import zlib

    import numpy as np

    out = dict(_drawn_inputs(seed))
    spreads = {}
    factors = {'L0_attn_b_qkv': 4.962, 'L0_attn_b_out': 5.555}
    for name, (base, spread) in spreads.items():
        noise = np.random.default_rng([zlib.crc32(name.encode()), seed]).standard_normal(out[name].shape)
        drawn = base * np.exp(spread * noise) if base else spread * noise
        out[name] = jnp.asarray(drawn.astype(out[name].dtype))
    for name, factor in factors.items():
        out[name] = (out[name] * factor).astype(out[name].dtype)
    return out
```

```python
from contextlib import ExitStack

import concourse.bass as bass
from concourse import mybir

F32 = mybir.dt.float32
BF16 = mybir.dt.bfloat16
F16 = mybir.dt.float16
I32 = mybir.dt.int32
U32 = mybir.dt.uint32
ALU = mybir.AluOpType
ACT = mybir.ActivationFunctionType
AX_X = mybir.AxisListType.X

P = 128
B, S, D = 8, 512, 256
H, HD, BAND = 16, 16, 64
E, K, G, TG = 64, 8, 8, 4
CAP, I = 256, 128
N = B * S
T = S // P
C = D // P
U = T + 1
KW = S + 2 * BAND
QUADS, HQ = H // 4, 4
SLOTS = QUADS * U
EG = E // G
SCALE = float(HD) ** -0.5
EPS = 1e-5
ROUTE_SCALE = 2.5
HW = D + E
LO, HI = 16, CAP // 16
FAR = 16.0 * 256
NEG = -1e30
TAKEN = -3e38
PAIRS = [(0, 0), (0, 1), (1, 0), (1, 1), (0, 2), (2, 0)]
MROW = len(PAIRS) * HD
KROWS = MROW + 2
NPT = 4
SEL_BEFORE = [0, 1, 3, 5, 7]
SEL_OF = [1, 2, 2, 2, 1]

PER = dict(
    xn=T, mcol=1, stats=T, aggr=T, rstd=2, hTp=C, hT=C, proj=4, p32=4, hpart=4, r32=4, mpart=4,
    lpart=4, vp=3, v=3, Sp=8 * QUADS, smax=2 * 8 * QUADS, m2=2 * QUADS, mTp=QUADS, mT=QUADS, STp=10 * QUADS,
    exp=10 * QUADS, cut=16 * QUADS, pv=10 * QUADS, oTs=QUADS, oTp=QUADS, rec=QUADS, on=QUADS,
    onTp=C, onT=C, op=2, t1=2, xb=2, x1=2, stats2=T, aggr2=T, rstd2=2, xn2=T, h2=2, h2Tp=C, h2T=C,
    lg=1, ex=1, route=38, pre=T + 1, vt=1, cntp=1, pos=4, oneh=3 * T, idxp=2, idx=2,
    qk_ld=192, mt_st=64, mrow_ld=64, c_ld=32, x1_st=16, h_st=16,
)


class Batch:

    def __init__(self, b, half, par):
        self.b, self.half, self.par = b, half, par


def batch(b):
    return Batch(b, b // 2, b % 2)


def build(nc, x, w_qkv, b_qkv, w_out, b_out, gate_w, gate_bias, w_gate, w_up, w_down, c, wmod, out):
    with ExitStack() as ctx:
        sems = {name: ctx.enter_context(nc.semaphore("s_" + name)) for name in PER}

        def sem(name):
            return ctx.enter_context(nc.semaphore(name))

        def ps(name, n=512):
            return ctx.enter_context(nc.psum_tensor(name, [P, n], F32))

        def dram(name, shape, dt=F32):
            return nc.dram_tensor(name, shape, dt, kind="Internal").ap()

        def hold(eng, s, v):
            if not isinstance(v, int):
                eng.compute_val(v)
                eng.wait_ge(s_const, NCONST)
            eng.wait_ge(s, v)

        def need(eng, s, v):
            if not isinstance(v, int) or v > 0:
                eng.wait_ge(s, v)

        def after(eng, name, bt, k, apart=False):
            v = bt.b * PER[name] + k
            if isinstance(v, int) and v <= 0:
                return
            if apart or eng is nc.sync or eng is nc.gpsimd:
                hold(eng, sems[name], v)
            else:
                eng.wait_ge(sems[name], v)

        def parts_stored(eng, bt, j, k):
            v = bt.b * 32 + 16 * k
            if isinstance(v, int) and v <= 0:
                return
            hold(eng, parts_st[j % 2], v)

        s_par = sem("params_loaded")
        s_par2 = sem("wmod_loaded")
        s_const = sem("constants_made")
        s_pe0 = sem("start_products")
        s_v0 = sem("start_vector_steps")
        s_a0 = sem("start_scalar_steps")
        s_mod_st = sem("mod_rows_stored")
        s_zero = sem("accumulators_zeroed")
        parts_st = [sem("parts_stored_even"), sem("parts_stored_odd")]
        x_ld = [sem("x_loaded_even"), sem("x_loaded_odd")]
        s_ix = sem("index_steps")
        s_i2 = sem("index_sums")
        s_ix2 = sem("operand_constants")
        s_v1 = sem("gate_steps")
        s_tab_st = sem("tables_stored")
        s_tab_ld = sem("tables_loaded")
        s_tabT = sem("tables_turned")

        def sbt(stack, name, shape, dt=F32):
            return stack.enter_context(nc.sbuf_tensor(name, shape, dt))

        ident = sbt(ctx, "ident", [P, P])
        iacc = sbt(ctx, "iacc", [P, G, EG, LO])
        zero = sbt(ctx, "zero", [P, 512])

        bS = [ps("scores0"), ps("scores1")]
        bST = [ps("scoresT0"), ps("scoresT1")]
        bO = ps("outT")
        bT = ps("turns")
        bA = ps("stageA")
        bC = ps("stageC")

        parts_d = [dram(f"parts_d{i}", [2, 3, D, S], BF16) for i in range(2)]
        mt_d = dram("mt_d", [2 * HQ * T, P], BF16)
        mod_d = dram("mod_d", [B, 4, D])
        x1_d = dram("x1_d", [B, S, D])
        htab = dram("htab", [N, HW])
        tab_d = [dram("gather_tab", [E, CAP]), dram("scatter_tab", [E, CAP])]
        ACCROWS = N + CAP
        acc_d = [dram(f"acc_d{i}", [ACCROWS, D]) for i in range(4)]

        att = ExitStack()
        sb = lambda name, shape, dt=F32: sbt(att, name, shape, dt)
        identb = sb("identb", [P, P], BF16)
        onesb = sb("onesb", [P, P], BF16)
        before = sb("before", [P, P], BF16)
        mask = sb("mask", [P, 3, 2 * P], BF16)
        iota16 = sb("iota16", [P, LO], I32)
        lowerg = sb("lowerg", [P, G, G])
        valt = sb("valt", [P, N // P])
        half_c = sb("half_c", [P, T])
        wqkv = sb("wqkv", [P, C, 3 * D])
        wo = sb("wo", [P, C, D])
        bqk = sb("bqk", [P, 4])
        bv = sb("bv", [P, D])
        bo = sb("bo", [P, D])
        gwT = sb("gwT", [P, C, E])
        gb = sb("gbias", [P, E])
        silT = sb("silT", [P, C, B])
        modT = sb("modT", [P, B, 4])
        xt = sb("xt", [P, T, D])
        xn = sb("xn", [P, T, D])
        stats = sb("stats", [P, T, 6])
        mv = sb("mv", [P, T, 2])
        ve = sb("ve", [P, T])
        rs = sb("rs", [P, T])
        mcol = sb("mcol", [P, 4])
        hT = sb("hT", [P, C, KW])
        p32 = [sb(f"p32_{i}", [P, S]) for i in range(2)]
        r32 = sb("r32", [P, S])
        parts = sb("parts", [P, 2, 3, S], BF16)
        Qs = [sb(f"Qs{i}", [P, H, S], BF16) for i in range(2)]
        Ks = [sb(f"Ks{i}", [P, H, KW], BF16) for i in range(2)]
        Va = [sb(f"Va{i}", [P, U, H, 32]) for i in range(2)]
        junk = sb("junk", [P, 2, 2 * P], BF16)
        mrowmax = sb("mrowmax", [P, HQ, T])
        M2 = sb("M2", [P, P], BF16)
        MT = sb("MT", [32, P], BF16)
        PT = [sb(f"PT{i}", [P, 2, 2 * P]) for i in range(NPT)]
        OTs = sb("OTs", [P, S])
        rec = sb("rec", [P, T, HQ])
        on = sb("on", [P, T, D])
        onT = sb("onT", [P, C, S])
        xc = sb("xc", [P, T, D])
        mr = sb("mr", [P, 3, D])
        gbo = sb("gbo", [P, D])
        x1 = sb("x1", [P, T, D])
        stats2 = sb("stats2", [P, T, 6])
        mv2 = sb("mv2", [P, T, 2])
        ve2 = sb("ve2", [P, T])
        rs2 = sb("rs2", [P, T])
        H2 = sb("H2", [P, T, HW])
        xn2 = H2[:, :, 0:D]
        h2T = onT
        ex = sb("ex", [P, T * E])
        sc = sb("sc", [P, T * E])
        sfc = sb("sfc", [P, T * G, EG])
        tmp = sb("tmp", [P, T * G, EG])
        rep = sb("rep", [P, T * G, EG])
        pairs = sb("pairs", [P, 6, T * G, 4])
        gs = sb("gs", [P, 4, T * G])
        cmp1 = sb("cmp1", [P, T, G, G])
        cmp2 = sb("cmp2", [P, T, G, G])
        top8 = sb("top8", [P, T, 8])
        selb = sb("selb", [P, T * E], BF16)
        wsum = sb("wsum", [P, 3, T])
        Spre = sb("Spre", [P, T + 1, E], BF16)
        posf = ex
        posi = sb("posi", [P, 3, T * E], I32)
        vt = sb("vt", [P, T])
        oneh = sb("oneh", [P, T + T + 1, E, 16], F16)
        wm = oneh[:, 0:6].rearrange("p a e b -> p (a e b)").bitcast(F32).rearrange("p (c n) -> p c n", c=C)
        gw = on[0:E, 0, :]
        cin = xc[0:B, 0, :]
        sil = x1[0:B, 0:3, :]
        gates = onT[0:B, :, :].rearrange("b i (k d) -> b i k d", k=2)
        att.close()

        moe = ExitStack()
        sb = lambda name, shape, dt=F32: sbt(moe, name, shape, dt)
        NW, NX, NY = 4, 4, 4
        dmask = sb("dmask", [P, EG, LO])
        post = sb("post", [P, G, LO], I32)
        iv = sb("iv", [P, 6, G, LO])
        tabs = sb("tabs", [P, 2, P])
        gidx = sb("gidx", [P, 2 * E], U32)
        sidx = sb("sidx", [P, 2 * E], U32)
        gstage = sb("gstage", [P, 4, 2], U32)
        sstage = sb("sstage", [P, 4, 2], U32)
        wgu = [sb(f"wgu{i}", [P, 2, C, I]) for i in range(NW)]
        wd = [sb(f"wd{i}", [P, D]) for i in range(NW)]
        xg = [sb(f"xg{i}", [P, 2, HW]) for i in range(NX)]
        wcol = [sb(f"wcol{i}", [P, 2]) for i in range(NX)]
        xgT = [sb(f"xgT{i}", [P, C, CAP]) for i in range(2)]
        sg = [sb(f"sg{i}", [P, CAP]) for i in range(2)]
        hm = [sb(f"hm{i}", [P, CAP]) for i in range(2)]
        ys = [sb(f"ys{i}", [P, 2, D]) for i in range(NY)]
        fx = [sb(f"fx{i}", [P, T, D]) for i in range(2)]
        fa = [sb(f"fa{i}", [P, 4, T, D]) for i in range(2)]
        fg = [sb(f"fg{i}", [P, D]) for i in range(2)]
        fo = [sb(f"fo{i}", [P, T, D]) for i in range(2)]
        moe.close()
        eng_moe = dict(
            w_ld=[sem(f"weights_loaded{i}") for i in range(NW)],
            x_ld=[sem(f"rows_gathered{i}") for i in range(NX)],
            y_st=[sem(f"rows_added{i}") for i in range(NY)],
            gst=sem("gather_indices_staged"), sst=sem("scatter_indices_staged"),
            xTp=sem("rows_turned"), xTc=sem("first_features_kept"), xTd=sem("second_features_kept"), gp=sem("gate_up_made"),
            sg=sem("silu_done"), wc=sem("slot_weights_staged"),
            hm=sem("hidden_done"), yp=sem("expert_out_made"), yc=sem("expert_out_scaled"),
            f_ld=[sem("last_loads_even"), sem("last_loads_odd")], fsum=sem("last_sums"), f_st=sem("out_stored"),
        )
        mo = eng_moe

        NCONST = 17
        block = ctx.enter_context(nc.Block())

        def loops(eng, body, prolog=None, epilog=None):
            body(None, batch(0), batch(1))
            with eng.Fori(0, (B - 2) // 2) as it:
                for j in range(2):
                    now = Batch(it * 2 + (1 + j), it + j, 1 - j)
                    prev = Batch(it * 2 + j, it, j)
                    nxt = Batch(it * 2 + (2 + j), it + 1, j)
                    body(prev, now, nxt)
            body(batch(B - 2), batch(B - 1), None)

        @block.sync
        def _(sp):
            bc = lambda ap, n: ap.rearrange("(o d) -> o d", o=1).to_broadcast([P, n])
            sp.dma_start(xt[:], x[0].rearrange("(t p) d -> p t d", p=P)).then_inc(x_ld[0], 16)
            sp.dma_start(cin, c[:, :]).then_inc(s_par, 16)
            sp.dma_start(wm, wmod.rearrange("(c p) n -> p c n", p=P)).then_inc(s_par2, 16)
            sp.dma_start(wqkv[:], w_qkv.rearrange("(c p) n -> p c n", p=P)).then_inc(s_par, 16)
            sp.dma_start(bqk[:], b_qkv[0:4 * P].rearrange("(c p) -> p c", p=P),
                         allow_slow_non_contiguous=True).then_inc(s_par, 16)
            sp.dma_start(bv[:], bc(b_qkv[2 * D:3 * D], D)).then_inc(s_par, 16)
            sp.dma_start(bo[:], bc(b_out, D)).then_inc(s_par, 16)
            sp.dma_start(gb[:], bc(gate_bias, E)).then_inc(s_par, 16)
            sp.dma_start(gw, gate_w[:, :]).then_inc(s_par, 16)
            sp.dma_start(wo[:], w_out.rearrange("(c p) n -> p c n", p=P)).then_inc(s_par, 16)
            sp.wait_ge(s_v0, 9)
            sp.dma_start(mod_d[:, 0:4:3, :], gates[:, 0, :, :]).then_inc(s_mod_st, 16)
            sp.dma_start(mod_d[:, 1:3, :], gates[:, 1, :, :]).then_inc(s_mod_st, 16)
            sp.wait_ge(s_const, NCONST)
            for i in range(4):
                for r in range(0, ACCROWS, 2 * P):
                    n = min(2 * P, ACCROWS - r)
                    sp.dma_start(acc_d[i][r:r + n, :].rearrange("(p a) d -> p (a d)", p=P),
                                 zero[:, 0:n * D // P]).then_inc(s_zero, 16)

            def load_x(bt):
                after(sp, "xn", bt, 0)
                row = x[bass.ds(bt.b, 1)] if not isinstance(bt.b, int) else x[bt.b:bt.b + 1]
                sp.dma_start(xt[:], row.rearrange("o (t p) d -> p (o t) d", p=P)).then_inc(x_ld[bt.par], 16)

            def load_c(bt):
                after(sp, "h2", bt, 0)
                after(sp, "x1", bt, 0)
                i = bass.ds(bt.b, 1) if not isinstance(bt.b, int) else slice(bt.b, bt.b + 1)
                sp.dma_start(xc[:], x[i].rearrange("o (t p) d -> p (o t) d", p=P)).then_inc(sems["c_ld"], 16)
                sp.dma_start(mr[:], mod_d[i, 0:3, :].rearrange("o k d -> o (k d)").to_broadcast([P, 3 * D])
                             ).then_inc(sems["c_ld"], 16)

            def store_parts(bt, j):
                after(sp, "lpart", bt, j + 1)
                after(sp, "mpart", bt, j + 1)
                after(sp, "hpart", bt, j + 1)
                if j % 2 == 0:
                    after(sp, "qk_ld", bt, 0)
                dst = parts_d[bt.par][j // 2, :, (j % 2) * P:(j % 2 + 1) * P, :]
                sp.dma_start(dst.rearrange("k p s -> p k s"), parts[:, j % 2, :, :]).then_inc(parts_st[j % 2], 16)

            def load_stack(bt, which):
                parts_stored(sp, bt, 0, which + 1)
                parts_stored(sp, bt, 1, which + 1)
                if not isinstance(bt.b, int) or bt.b >= 2:
                    after(sp, "STp", Batch(bt.b - 1, 0, 0), 0)
                dst = Qs[bt.par] if which == 0 else Ks[bt.par]
                lo = 0 if which == 0 else BAND
                for n, pair in enumerate(PAIRS):
                    src = parts_d[bt.par][which, pair[which]].rearrange("(h d) s -> d h s", d=HD)
                    sp.dma_start(dst[n * HD:(n + 1) * HD, :, lo:lo + S], src).then_inc(sems["qk_ld"], 16)

            def mrows(bt, g):
                after(sp, "mT", bt, g + 1)
                sp.dma_start(mt_d[:, :], MT[:]).then_inc(sems["mt_st"], 16)
                after(sp, "mt_st", bt, 16 * (g + 1))
                sp.dma_start(Qs[bt.par][MROW:KROWS, HQ * g:HQ * g + HQ, :].rearrange("a h q -> a (h q)"),
                             mt_d.rearrange("(a r) q -> a (r q)", a=2)).then_inc(sems["mrow_ld"], 16)

            def body(prev, now, nxt):
                for slot in range(SLOTS):
                    g, u = divmod(slot, U)
                    if slot == 0 and nxt:
                        load_x(nxt)
                    if slot == 0 and prev:
                        load_c(prev)
                    if nxt and 5 <= slot <= 8:
                        store_parts(nxt, slot - 5)
                    if nxt and slot in (7, 9):
                        load_stack(nxt, (slot - 7) // 2)
                    if u == 3 and (g < QUADS - 1 or nxt):
                        mrows(*((now, g + 1) if g < QUADS - 1 else (nxt, 0)))
                    if prev and slot == 13:
                        store_c(prev, 0)
                    if prev and slot == 17:
                        store_c(prev, 1)

            def store_c(bt, which):
                i = bass.ds(bt.b, 1) if not isinstance(bt.b, int) else slice(bt.b, bt.b + 1)
                if which == 0:
                    after(sp, "x1", bt, 2)
                    sp.dma_start(x1_d[i].rearrange("o (t p) d -> p (o t) d", p=P), x1[:]).then_inc(sems["x1_st"], 16)
                else:
                    after(sp, "route", bt, PER["route"])
                    after(sp, "h2", bt, 2)
                    sp.dma_start(htab.rearrange("(b t p) d -> b p t d", p=P, t=T)[i].rearrange("o p t d -> p (o t) d"),
                                 H2[:]).then_inc(sems["h_st"], 16)

            first = batch(0)
            for j in range(4):
                store_parts(first, j)
                if j % 2:
                    load_stack(first, j // 2)
            mrows(first, 0)
            sp.wait_ge(s_mod_st, 32)
            loops(sp, body)
            last = batch(B - 1)
            load_c(last)
            store_c(last, 0)
            store_c(last, 1)

            sp.wait_ge(s_ix, 8)
            for k in range(2):
                for g in range(G):
                    sp.dma_start(tab_d[k].rearrange("(g e) (a b) -> g (e a) b", g=G, b=LO)[g], iv[:, 4 + k, g, :]
                                 ).then_inc(s_tab_st, 16)
            sp.wait_ge(s_tab_st, 32 * G)
            for k in range(2):
                sp.dma_start(tabs[:, k, :], tab_d[k].rearrange("e (h p) -> (e h) p", h=2)).then_inc(s_tab_ld, 16)

            def load_w(e, half, n):
                sp.dma_start(wgu[n][:, 0], w_gate[e].rearrange("o (c p) i -> p (o c) i", p=P)).then_inc(mo["w_ld"][n], 16)
                sp.dma_start(wgu[n][:, 1], w_up[e].rearrange("o (c p) i -> p (o c) i", p=P)).then_inc(mo["w_ld"][n], 16)
                sp.dma_start(wd[n][:], w_down[e].rearrange("o i d -> i (o d)")).then_inc(mo["w_ld"][n], 16)

            for n in range(NW):
                load_w(slice(n, n + 1), 0, n)
            with sp.Fori(1, E // NW) as it:
                for n in range(NW):
                    hold(sp, mo["yp"], it * NW + (n - NW + 1))
                    load_w(bass.ds(it * NW + n, 1), it, n)

            def load_f(i, half, par):
                src = lambda t: t.rearrange("o (t p) d -> p (o t) d", p=P)
                sp.dma_start(fx[par][:], src(x1_d[i])).then_inc(mo["f_ld"][par], 16)
                sp.dma_start(fg[par][:], mod_d[i, 3, :].to_broadcast([P, D])).then_inc(mo["f_ld"][par], 16)
                for k in range(4):
                    sp.dma_start(fa[par][:, k], src(acc_d[k][0:N, :].rearrange("(b s) d -> b s d", b=B)[i])
                                 ).then_inc(mo["f_ld"][par], 16)

            def store_f(i, count, par):
                hold(sp, mo["fsum"], count)
                sp.dma_start(out[i].rearrange("o (t p) d -> p (o t) d", p=P), fo[par][:]).then_inc(mo["f_st"], 16)

            for n in range(NY):
                sp.wait_ge(mo["y_st"][n], 32 * E // NY)
            load_f(slice(0, 1), 0, 0)
            load_f(slice(1, 2), 0, 1)
            with sp.Fori(1, B // 2) as it:
                for par in range(2):
                    store_f(bass.ds((it - 1) * 2 + par, 1), (it - 1) * 10 + (5 * par + 5), par)
                    load_f(bass.ds(it * 2 + par, 1), it, par)
            store_f(slice(B - 2, B - 1), 5 * B - 5, 0)
            store_f(slice(B - 1, B), 5 * B, 1)
            sp.wait_ge(mo["f_st"], 16 * B)

        @block.gpsimd
        def _(pool):
            gp = nc.gpsimd
            n = [0]
            nothing = pool.to_reg(0.0)
            last_row = pool.to_reg(N - 1)
            last_acc = pool.to_reg(ACCROWS - 1)

            def const(ins):
                ins.then_inc(s_const, 1)
                n[0] += 1
                pool.wait_ge(s_const, n[0])

            const(gp.memset(ident[:], 0.0))
            const(gp.affine_select(out=ident[:], in_=ident[:], compare_op=ALU.not_equal, fill=1.0, base=0,
                                   pattern=[[-1, P]], channel_multiplier=1))
            const(gp.tensor_copy(identb[:], ident[:]))
            const(gp.memset(onesb[:], 1.0))
            const(gp.affine_select(out=before[:], in_=onesb[:], compare_op=ALU.is_gt, fill=0.0, base=0,
                                   pattern=[[1, P]], channel_multiplier=-1))
            const(gp.memset(mask[:], 0.0))
            const(gp.affine_select(out=mask[:], in_=mask[:], compare_op=ALU.is_ge, fill=NEG, base=0,
                                   pattern=[[0, 3], [1, 2 * P]], channel_multiplier=-1))
            const(gp.affine_select(out=mask[:], in_=mask[:], compare_op=ALU.is_ge, fill=NEG, base=2 * BAND,
                                   pattern=[[0, 3], [-1, 2 * P]], channel_multiplier=1))
            const(gp.memset(mask[:, 0, 0:BAND], NEG))
            const(gp.memset(mask[:, 2, 2 * P - BAND:2 * P], NEG))
            const(gp.iota(iota16[:], pattern=[[1, LO]], base=0, channel_multiplier=0))
            const(gp.memset(lowerg[:], 1.0))
            const(gp.affine_select(out=lowerg[:], in_=lowerg[:], compare_op=ALU.is_gt, fill=0.0, base=0,
                                   pattern=[[1, G], [-1, G]], channel_multiplier=0))
            half = N // P // 2
            const(gp.iota(valt[:, 0:half], pattern=[[P, half]], base=1, channel_multiplier=1,
                          allow_small_or_imprecise_dtypes=True))
            const(gp.iota(valt[:, half:], pattern=[[-P, half]], base=-1, channel_multiplier=-1,
                          allow_small_or_imprecise_dtypes=True))
            const(gp.memset(half_c[:], -0.5))
            const(gp.memset(zero[:], 0.0))
            assert n[0] == NCONST

            def a_rstd(bt):
                after(pool, "aggr", bt, T)
                after(pool, "xn", bt, 0)
                gp.tensor_scalar(ve[:], mv[:, :, 1], EPS, None, ALU.add).then_inc(sems["rstd"], 1)
                after(pool, "rstd", bt, 1)
                gp.tensor_tensor(rs[:], ve[:], half_c[:], ALU.pow).then_inc(sems["rstd"], 1)

            def a_split(bt, j):
                after(pool, "hpart", bt, j + 1)
                parts_stored(pool, bt, j, j // 2)
                after(pool, "lpart", bt, j)
                gp.tensor_tensor(r32[:], p32[j % 2][:], parts[:, j % 2, 0, :], ALU.subtract).then_inc(sems["r32"], 1)
                gp.tensor_tensor(parts[:, j % 2, 1, :], p32[j % 2][:], parts[:, j % 2, 0, :], ALU.subtract
                                 ).then_inc(sems["mpart"], 1)
                after(pool, "r32", bt, j + 1)
                after(pool, "mpart", bt, j + 1)
                gp.tensor_tensor(parts[:, j % 2, 2, :], r32[:], parts[:, j % 2, 1, :], ALU.subtract).then_inc(sems["lpart"], 1)

            def cuts(bt, g, u):
                for p in range(2):
                    m = 10 * g + 2 * u + p
                    pt = PT[m % NPT]
                    after(pool, "exp", bt, m + 1)
                    if u > 0:
                        v = pt[:, :, 0:P]
                        gp.affine_select(out=v, in_=v, compare_op=ALU.is_ge, fill=nothing, base=0,
                                         pattern=[[0, 2], [1, P]], channel_multiplier=-1).then_inc(sems["cut"], 1)
                    if u < U - 1:
                        v = pt[:, :, 0:P] if u == 0 else pt[:, :, P:2 * P]
                        gp.affine_select(out=v, in_=v, compare_op=ALU.is_ge, fill=nothing, base=0,
                                         pattern=[[0, 2], [-1, P]], channel_multiplier=1).then_inc(sems["cut"], 1)

            def c_xb(bt):
                after(pool, "c_ld", bt, 32)
                after(pool, "xb", bt, 0)
                gp.tensor_tensor(gbo[:], mr[:, 0, :], bo[:], ALU.mult).then_inc(sems["xb"], 1)
                after(pool, "xb", bt, 1)
                gp.tensor_tensor(xc[:], xc[:], gbo[:, :].unsqueeze(1).to_broadcast([P, T, D]), ALU.add
                                 ).then_inc(sems["xb"], 1)

            def c_rstd(bt):
                after(pool, "aggr2", bt, T)
                after(pool, "xn2", bt, 0)
                gp.tensor_scalar(ve2[:], mv2[:, :, 1], EPS, None, ALU.add).then_inc(sems["rstd2"], 1)
                after(pool, "rstd2", bt, 1)
                gp.tensor_tensor(rs2[:], ve2[:], half_c[:], ALU.pow).then_inc(sems["rstd2"], 1)

            def c_mod(bt, k):
                if k == 0:
                    after(pool, "xn2", bt, T)
                    gp.tensor_tensor(xn2, xn2, mr[:, 2, :].unsqueeze(1).to_broadcast([P, T, D]), ALU.mult
                                     ).then_inc(sems["h2"], 1)
                else:
                    after(pool, "h2", bt, 1)
                    gp.tensor_tensor(xn2, xn2, mr[:, 1, :].unsqueeze(1).to_broadcast([P, T, D]), ALU.add
                                     ).then_inc(sems["h2"], 1)

            def body(prev, now, nxt):
                for slot in range(SLOTS):
                    g, u = divmod(slot, U)
                    cuts(now, g, u)
                    if nxt and slot == 0:
                        a_rstd(nxt)
                    if nxt and 4 <= slot <= 7:
                        a_split(nxt, slot - 4)
                    if prev and slot == 2:
                        c_xb(prev)
                    if prev and slot == 9:
                        c_rstd(prev)
                    if prev and slot in (10, 11):
                        c_mod(prev, slot - 10)

            pool.wait_ge(s_par, 16 * 8)
            a_rstd(batch(0))
            for j in range(4):
                a_split(batch(0), j)
            loops(pool, body)
            last = batch(B - 1)
            c_xb(last)
            c_rstd(last)
            c_mod(last, 0)
            c_mod(last, 1)

            done = Batch(B, 0, 0)
            after(pool, "h2Tp", done, 0)
            after(pool, "idx", done, 0)
            gp.memset(dmask[:], 1.0).then_inc(s_ix, 1)
            pool.wait_ge(s_ix, 1)
            gp.affine_select(out=dmask[:], in_=dmask[:], compare_op=ALU.is_ge, fill=0.0, base=0,
                             pattern=[[-HI, EG], [0, LO]], channel_multiplier=1).then_inc(s_ix, 1)
            pool.wait_ge(s_ix, 2)
            gp.affine_select(out=dmask[:], in_=dmask[:], compare_op=ALU.is_ge, fill=0.0, base=HI - 1,
                             pattern=[[HI, EG], [0, LO]], channel_multiplier=-1).then_inc(s_ix, 1)
            gp.iota(post[:], pattern=[[0, G], [1, LO]], base=0, channel_multiplier=LO).then_inc(s_ix, 1)

            def gather(n4, count_half):
                for h in range(2):
                    pool.indirect_dma_start(
                        out=xg[n4][:, h, :], out_offset=None, in_=htab[:, :],
                        in_offset=bass.IndirectOffsetOnAxis(ap=gstage[:, n4, h:h + 1], axis=0),
                        bounds_check=last_row, oob_is_err=False).then_inc(mo["x_ld"][n4], 16)

            def scatter(n4):
                for h in range(2):
                    pool.indirect_dma_start(
                        out=acc_d[2 * (n4 % 2) + h][:, :], in_=ys[n4][:, h, :], in_offset=None,
                        out_offset=bass.IndirectOffsetOnAxis(ap=sstage[:, n4, h:h + 1], axis=0),
                        bounds_check=last_acc, oob_is_err=True, compute_op=ALU.add).then_inc(mo["y_st"][n4], 16)

            after(pool, "h_st", done, 0)
            pool.wait_ge(s_zero, 16 * 4 * (ACCROWS // (2 * P)))
            pool.wait_ge(mo["gst"], NX)
            for n4 in range(3):
                gather(n4, 0)
            with pool.Fori(0, E // 4 - 1) as it:
                for n4 in range(4):
                    m4 = (n4 + 3) % 4
                    hold(pool, mo["gst"], it * 4 + (n4 + 4))
                    hold(pool, mo["gp"], it * 4 + n4)
                    hold(pool, mo["wc"], it * 4 + n4)
                    gather(m4, 0)
                    hold(pool, mo["sst"], it * 4 + (n4 + 1))
                    hold(pool, mo["yc"], it * 8 + (2 * n4 + 2))
                    if n4 >= 2:
                        hold(pool, mo["y_st"][n4 - 2], it * 32 + 32)
                    else:
                        hold(pool, mo["y_st"][n4 + 2], it * 32)
                    scatter(n4)
            for n4 in range(4):
                e = E - 4 + n4
                if n4 == 0:
                    pool.wait_ge(mo["gst"], E)
                    pool.wait_ge(mo["gp"], e)
                    pool.wait_ge(mo["wc"], e)
                    gather(3, 0)
                pool.wait_ge(mo["sst"], e + 1)
                pool.wait_ge(mo["yc"], 2 * e + 2)
                pool.wait_ge(mo["y_st"][(n4 + 2) % 4], 32 * (E // 4 - (n4 < 2)))
                scatter(n4)

        @block.scalar
        def _(act):
            sc_ = nc.scalar
            act.wait_ge(s_par, 16 * 8)
            sc_.activation(sil[:, 0, :], cin, ACT.Exp, scale=-1.0).then_inc(s_a0, 1)
            act.wait_ge(s_v0, 1)

            def a_hT(bt, k):
                after(act, "hTp", bt, k + 1)
                after(act, "mcol", bt, 1)
                after(act, "vp", bt, 0)
                sc_.activation(hT[:, k, BAND:BAND + S], bA[:, :], ACT.Identity, scale=mcol[:, 2 + k:3 + k],
                               bias=mcol[:, k:k + 1]).then_inc(sems["hT"], 1)

            def a_p32(bt, j):
                after(act, "proj", bt, j + 1)
                if j >= 2:
                    after(act, "lpart", bt, j - 1)
                else:
                    after(act, "lpart", bt, 0)
                sc_.activation(p32[j % 2][:], bA[:, :], ACT.Identity, scale=SCALE if j < 2 else 1.0,
                               bias=bqk[:, j:j + 1]).then_inc(sems["p32"], 1)
                after(act, "p32", bt, j + 1)
                parts_stored(act, bt, j, j // 2)
                sc_.activation(parts[:, j % 2, 0, :], p32[j % 2][:], ACT.Copy).then_inc(sems["hpart"], 1)

            def exps(bt, g, u):
                for p in range(2):
                    m = 10 * g + 2 * u + p
                    after(act, "STp", bt, m + 1)
                    after(act, "pv", bt, m - NPT + 1)
                    w = P if u in (0, U - 1) else 2 * P
                    src = bST[m % 2][:, 0:2 * w].rearrange("p (h q) -> p h q", h=2)
                    sc_.activation(PT[m % NPT][:, :, 0:w], src, ACT.Exp).then_inc(sems["exp"], 1)

            def take_mT(bt, g):
                after(act, "mTp", bt, g + 1)
                after(act, "mrow_ld", bt, 16 * g)
                sc_.activation(MT[:], bT[0:32, 0:P // 2].bitcast(BF16), ACT.Copy).then_inc(sems["mT"], 1)

            def take_oT(bt, g):
                after(act, "pv", bt, 10 * g + 10)
                after(act, "oTp", bt, g)
                sc_.activation(OTs[:], bO[:, :], ACT.Copy).then_inc(sems["oTs"], 1)

            def c_onT(bt, k):
                after(act, "onTp", bt, k + 1)
                after(act, "op", bt, 0)
                sc_.activation(onT[:, k, :], bC[:, :], ACT.Copy).then_inc(sems["onT"], 1)

            def c_h2T(bt, k):
                after(act, "h2Tp", bt, k + 1)
                after(act, "lg", bt, 0)
                sc_.activation(h2T[:, k, :], bC[:, :], ACT.Copy).then_inc(sems["h2T"], 1)

            def c_ex(bt):
                after(act, "lg", bt, 1)
                after(act, "pos", bt, 0)
                sc_.activation(ex[:], bC[:, 0:T * E], ACT.Exp, scale=-1.0).then_inc(sems["ex"], 1)

            def body(prev, now, nxt):
                for slot in range(SLOTS):
                    g, u = divmod(slot, U)
                    exps(now, g, u)
                    if u == 0 and (g > 0 or prev):
                        take_oT(*((now, g - 1) if g > 0 else (prev, QUADS - 1)))
                    if u == 3 and (g < QUADS - 1 or nxt):
                        take_mT(*((now, g + 1) if g < QUADS - 1 else (nxt, 0)))
                    if nxt and slot in (2, 3):
                        a_hT(nxt, slot - 2)
                    if nxt and 4 <= slot <= 7:
                        a_p32(nxt, slot - 4)
                    if prev and slot in (3, 4):
                        c_onT(prev, slot - 3)
                    if prev and slot in (12, 13):
                        c_h2T(prev, slot - 12)
                    if prev and slot == 14:
                        c_ex(prev)

            a_hT(batch(0), 0)
            a_hT(batch(0), 1)
            for j in range(4):
                a_p32(batch(0), j)
            take_mT(batch(0), 0)
            loops(act, body)
            last = batch(B - 1)
            take_oT(last, QUADS - 1)
            for k in range(C):
                c_onT(last, k)
            for k in range(C):
                c_h2T(last, k)
            c_ex(last)

            def take_x(it, n):
                need(act, mo["xTp"], it * 8 + (2 * n + 1))
                need(act, mo["gp"], it * 4 + (n - 1))
                sc_.activation(xgT[n % 2][:, 0, :], bS[n % 2][:, 0:CAP], ACT.Copy).then_inc(mo["xTc"], 1)

            def silu(it, n):
                need(act, mo["gp"], it * 4 + (n + 1))
                need(act, mo["hm"], it * 4 + (n - 1))
                sc_.activation(sg[n % 2][:], bST[n % 2][:, 0:CAP], ACT.Silu).then_inc(mo["sg"], 1)

            def scale_y(it, n):
                need(act, mo["yp"], it * 4 + (n + 1))
                need(act, mo["wc"], it * 4 + (n + 1))
                need(act, mo["y_st"][n % 4], (it + n // 4) * 32)
                yb = bO if n % 2 == 0 else bT
                for h in range(2):
                    sc_.activation(ys[n % 4][:, h, :], yb[:, h * D:(h + 1) * D], ACT.Copy,
                                   scale=wcol[n % 4][:, h:h + 1]).then_inc(mo["yc"], 1)

            def four(it, first=False, final=False):
                for n in range(4):
                    silu(it, n)
                    if not (final and n == 3):
                        take_x(it, n + 1)
                    if not (first and n == 0):
                        scale_y(it, n - 1)

            take_x(0, 0)
            four(0, first=True)
            with act.Fori(1, E // 4 - 1) as it:
                four(it)
            four(E // 4 - 1, final=True)
            scale_y(E // 4 - 1, 3)

        @block.tensor
        def _(pe):
            mm = nc.tensor.matmul
            pe.wait_ge(s_const, NCONST)
            pe.wait_ge(s_v0, 3)
            for k in range(C):
                nc.tensor.transpose(bA[:, k * B:(k + 1) * B], sil[:, 2, k * P:(k + 1) * P], ident[0:B, 0:B]
                                    ).then_inc(s_pe0, 1)
            for k in range(C):
                nc.tensor.transpose(bC[:, k * E:(k + 1) * E], gw[:, k * P:(k + 1) * P], ident[0:E, 0:E]
                                    ).then_inc(s_pe0, 1)
            pe.wait_ge(s_v0, 5)
            pe.wait_ge(s_par2, 16)
            for n in range(4):
                col = (n // 2) * D + (n % 2) * P
                for k in range(C):
                    last = mm(bT[:, n * B:(n + 1) * B], wm[:, k, col:col + P], silT[:, k, :], start=(k == 0), stop=(k == C - 1))
            last.then_inc(s_pe0, 1)
            for n, bank in enumerate((bS[0], bS[1])):
                for q, col in enumerate(((2, 5), (3, 4))[n]):
                    for k in range(C):
                        last = mm(bank[0:B, q * D:(q + 1) * D], silT[:, k, :], wm[:, k, col * D:(col + 1) * D],
                                  start=(k == 0), stop=(k == C - 1))
                last.then_inc(s_pe0, 1)

            def a_hT(bt, k):
                after(pe, "xn", bt, T)
                if k == 0:
                    after(pe, "v", bt, 0)
                else:
                    after(pe, "hT", bt, k)
                for t in range(T):
                    last = nc.tensor.transpose(bA[:, t * P:(t + 1) * P], xn[:, t, k * P:(k + 1) * P], ident[:])
                last.then_inc(sems["hTp"], 1)

            def a_proj(bt, j):
                if j == 0:
                    after(pe, "hT", bt, C)
                else:
                    after(pe, "p32", bt, j)
                for k in range(C):
                    last = mm(bA[:, :], wqkv[:, k, j * P:(j + 1) * P], hT[:, k, BAND:BAND + S], start=(k == 0), stop=(k == C - 1))
                last.then_inc(sems["proj"], 1)

            def a_v(bt, j):
                if j == 0:
                    after(pe, "p32", bt, 4)
                else:
                    after(pe, "v", bt, j)
                for i, u in enumerate(range(2 * j, min(2 * j + 2, U))):
                    for k in range(C):
                        last = mm(bA[:, i * D:(i + 1) * D], hT[:, k, u * P:(u + 1) * P], wqkv[:, k, 2 * D:3 * D],
                                  start=(k == 0), stop=(k == C - 1))
                last.then_inc(sems["vp"], 1)

            def fills(bt, g, ks):
                if g == 0 and ks[0] == 0:
                    after(pe, "qk_ld", bt, 192)
                q, kk = Qs[bt.par], Ks[bt.par]
                for n in ks:
                    t, pr = divmod(n, 2)
                    after(pe, "smax", bt, 2 * (8 * g + n - 1))
                    for i in range(2):
                        h = HQ * g + 2 * pr + i
                        last = mm(bS[n % 2][:, i * 2 * P:(i + 1) * 2 * P], q[0:MROW, h, t * P:(t + 1) * P],
                                  kk[0:MROW, h, t * P:(t + 2) * P], start=True, stop=True)
                    last.then_inc(sems["Sp"], 1)

            def turn_m(bt, g):
                after(pe, "m2", bt, 2 * g + 2)
                after(pe, "on", bt, g - 1)
                nc.tensor.transpose(bT[:, 0:P // 2].bitcast(BF16), M2[:], identb[:]).then_inc(sems["mTp"], 1)

            def qrange(u):
                return max(u - 1, 0) * P, min(u + 1, T) * P

            def scoresT(bt, g, u):
                if u == 0:
                    after(pe, "mrow_ld", bt, 16 * (g + 1))
                q, kk = Qs[bt.par], Ks[bt.par]
                lo, hi = qrange(u)
                for p in range(2):
                    m = 10 * g + 2 * u + p
                    after(pe, "exp", bt, m - 1)
                    for i in range(2):
                        h = HQ * g + 2 * p + i
                        last = mm(bST[m % 2][:, i * (hi - lo):(i + 1) * (hi - lo)], kk[0:KROWS, h, u * P:(u + 1) * P],
                                  q[0:KROWS, h, lo:hi], start=True, stop=True)
                    last.then_inc(sems["STp"], 1)

            def values(bt, g, u):
                if g == 0 and u == 0:
                    after(pe, "v", bt, 3)
                if u == 0:
                    after(pe, "oTs", bt, g)
                lo, hi = qrange(u)
                rows = slice(BAND, P) if u == 0 else slice(0, BAND) if u == U - 1 else slice(0, P)
                for p in range(2):
                    m = 10 * g + 2 * u + p
                    after(pe, "cut", bt, 16 * g + 2 * SEL_BEFORE[u] + SEL_OF[u] * (p + 1), apart=True)
                    for i in range(2):
                        j = 2 * p + i
                        last = mm(bO[32 * j:32 * j + 32, lo:hi], Va[bt.par][rows, u, HQ * g + j, :],
                                  PT[m % NPT][rows, i, 0:hi - lo], start=(u == 0), stop=(u == U - 1),
                                  skip_group_check=True)
                    last.then_inc(sems["pv"], 1)

            def turn_o(bt, g):
                after(pe, "oTs", bt, g + 1)
                after(pe, "mT", *((bt, g + 2) if g < QUADS - 1 else (Batch(bt.b + 1, 0, 0), 1))) if True else None
                for t in range(T):
                    last = nc.tensor.transpose(bT[:, t * P:(t + 1) * P], OTs[:, t * P:(t + 1) * P], ident[:])
                last.then_inc(sems["oTp"], 1)

            def turn_o_last(bt):
                after(pe, "oTs", bt, QUADS)
                for t in range(T):
                    last = nc.tensor.transpose(bT[:, t * P:(t + 1) * P], OTs[:, t * P:(t + 1) * P], ident[:])
                last.then_inc(sems["oTp"], 1)

            def c_onT(bt, k):
                after(pe, "on", bt, QUADS)
                if k == 0:
                    after(pe, "idx", bt, 0)
                else:
                    after(pe, "onT", bt, k)
                for t in range(T):
                    last = nc.tensor.transpose(bC[:, t * P:(t + 1) * P], on[:, t, k * P:(k + 1) * P], ident[:])
                last.then_inc(sems["onTp"], 1)

            def c_op(bt, n):
                after(pe, "onT", bt, C)
                after(pe, "t1", bt, n)
                for i in range(2):
                    t = 2 * n + i
                    for k in range(C):
                        last = mm(bC[:, i * D:(i + 1) * D], onT[:, k, t * P:(t + 1) * P], wo[:, k, :],
                                  start=(k == 0), stop=(k == C - 1))
                last.then_inc(sems["op"], 1)

            def c_h2T(bt, k):
                after(pe, "h2", bt, 2)
                if k == 0:
                    after(pe, "t1", bt, 2)
                else:
                    after(pe, "h2T", bt, k)
                for t in range(T):
                    last = nc.tensor.transpose(bC[:, t * P:(t + 1) * P], H2[:, t, k * P:(k + 1) * P], ident[:])
                last.then_inc(sems["h2Tp"], 1)

            def c_lg(bt):
                after(pe, "h2T", bt, C)
                for t in range(T):
                    for k in range(C):
                        last = mm(bC[:, t * E:(t + 1) * E], h2T[:, k, t * P:(t + 1) * P], gwT[:, k, :],
                                  start=(k == 0), stop=(k == C - 1))
                last.then_inc(sems["lg"], 1)

            def c_cnt(bt):
                after(pe, "ex", bt, 1)
                after(pe, "pre", bt, T + 1)
                mm(bC[:, 0:T * E], before[:], selb[:], start=True, stop=False)
                mm(bC[:, 0:T * E], onesb[:], Spre[:, 0:T, :].rearrange("p t e -> p (t e)"), start=False, stop=True
                   ).then_inc(sems["cntp"], 1)

            def c_idx(bt, half):
                if half == 0:
                    after(pe, "pos", bt, 1)
                    after(pe, "oneh", bt, 3 * T)
                else:
                    after(pe, "idx", bt, 1)
                for i in range(G // 2):
                    es = slice((half * (G // 2) + i) * EG, (half * (G // 2) + i + 1) * EG)
                    for t in range(T):
                        last = mm(bC[:, i * P:(i + 1) * P], oneh[:, t, es, :].rearrange("p e a -> p (e a)"),
                                  oneh[:, T + t, es, :].rearrange("p e a -> p (e a)"), start=(t == 0), stop=(t == T - 1))
                last.then_inc(sems["idx" + "p"], 1)

            FILLS = {0: [0, 1, 2], 1: [3, 4, 5], 2: [6, 7]}

            def body(prev, now, nxt):
                for slot in range(SLOTS):
                    g, u = divmod(slot, U)
                    ahead = (now, g + 1) if g < QUADS - 1 else (nxt, 0)
                    if u in FILLS and ahead[0]:
                        fills(*ahead, FILLS[u])
                    scoresT(now, g, u)
                    if slot > 0:
                        values(now, *divmod(slot - 1, U))
                    elif prev:
                        values(prev, QUADS - 1, U - 1)
                    if u == 1 and (g > 0 or prev):
                        turn_o(*((now, g - 1) if g > 0 else (prev, QUADS - 1)))
                    if u == 3 and ahead[0]:
                        turn_m(*ahead)
                    if nxt:
                        if slot in (2, 3):
                            a_hT(nxt, slot - 2)
                        if 4 <= slot <= 7:
                            a_proj(nxt, slot - 4)
                        if 8 <= slot <= 10:
                            a_v(nxt, slot - 8)
                    if prev:
                        if slot in (3, 4):
                            c_onT(prev, slot - 3)
                        if slot in (6, 8):
                            c_op(prev, (slot - 6) // 2)
                        if slot in (12, 13):
                            c_h2T(prev, slot - 12)
                        if slot == 14:
                            c_lg(prev)
                        if slot == 16:
                            c_cnt(prev)
                        if slot == 19:
                            c_idx(prev, 0)
                            c_idx(prev, 1)

            first = batch(0)
            pe.wait_ge(s_v0, 9)
            pe.wait_ge(s_par, 16 * 8)
            a_hT(first, 0)
            a_hT(first, 1)
            for j in range(4):
                a_proj(first, j)
            for j in range(3):
                a_v(first, j)
            fills(first, 0, list(range(8)))
            turn_m(first, 0)
            loops(pe, body)
            last = batch(B - 1)
            values(last, QUADS - 1, U - 1)
            turn_o_last(last)
            for k in range(C):
                c_onT(last, k)
            for n in range(2):
                c_op(last, n)
            for k in range(C):
                c_h2T(last, k)
            c_lg(last)
            c_cnt(last)
            c_idx(last, 0)
            c_idx(last, 1)

            pe.wait_ge(s_tab_ld, 32)
            pe.wait_ge(sems["idx"], 2 * B)
            for k in range(2):
                last_t = nc.tensor.transpose(bC[:, k * P:(k + 1) * P], tabs[:, k, :], ident[:])
            last_t.then_inc(s_tabT, 1)

            def turn_x(it, n):
                par = n % 2
                pe.wait_ge(mo["x_ld"][n % 4], (it + n // 4) * 32 + 32)
                need(pe, mo["xTc"], it * 4 + (n - 1))
                need(pe, mo["xTd"], it * 4 + (n - 1))
                if isinstance(it, int) and it == 0 and n == 1:
                    pe.wait_ge(s_ix, 10)
                for k, bank in ((0, bS[par]), (1, bA if par == 0 else bC)):
                    for h in range(2):
                        last = nc.tensor.transpose(bank[:, h * P:(h + 1) * P], xg[n % 4][:, h, k * P:(k + 1) * P], ident[:])
                    last.then_inc(mo["xTp"], 1)

            def expert(it, n):
                par = n % 2
                need(pe, mo["xTc"], it * 4 + (n + 1))
                need(pe, mo["xTd"], it * 4 + (n + 1))
                need(pe, mo["w_ld"][n], it * 48 + 48)
                need(pe, mo["hm"], it * 4 + (n - 1))
                for a in range(2):
                    for k in range(C):
                        last = mm(bST[par][:, a * CAP:(a + 1) * CAP], wgu[n][:, a, k, :], xgT[par][:, k, :],
                                  start=(k == 0), stop=(k == C - 1))
                last.then_inc(mo["gp"], 1)

            def expert_out(it, n):
                par = n % 2
                need(pe, mo["hm"], it * 4 + (n + 1))
                need(pe, mo["yc"], it * 8 + (2 * n - 2))
                yb = bO if par == 0 else bT
                for h in range(2):
                    last = mm(yb[:, h * D:(h + 1) * D], hm[par][:, h * P:(h + 1) * P], wd[n % 4][:], start=True, stop=True)
                last.then_inc(mo["yp"], 1)

            def four(it, first=False, final=False):
                for n in range(4):
                    expert(it, n)
                    if not (final and n == 3):
                        turn_x(it, n + 1)
                    if not (first and n == 0):
                        expert_out(it, n - 1)

            turn_x(0, 0)
            four(0, first=True)
            with pe.Fori(1, E // 4 - 1) as it:
                four(it)
            four(E // 4 - 1, final=True)
            expert_out(E // 4 - 1, 3)

        @block.vector
        def _(dve):
            v = nc.vector

            def a_stats(bt):
                dve.wait_ge(x_ld[bt.par], bt.half * 16 + 16)
                for t in range(T):
                    v.bn_stats(stats[:, t, :], xt[:, t, :]).then_inc(sems["stats"], 1)
                after(dve, "rstd", bt, 0, apart=True)
                for t in range(T):
                    after(dve, "stats", bt, t + 1, apart=True)
                    v.bn_aggr(mv[:, t, :], stats[:, t, :]).then_inc(sems["aggr"], 1)

            def a_norm(bt):
                after(dve, "hT", bt, 0)
                i = bt.b if isinstance(bt.b, int) else None
                src = modT[:, i, :] if i is not None else modT[:, bass.ds(bt.b, 1), :].rearrange("p o n -> p (o n)")
                v.tensor_copy(mcol[:], src).then_inc(sems["mcol"], 1)
                after(dve, "rstd", bt, 2)
                after(dve, "hTp", bt, 0)
                for t in range(T):
                    v.tensor_scalar(xn[:, t, :], xt[:, t, :], mv[:, t, 0:1], rs[:, t:t + 1], ALU.subtract,
                                    ALU.mult).then_inc(sems["xn"], 1)

            def a_v(bt, j):
                after(dve, "vp", bt, j + 1)
                if not isinstance(bt.b, int) or bt.b >= 2:
                    after(dve, "pv", Batch(bt.b - 1, 0, 0), 0)
                us = slice(2 * j, min(2 * j + 2, U))
                nu = us.stop - us.start
                v.tensor_tensor(Va[bt.par][:, us, :, 0:HD],
                                bA[:, 0:nu * D].rearrange("p (u h d) -> p u h d", u=nu, d=HD),
                                bv[:, :].rearrange("p (h d) -> p h d", d=HD).unsqueeze(1).to_broadcast([P, nu, H, HD]),
                                ALU.add).then_inc(sems["v"], 1)

            def maxima(bt, g, ks):
                for n in ks:
                    t, pr = divmod(n, 2)
                    after(dve, "Sp", bt, 8 * g + n + 1)
                    if n == 0:
                        after(dve, "m2", bt, 2 * g)
                    edge = 0 if t == 0 else 2 if t == T - 1 else 1
                    for i in range(2):
                        at = 2 * (8 * g + n) + i
                        after(dve, "smax", bt, at - 1, apart=True)
                        h = 2 * pr + i
                        ins = v.tensor_tensor_reduce(out=junk[:, i, :], in0=bS[n % 2][:, i * 2 * P:(i + 1) * 2 * P],
                                                     in1=mask[:, edge, :], scale=1.0, scalar=TAKEN, op0=ALU.add,
                                                     op1=ALU.max, accum_out=mrowmax[:, h, t:t + 1])
                        ins.then_inc(sems["smax"], 1)

            def split_m(bt, g):
                after(dve, "mTp", bt, g)
                after(dve, "smax", bt, 16 * (g + 1))
                flat = mrowmax[:, :, :].rearrange("p h t -> p (h t)")
                v.tensor_scalar(M2[:, 0:16], flat, -1.0, None, ALU.mult).then_inc(sems["m2"], 1)
                after(dve, "m2", bt, 2 * g + 1)
                v.scalar_tensor_tensor(M2[:, 16:32], flat, -1.0, M2[:, 0:16], ALU.mult, ALU.subtract
                                       ).then_inc(sems["m2"], 1)

            def norm_o(bt, g):
                after(dve, "oTp", bt, g + 1)
                if g == 0:
                    after(dve, "onTp", bt, 0)
                after(dve, "on", bt, g)
                src = bT[:, :].rearrange("p (t h d) -> p t h d", t=T, d=32)
                v.reciprocal(rec[:], src[:, :, :, HD]).then_inc(sems["rec"], 1)
                after(dve, "rec", bt, g + 1)
                v.tensor_tensor(on[:, :, g * 64:(g + 1) * 64].rearrange("p t (h d) -> p t h d", d=HD), src[:, :, :, 0:HD],
                                rec[:, :, :].unsqueeze(3).to_broadcast([P, T, HQ, HD]), ALU.mult).then_inc(sems["on"], 1)

            def c_x1(bt, n):
                after(dve, "op", bt, n + 1)
                after(dve, "x1_st", bt, 0)
                after(dve, "stats2", bt, 0)
                after(dve, "xb", bt, 2)
                dst = x1[:, 2 * n:2 * n + 2, :]
                v.tensor_tensor(dst, bC[:, :].rearrange("p (t d) -> p t d", t=2),
                                mr[:, 0, :].unsqueeze(1).to_broadcast([P, 2, D]), ALU.mult).then_inc(sems["t1"], 1)
                after(dve, "t1", bt, n + 1)
                v.tensor_tensor(dst, dst, xc[:, 2 * n:2 * n + 2, :], ALU.add).then_inc(sems["x1"], 1)

            def c_stats(bt):
                after(dve, "x1", bt, 2)
                for t in range(T):
                    v.bn_stats(stats2[:, t, :], x1[:, t, :]).then_inc(sems["stats2"], 1)
                after(dve, "rstd2", bt, 0, apart=True)
                for t in range(T):
                    after(dve, "stats2", bt, t + 1, apart=True)
                    v.bn_aggr(mv2[:, t, :], stats2[:, t, :]).then_inc(sems["aggr2"], 1)

            def c_norm(bt):
                after(dve, "rstd2", bt, 2)
                after(dve, "h_st", bt, 0)
                after(dve, "h2Tp", bt, 0)
                for t in range(T):
                    v.tensor_scalar(xn2[:, t, :], x1[:, t, :], mv2[:, t, 0:1], rs2[:, t:t + 1], ALU.subtract,
                                    ALU.mult).then_inc(sems["xn2"], 1)

            def c_route(bt):
                done = [0]

                def step(ins, apart=False):
                    ins.then_inc(sems["route"], 1)
                    done[0] += 1
                    after(dve, "route", bt, done[0], apart=apart)

                after(dve, "ex", bt, 1)
                step(v.tensor_scalar(ex[:], ex[:], 1.0, None, ALU.add))
                step(v.reciprocal(sc[:], ex[:]))
                step(v.tensor_tensor(sfc[:, :, :].rearrange("p (t g) e -> p t (g e)", t=T),
                                     sc[:, :].rearrange("p (t e) -> p t e", t=T),
                                     gb[:, :].unsqueeze(1).to_broadcast([P, T, E]), ALU.add))
                hi4, lo4, hi2, q2, r2, lo2 = (pairs[:, i] for i in range(6))
                step(v.tensor_tensor(hi4, sfc[:, :, 0:4], sfc[:, :, 4:8], ALU.max))
                step(v.tensor_tensor(lo4, sfc[:, :, 0:4], sfc[:, :, 4:8], ALU.min))
                step(v.tensor_tensor(hi2[:, :, 0:2], hi4[:, :, 0:2], hi4[:, :, 2:4], ALU.max))
                step(v.tensor_tensor(q2[:, :, 0:2], hi4[:, :, 0:2], hi4[:, :, 2:4], ALU.min))
                step(v.tensor_tensor(r2[:, :, 0:2], lo4[:, :, 0:2], lo4[:, :, 2:4], ALU.max))
                step(v.tensor_tensor(lo2[:, :, 0:2], q2[:, :, 0:2], r2[:, :, 0:2], ALU.max))
                step(v.tensor_tensor(gs[:, 0, :], hi2[:, :, 0], hi2[:, :, 1], ALU.max))
                step(v.tensor_tensor(gs[:, 1, :], hi2[:, :, 0], hi2[:, :, 1], ALU.min))
                step(v.tensor_tensor(gs[:, 2, :], lo2[:, :, 0], lo2[:, :, 1], ALU.max))
                step(v.tensor_tensor(gs[:, 1, :], gs[:, 1, :], gs[:, 2, :], ALU.max))
                step(v.tensor_tensor(gs[:, 3, :], gs[:, 0, :], gs[:, 1, :], ALU.add))
                g4 = gs[:, 3, :].rearrange("p (t g) -> p t g", t=T)
                other = g4.unsqueeze(2).to_broadcast([P, T, G, G])
                own = g4.unsqueeze(3).to_broadcast([P, T, G, G])
                step(v.tensor_tensor(cmp1[:], other, own, ALU.is_gt))
                step(v.tensor_tensor(cmp2[:], other, own, ALU.is_equal))
                step(v.tensor_tensor(cmp2[:], cmp2[:], lowerg[:, :, :].unsqueeze(1).to_broadcast([P, T, G, G]), ALU.mult))
                step(v.tensor_tensor(cmp1[:], cmp1[:], cmp2[:], ALU.add))
                step(v.tensor_reduce(gs[:, 0, :], cmp1[:, :, :, :].rearrange("p t g h -> p (t g) h"), AX_X, ALU.add))
                step(v.tensor_scalar(gs[:, 1, :], gs[:, 0, :], TG - 0.5, None, ALU.is_lt))
                step(v.tensor_scalar(gs[:, 2, :], gs[:, 1, :], 1.0, -NEG, ALU.subtract, ALU.mult))
                wide = lambda n: gs[:, n, :].unsqueeze(2).to_broadcast([P, T * G, EG])
                step(v.tensor_tensor(tmp[:], sfc[:], wide(1), ALU.mult))
                step(v.tensor_tensor(tmp[:], tmp[:], wide(2), ALU.add), apart=True)
                for t in range(T):
                    tt = tmp[:, t * G:(t + 1) * G, :].rearrange("p g e -> p (g e)")
                    rr = rep[:, t * G:(t + 1) * G, :].rearrange("p g e -> p (g e)")
                    step(v.max(top8[:, t, :], tt), apart=True)
                    step(v.match_replace(rr, top8[:, t, :], tt, TAKEN), apart=t < T - 1)
                after(dve, "cntp", bt, 0)
                step(v.tensor_scalar(selb[:], rep[:, :, :].rearrange("p g e -> p (g e)"), TAKEN / 1.5, None, ALU.is_lt))
                per_t = lambda ap: ap.rearrange("p (t e) -> p t e", t=T)
                step(v.tensor_tensor(sc[:], sc[:], selb[:], ALU.mult))
                step(v.tensor_reduce(wsum[:, 0, :], per_t(sc[:, :]), AX_X, ALU.add))
                step(v.tensor_scalar(wsum[:, 1, :], wsum[:, 0, :], 1e-20, None, ALU.add))
                step(v.reciprocal(wsum[:, 2, :], wsum[:, 1, :]))
                step(v.tensor_tensor(per_t(sc[:, :]), per_t(sc[:, :]), wsum[:, 2, :].unsqueeze(2).to_broadcast([P, T, E]),
                                     ALU.mult))
                after(dve, "h_st", bt, 0)
                step(v.tensor_scalar(H2[:, :, D:HW], per_t(sc[:, :]), ROUTE_SCALE, None, ALU.mult))
                assert done[0] == PER["route"], done[0]
                v.tensor_copy(Spre[:, 0, :], Spre[:, T, :]).then_inc(sems["pre"], 1)
                for t in range(T):
                    after(dve, "pre", bt, t + 1)
                    v.tensor_tensor(Spre[:, t + 1, :], Spre[:, t, :], selb[:, t * E:(t + 1) * E], ALU.add
                                    ).then_inc(sems["pre"], 1)

            def c_pos(bt):
                after(dve, "cntp", bt, 1)
                v.scalar_tensor_tensor(posf[:], selb[:], -FAR, bC[:, 0:T * E], ALU.mult, ALU.add).then_inc(sems["pos"], 1)
                after(dve, "pos", bt, 1)
                v.tensor_scalar(posi[:, 0, :], posf[:], FAR, None, ALU.add).then_inc(sems["pos"], 1)
                after(dve, "pos", bt, 2)
                v.tensor_scalar(posi[:, 1, :], posi[:, 0, :], 4, None, ALU.logical_shift_right).then_inc(sems["pos"], 1)
                v.tensor_scalar(posi[:, 2, :], posi[:, 0, :], LO - 1, None, ALU.bitwise_and).then_inc(sems["pos"], 1)
                i = bt.b * T
                src = valt[:, bass.ds(i, T)] if not isinstance(i, int) else valt[:, i:i + T]
                v.tensor_copy(vt[:], src).then_inc(sems["vt"], 1)

            def c_onehot(bt, t):
                after(dve, "pos", bt, 4)
                after(dve, "vt", bt, 1)
                after(dve, "idxp", bt, 0)
                es = slice(t * E, (t + 1) * E)
                digits = iota16[:, :].unsqueeze(1).to_broadcast([P, E, LO])
                low = oneh[:, 2 * T]
                after(dve, "oneh", bt, 3 * t)
                v.tensor_tensor(oneh[:, t], posi[:, 1, es].unsqueeze(2).to_broadcast([P, E, LO]), digits, ALU.is_equal
                                ).then_inc(sems["oneh"], 1)
                v.tensor_tensor(low, posi[:, 2, es].unsqueeze(2).to_broadcast([P, E, LO]), digits, ALU.is_equal
                                ).then_inc(sems["oneh"], 1)
                after(dve, "oneh", bt, 3 * t + 2)
                v.tensor_scalar(oneh[:, T + t], low, vt[:, t:t + 1], None, ALU.mult).then_inc(sems["oneh"], 1)

            def c_idx(bt, half):
                after(dve, "idxp", bt, half + 1)
                dst = iacc[:, half * 4:half * 4 + 4].rearrange("p g e b -> p (g e b)")
                v.tensor_tensor(dst, dst, bC[:, :], ALU.add).then_inc(sems["idx"], 1)

            FILLS = {0: [0, 1, 2], 1: [3, 4, 5], 2: [6, 7]}

            def body(prev, now, nxt):
                for slot in range(SLOTS):
                    g, u = divmod(slot, U)
                    ahead = (now, g + 1) if g < QUADS - 1 else (nxt, 0)
                    if u in FILLS and ahead[0]:
                        maxima(*ahead, FILLS[u])
                    if u == 2 and ahead[0]:
                        split_m(*ahead)
                    if u == 2 and (g > 0 or prev):
                        norm_o(*((now, g - 1) if g > 0 else (prev, QUADS - 1)))
                    if nxt:
                        if slot == 0:
                            a_stats(nxt)
                        if slot == 1:
                            a_norm(nxt)
                        if 9 <= slot <= 11:
                            a_v(nxt, slot - 9)
                    if prev:
                        if slot in (7, 8):
                            c_x1(prev, slot - 7)
                        if slot == 9:
                            c_stats(prev)
                        if slot == 10:
                            c_norm(prev)
                        if slot == 15:
                            c_route(prev)
                        if slot == 16:
                            c_pos(prev)
                        if 17 <= slot <= 18:
                            c_onehot(prev, 2 * (slot - 17))
                            c_onehot(prev, 2 * (slot - 17) + 1)
                        if slot == 19:
                            c_idx(prev, 0)
                            c_idx(prev, 1)

            nset = [0]

            def setup(ins):
                ins.then_inc(s_ix2, 1)
                nset[0] += 1

            for i in range(2):
                setup(v.memset(Ks[i][:, :, 0:BAND], 0.0))
                setup(v.memset(Ks[i][:, :, BAND + S:KW], 0.0))
                setup(v.memset(Ks[i][MROW:P, :, BAND:BAND + S], 1.0))
                setup(v.memset(Va[i][:], 0.0))
                dve.wait_ge(s_ix2, nset[0])
                setup(v.memset(Va[i][:, :, :, HD:HD + 1], 1.0))
                setup(v.memset(Ks[i][MROW:P, :, 0:BAND], 1.0))
                setup(v.memset(Ks[i][MROW:P, :, BAND + S:KW], 1.0))
            setup(v.memset(hT[:, :, 0:BAND], 0.0))
            setup(v.memset(hT[:, :, BAND + S:KW], 0.0))
            setup(v.memset(M2[:], 0.0))
            setup(v.memset(Spre[:, T, :], 0.0))
            setup(v.memset(iacc[:], 0.0))
            dve.wait_ge(s_par, 16 * 8)
            dve.wait_ge(s_a0, 1)
            v.tensor_scalar(sil[:, 1, :], sil[:, 0, :], 1.0, None, ALU.add).then_inc(s_v0, 1)
            dve.wait_ge(s_v0, 1)
            v.reciprocal(sil[:, 0, :], sil[:, 1, :]).then_inc(s_v0, 1)
            dve.wait_ge(s_v0, 2)
            dve.wait_ge(s_ix2, nset[0])
            v.tensor_tensor(sil[:, 2, :], cin, sil[:, 0, :], ALU.mult).then_inc(s_v0, 1)
            dve.wait_ge(s_pe0, 4)
            v.tensor_copy(silT[:], bA[:, 0:C * B].rearrange("p (c b) -> p c b", c=C)).then_inc(s_v0, 1)
            v.tensor_copy(gwT[:], bC[:, 0:C * E].rearrange("p (c e) -> p c e", c=C)).then_inc(s_v0, 1)
            dve.wait_ge(s_pe0, 7)
            cols = bT[:, 0:4 * B].rearrange("p (n b) -> p b n", n=4)
            v.tensor_copy(modT[:, :, 0:2], cols[:, :, 0:2]).then_inc(s_v0, 1)
            v.tensor_scalar(modT[:, :, 2:4], cols[:, :, 2:4], 1.0, None, ALU.add).then_inc(s_v0, 1)
            v.tensor_copy(gates[:, 1, 0, :], bS[1][0:B, 0:D]).then_inc(s_v1, 1)
            v.tensor_scalar(gates[:, 1, 1, :], bS[1][0:B, D:2 * D], 1.0, None, ALU.add).then_inc(s_v1, 1)
            gg = gates[:, 0].rearrange("b k d -> b (k d)")
            sgn = sil[:, 0:2, :].rearrange("b k d -> b (k d)")
            v.tensor_copy(gg, bS[0][0:B, :]).then_inc(s_v1, 1)
            dve.wait_ge(s_v1, 3)
            v.tensor_scalar(sgn, gg, 0.0, 2.0, ALU.is_ge, ALU.mult).then_inc(s_v1, 1)
            dve.wait_ge(s_v1, 4)
            v.scalar_tensor_tensor(gg, gg, -1.0, gg, ALU.mult, ALU.max).then_inc(s_v1, 1)
            v.tensor_scalar(sgn, sgn, 1.0, None, ALU.subtract).then_inc(s_v1, 1)
            dve.wait_ge(s_v1, 6)
            v.tensor_scalar(gg, gg, 0.25, None, ALU.max).then_inc(s_v1, 1)
            dve.wait_ge(s_v1, 7)
            v.tensor_tensor(gg, gg, sgn, ALU.mult).then_inc(s_v0, 1)
            v.tensor_scalar(bqk[:, 0:2], bqk[:, 0:2], SCALE, None, ALU.mult).then_inc(s_v0, 1)
            dve.wait_ge(s_v0, 9)
            a_stats(batch(0))
            a_norm(batch(0))
            for j in range(3):
                a_v(batch(0), j)
            maxima(batch(0), 0, list(range(8)))
            split_m(batch(0), 0)
            loops(dve, body)
            last = batch(B - 1)
            norm_o(last, QUADS - 1)
            c_x1(last, 0)
            c_x1(last, 1)
            c_stats(last)
            c_norm(last)
            c_route(last)
            c_pos(last)
            for t in range(T):
                c_onehot(last, t)
            c_idx(last, 0)
            c_idx(last, 1)

            k = [4]

            def step(ins):
                ins.then_inc(s_ix, 1)
                k[0] += 1
                dve.wait_ge(s_ix, k[0])

            dve.wait_ge(s_ix, 4)
            after(dve, "idx", Batch(B, 0, 0), 0)
            dm = dmask[:, :, :].rearrange("p e b -> p (e b)").unsqueeze(1).to_broadcast([P, G, P])
            flat = iacc[:, :, :, :].rearrange("p g e b -> p g (e b)")
            v.tensor_tensor(flat, flat, dm, ALU.mult).then_inc(s_i2, 1)
            dve.wait_ge(s_i2, 1)
            v.tensor_reduce(iv[:, 0], iacc[:, :, :, :].rearrange("p g e b -> p g b e"), AX_X, ALU.add).then_inc(s_i2, 1)
            dve.wait_ge(s_i2, 2)
            v.tensor_scalar(iv[:, 1], iv[:, 0], 0.0, None, ALU.is_lt).then_inc(s_i2, 1)
            dve.wait_ge(s_i2, 3)
            v.tensor_scalar(iv[:, 2], iv[:, 1], -2.0, 1.0, ALU.mult, ALU.add).then_inc(s_i2, 1)
            v.tensor_scalar(iv[:, 1], iv[:, 1], N / 2.0, -1.0, ALU.mult, ALU.add).then_inc(s_i2, 1)
            dve.wait_ge(s_i2, 5)
            v.tensor_tensor(iv[:, 2], iv[:, 2], iv[:, 0], ALU.mult).then_inc(s_i2, 1)
            dve.wait_ge(s_i2, 6)
            v.tensor_tensor(iv[:, 2], iv[:, 2], iv[:, 1], ALU.add).then_inc(s_i2, 1)
            dve.wait_ge(s_i2, 7)
            step(v.tensor_scalar(iv[:, 4], iv[:, 2], 0.0, None, ALU.max))
            step(v.tensor_scalar(post[:], post[:], CAP - 1, None, ALU.bitwise_and))
            v.tensor_scalar(iv[:, 0], post[:], N + 1.0, None, ALU.add).then_inc(s_i2, 1)
            v.tensor_scalar(iv[:, 1], iv[:, 2], 0.0, None, ALU.is_lt).then_inc(s_i2, 1)
            dve.wait_ge(s_i2, 9)
            step(v.tensor_tensor(iv[:, 3], iv[:, 0], iv[:, 1], ALU.mult))
            step(v.tensor_tensor(iv[:, 5], iv[:, 3], iv[:, 2], ALU.add))
            dve.wait_ge(s_tabT, 1)
            step(v.tensor_copy(gidx[:], bC[:, 0:P]))
            step(v.tensor_copy(sidx[:], bC[:, P:2 * P]))

            def stage(dst, table, it, n):
                at = it * 8 + 2 * n
                src = table[:, bass.ds(at, 2)] if not isinstance(at, int) else table[:, at:at + 2]
                return v.tensor_copy(dst[:, n % 4, :], src)

            def take_x(it, n):
                need(dve, mo["xTp"], it * 8 + (2 * n + 2))
                need(dve, mo["gp"], it * 4 + (n - 1))
                bank = bA if n % 2 == 0 else bC
                v.tensor_copy(xgT[n % 2][:, 1, :], bank[:, 0:CAP]).then_inc(mo["xTd"], 1)
                need(dve, mo["y_st"][n % 4], (it + n // 4) * 32)
                stage(sstage, sidx, it, n).then_inc(mo["sst"], 1)
                need(dve, mo["yc"], it * 8 + (2 * n - 6))
                need(dve, mo["x_ld"][n % 4], (it + n // 4) * 32 + 32)
                at = it * 4 + (D + n)
                col = bass.ds(at, 1) if not isinstance(at, int) else slice(at, at + 1)
                v.tensor_copy(wcol[n % 4][:, :].unsqueeze(2), xg[n % 4][:, :, col]).then_inc(mo["wc"], 1)

            def hidden(it, n):
                need(dve, mo["sg"], it * 4 + (n + 1))
                need(dve, mo["yp"], it * 4 + (n - 1))
                v.tensor_tensor(hm[n % 2][:], bST[n % 2][:, CAP:2 * CAP], sg[n % 2][:], ALU.mult).then_inc(mo["hm"], 1)

            for n in range(4):
                stage(gstage, gidx, 0, n).then_inc(mo["gst"], 1)
            def four(it, final=False):
                for n in range(4):
                    if not (final and n == 3):
                        take_x(it, n + 1)
                    if not final:
                        stage(gstage, gidx, it, n + 4).then_inc(mo["gst"], 1)
                    hidden(it, n)

            take_x(0, 0)
            four(0)
            with dve.Fori(1, E // 4 - 1) as it:
                four(it)
            four(E // 4 - 1, final=True)

            def finish(base, half, par, n_f):
                dve.wait_ge(mo["f_ld"][par], half * 96 + 96)
                a = fa[par]
                v.tensor_tensor(a[:, 0], a[:, 0], a[:, 1], ALU.add).then_inc(mo["fsum"], 1)
                v.tensor_tensor(a[:, 2], a[:, 2], a[:, 3], ALU.add).then_inc(mo["fsum"], 1)
                dve.wait_ge(mo["fsum"], base + 2)
                v.tensor_tensor(a[:, 0], a[:, 0], a[:, 2], ALU.add).then_inc(mo["fsum"], 1)
                dve.wait_ge(mo["fsum"], base + 3)
                v.tensor_tensor(a[:, 0], a[:, 0], fg[par][:, :].unsqueeze(1).to_broadcast([P, T, D]), ALU.mult
                                ).then_inc(mo["fsum"], 1)
                dve.wait_ge(mo["fsum"], base + 4)
                if not isinstance(n_f, int):
                    dve.wait_ge(mo["f_st"], n_f)
                v.tensor_tensor(fo[par][:], a[:, 0], fx[par][:], ALU.add).then_inc(mo["fsum"], 1)

            finish(0, 0, 0, 0)
            finish(5, 0, 1, 0)
            with dve.Fori(1, B // 2) as it:
                for par in range(2):
                    finish(it * 10 + 5 * par, it, par, it * 32 + (16 * par - 16))


_INS = ["L0_attn_x", "L0_attn_w_qkv", "L0_attn_b_qkv", "L0_attn_w_out", "L0_attn_b_out", "L0_ffn_gate_w",
        "L0_ffn_gate_bias", "L0_ffn_w_gate", "L0_ffn_w_up", "L0_ffn_w_down", "L0_c", "L0_wmod"]


def kernel(**inputs):
    import numpy as np
    import concourse.bacc as bacc
    from concourse.bass_utils import run_bass_kernel_spmd

    nc = bacc.Bacc("TRN2", target_bir_lowering=False, num_devices=1)
    arrays, args = {}, []
    for name in _INS:
        a = np.ascontiguousarray(inputs[name])
        arrays[name + "_dram"] = a
        args.append(nc.dram_tensor(name + "_dram", a.shape, mybir.dt.from_np(a.dtype), kind="ExternalInput").ap())
    out = nc.dram_tensor("out_dram", (B, S, D), F32, kind="ExternalOutput").ap()
    build(nc, *args, out)
    r = run_bass_kernel_spmd(nc, [arrays], core_ids=[0])
    return r.results[0]["out_dram"]
```

```python
from contextlib import ExitStack

import concourse.bass as bass
from concourse import mybir

F32 = mybir.dt.float32
BF16 = mybir.dt.bfloat16
F16 = mybir.dt.float16
I32 = mybir.dt.int32
I16 = mybir.dt.int16
U32 = mybir.dt.uint32
ALU = mybir.AluOpType
ACT = mybir.ActivationFunctionType
AX_X = mybir.AxisListType.X

P = 128
B, S, D = 8, 512, 256
H, HD, BAND = 16, 16, 64
E, K, G, TG = 64, 8, 8, 4
CAP, I = 256, 128
N = B * S
T = S // P
C = D // P
U = T + 1
KW = S + 2 * BAND
QUADS, HQ = H // 4, 4
SLOTS = QUADS * U
EG = E // G
SCALE = float(HD) ** -0.5
EPS = 1e-5
ROUTE_SCALE = 2.5
HW = D + E
LO, HI = 16, CAP // 16
FAR = 16.0 * 256
NEG = -1e30
TAKEN = -3e38
PAIRS = [(0, 0), (0, 1), (1, 0), (1, 1), (0, 2), (2, 0)]
MROW = len(PAIRS) * HD
KROWS = MROW + 2
NPT = 4
SEL_BEFORE = [0, 1, 3, 5, 7]
SEL_OF = [1, 2, 2, 2, 1]

PER = dict(
    xn=T, mcol=1, stats=T, aggr=T, rstd=4, hTp=C, hT=C, proj=4, p32=4, hpart=4, r32=4, mpart=4,
    lpart=4, vp=3, v=3, Sp=8 * QUADS, smax=2 * 8 * QUADS, m2=2 * QUADS, mTp=QUADS, mT=QUADS, STp=10 * QUADS,
    exp=10 * QUADS, cut=16 * QUADS, pv=10 * QUADS, oTs=QUADS, oTp=QUADS, rec=QUADS, on=QUADS,
    onTp=C, onT=C, op=2, t1=2, xb=2, x1=2, stats2=T, aggr2=T, rstd2=2, xn2=T, h2=T, h2Tp=C, h2T=C,
    lg=1, ex=1, route=38, pre=T + 1, vt=1, cntp=1, pos=4, oneh=3 * T, idxp=2, idx=2,
    qk_ld=192, mt_st=64, mrow_ld=64, c_ld=32, x1_st=16, h_st=16,
)

FROM_ONE = dict(
    SP=["h_st", "x1_st"], Pool=["xb", "rstd2"], Act=["t1"], PE=["op", "h2Tp", "lg", "cntp", "idxp"],
    DVE=["x1", "stats2", "xn2", "h2", "route", "pos", "oneh", "idx"],
)
STARTS = {name: 1 for names in FROM_ONE.values() for name in names}


ROUTE_PARTS = [0, 3, 7, 11, 14, 17, 20, 23, 27, 31, 32, 36, 38]


class Batch:

    def __init__(self, b, half, par):
        self.b, self.half, self.par = b, half, par


def batch(b):
    return Batch(b, b // 2, b % 2)


def build(nc, x, w_qkv, b_qkv, w_out, b_out, gate_w, gate_bias, w_gate, w_up, w_down, c, wmod, out):
    with ExitStack() as ctx:
        sems = {name: ctx.enter_context(nc.semaphore("s_" + name)) for name in PER}

        def sem(name):
            return ctx.enter_context(nc.semaphore(name))

        def ps(name, n=512):
            return ctx.enter_context(nc.psum_tensor(name, [P, n], F32))

        def dram(name, shape, dt=F32):
            return nc.dram_tensor(name, shape, dt, kind="Internal").ap()

        def hold(eng, s, v):
            if not isinstance(v, int):
                eng.compute_val(v)
                eng.wait_ge(s_const, NCONST)
            eng.wait_ge(s, v)

        def need(eng, s, v):
            if not isinstance(v, int) or v > 0:
                eng.wait_ge(s, v)

        def after(eng, name, bt, k, apart=False):
            v = bt.b * PER[name] + k
            if isinstance(v, int) and v <= 0:
                return
            v = v + STARTS.get(name, 0)
            assert isinstance(v, int) or v.min_val > 0, name
            if apart or eng is nc.sync or eng is nc.gpsimd:
                hold(eng, sems[name], v)
            else:
                eng.wait_ge(sems[name], v)

        def start_counts(eng, which):
            for name in FROM_ONE[which]:
                eng.sem_inc(sems[name], 1)

        def parts_stored(eng, bt, j, k):
            v = bt.b * 32 + 16 * k
            if isinstance(v, int) and v <= 0:
                return
            hold(eng, parts_st[j % 2], v)

        s_par = sem("params_loaded")
        s_par2 = sem("wmod_loaded")
        s_const = sem("constants_made")
        s_pe0 = sem("start_products")
        s_v0 = sem("start_vector_steps")
        s_a0 = sem("start_scalar_steps")
        s_cleared = sem("one_hots_cleared")
        s_ones = sem("rows_of_ones_loaded")
        s_mod_st = sem("mod_rows_stored")
        s_zero = sem("accumulators_zeroed")
        parts_st = [sem("parts_stored_even"), sem("parts_stored_odd")]
        x_ld = [sem("x_loaded_even"), sem("x_loaded_odd")]
        s_ix = sem("index_steps")
        s_i2 = sem("index_sums")
        s_ix2 = sem("operand_constants")
        s_v1 = sem("gate_steps")
        s_tabT = sem("tables_turned")
        s_fx = sem("residual_loaded")

        def sbt(stack, name, shape, dt=F32):
            return stack.enter_context(nc.sbuf_tensor(name, shape, dt))

        ident = sbt(ctx, "ident", [P, P])
        iacc = sbt(ctx, "iacc", [P, G, EG, LO])
        own_e = sbt(ctx, "own_e", [P, EG, LO])
        own_k = sbt(ctx, "own_k", [P, P // LO, LO])
        own_eh = sbt(ctx, "own_eh", [P, EG, 2])
        empty = sbt(ctx, "empty", [P, G, LO])
        ACCROWS = N + CAP
        ZCOLS = ACCROWS * D // B // P // 2

        bS = [ps("scores0"), ps("scores1")]
        bST = [ps("scoresT0"), ps("scoresT1")]
        bO = ps("outT")
        bT = ps("turns")
        bA = ps("stageA")
        bC = ps("stageC")

        parts_d = [dram(f"parts_d{i}", [2, 3, D, S], BF16) for i in range(2)]
        mt_d = dram("mt_d", [2 * HQ * T, P], BF16)
        mod_d = dram("mod_d", [B, 4, D])
        x1_d = dram("x1_d", [B, S, D])
        htab = dram("htab", [N, HW])
        acc_d = [dram(f"acc_d{i}", [ACCROWS, D]) for i in range(2)]

        att = ExitStack()
        sb = lambda name, shape, dt=F32: sbt(att, name, shape, dt)
        zero = sb("zero", [P, ZCOLS])
        identb = sb("identb", [P, P], BF16)
        onesb = sb("onesb", [P, P], BF16)
        before = sb("before", [P, P], BF16)
        mask = sb("mask", [P, 3, 2 * P], BF16)
        digits = sb("digits", [P, LO, EG], I16)
        lowerg = sb("lowerg", [P, G, G])
        valt = sb("valt", [P, N // P])
        half_c = sb("half_c", [P, T])
        wqkv = sb("wqkv", [P, C, 3 * D])
        wo = sb("wo", [P, C, D])
        bqk = sb("bqk", [P, 4])
        bv = sb("bv", [P, D])
        bo = sb("bo", [P, D])
        gwT = sb("gwT", [P, C, E])
        gb = sb("gbias", [P, E])
        silT = sb("silT", [P, C, B])
        modT = sb("modT", [P, B, 4])
        xt = sb("xt", [P, T, D])
        xn = sb("xn", [P, T, D])
        stats = sb("stats", [P, T, 6])
        mv = sb("mv", [P, T, 2])
        ve = sb("ve", [P, T])
        rs = sb("rs", [P, T])
        nmean = sb("nmean", [P, T])
        mcol = sb("mcol", [P, 4])
        hT = sb("hT", [P, C, KW])
        p32 = [sb(f"p32_{i}", [P, S]) for i in range(2)]
        r32 = sb("r32", [P, S])
        parts = sb("parts", [P, 2, 3, S], BF16)
        Qs = [sb(f"Qs{i}", [P, H, S], BF16) for i in range(2)]
        Ks = [sb(f"Ks{i}", [P, H, KW], BF16) for i in range(2)]
        Va = [sb(f"Va{i}", [P, U, H, 32]) for i in range(2)]
        junk = sb("junk", [P, 2, 2 * P], BF16)
        mrowmax = sb("mrowmax", [P, HQ, T])
        M2 = sb("M2", [P, P], BF16)
        MT = sb("MT", [32, P], BF16)
        PT = [sb(f"PT{i}", [P, 2, 2 * P]) for i in range(NPT)]
        OTs = sb("OTs", [P, S])
        rec = sb("rec", [P, T, HQ])
        on = sb("on", [P, T, D])
        onT = sb("onT", [P, C, S])
        xc = sb("xc", [P, T, D])
        mr = sb("mr", [P, 3, D])
        gbo = sb("gbo", [P, D])
        x1 = sb("x1", [P, T, D])
        stats2 = sb("stats2", [P, T, 6])
        mv2 = sb("mv2", [P, T, 2])
        ve2 = sb("ve2", [P, T])
        rs2 = sb("rs2", [P, T])
        H2 = sb("H2", [P, T, HW])
        xn2 = H2[:, :, 0:D]
        h2T = onT
        ex = sb("ex", [P, T * E])
        sc = sb("sc", [P, T * E])
        sfc = sb("sfc", [P, T * G, EG])
        tmp = sb("tmp", [P, T * G, EG])
        rep = sb("rep", [P, T * G, EG])
        pairs = sb("pairs", [P, 6, T * G, 4])
        gs = sb("gs", [P, 4, T * G])
        cmp1 = sb("cmp1", [P, T, G, G])
        cmp2 = sb("cmp2", [P, T, G, G])
        top8 = sb("top8", [P, T, 8])
        selb = sb("selb", [P, T * E], BF16)
        wsum = sb("wsum", [P, 3, T])
        Spre = sb("Spre", [P, T + 1, E], BF16)
        posf = ex
        posi = sb("posi", [P, 3, T * E], I16)
        vt = sb("vt", [P, T])
        oneh = sb("oneh", [P, T + T + 1, G, LO, EG], F16)
        wm = oneh[:, 0:6].rearrange("p t g b e -> p (t g b e)").bitcast(F32).rearrange("p (c n) -> p c n", c=C)
        bits_e = tmp[:, 0:16, :].rearrange("p g e -> p (g e)").bitcast(I32).rearrange("p (e b) -> p e b", b=LO)
        bits_k = rep[:, 0:16, :].rearrange("p g e -> p (g e)").bitcast(I32).rearrange("p (k b) -> p k b", b=LO)
        bits_eh = tmp[:, 16:18, :].rearrange("p g e -> p (g e)").bitcast(I32).rearrange("p (e h) -> p e h", h=2)
        high = rep[:, 16:32, :].rearrange("p g e -> p (g e)").bitcast(I32).rearrange("p (g b) -> p g b", b=LO)
        gw = on[0:E, 0, :]
        cin = xc[0:B, 0, :]
        sil = x1[0:B, 0:3, :]
        gates = onT[0:B, :, :].rearrange("b i (k d) -> b i k d", k=2)
        att.close()

        moe = ExitStack()
        sb = lambda name, shape, dt=F32: sbt(moe, name, shape, dt)
        NW, NX, NY = 4, 4, 4
        iv = sb("iv", [P, 6, G, LO])
        spread = sb("spread", [P, 2, G, P // LO, LO])
        gidx = sb("gidx", [P, 2 * E], U32)
        sidx = sb("sidx", [P, 2 * E], U32)
        gstage = sb("gstage", [P, 4, 2], U32)
        sstage = sb("sstage", [P, 4, 2], U32)
        wgu = [sb(f"wgu{i}", [P, 2, C, I]) for i in range(NW)]
        wd = [sb(f"wd{i}", [P, D]) for i in range(NW)]
        xg = [sb(f"xg{i}", [P, 2, HW]) for i in range(NX)]
        wcol = [sb(f"wcol{i}", [P, 2]) for i in range(NX)]
        xgT = [sb(f"xgT{i}", [P, C, CAP]) for i in range(2)]
        sg = [sb(f"sg{i}", [P, CAP]) for i in range(2)]
        hm = [sb(f"hm{i}", [P, CAP]) for i in range(2)]
        ys = [sb(f"ys{i}", [P, 2, D]) for i in range(NY)]
        NF = 8
        fx = sb("fx", [P, B * T, D])
        fg = sb("fg", [P, B, D])
        fa = [sb(f"fa{i}", [P, 2, T, D]) for i in range(NF)]
        moe.close()
        eng_moe = dict(
            w_ld=[sem(f"weights_loaded{i}") for i in range(NW)],
            x_ld=[sem(f"rows_gathered{i}") for i in range(NX)],
            y_st=[sem(f"rows_added{i}") for i in range(NY)],
            gst=sem("gather_indices_staged"), sst=sem("scatter_indices_staged"),
            xTp=sem("rows_turned"), xTc=sem("first_features_kept"), xTd=sem("second_features_kept"), gp=sem("gate_up_made"),
            sg=sem("silu_done"), wc=sem("slot_weights_staged"),
            hm=sem("hidden_done"), yp=sem("expert_out_made"), yc=sem("expert_out_scaled"),
            f_ld=[sem(f"sums_loaded{i}") for i in range(NF)], fsum=sem("last_sums"), fout=sem("out_made"),
            f_st=sem("out_stored"),
        )
        mo = eng_moe

        NCONST = 22
        NSET = 21
        PROJ_SLOTS = (4, 5, 7, 8)
        STORE_SLOTS = (5, 7, 8, 10)
        SPLITS = {4: 2, 5: 2, 6: 1, 7: 2, 8: 2, 9: 2, 10: 1}
        ROUTE_SLOTS = {13: [0, 1, 2, 3], 14: [4, 5, 6, 7], 15: [8], 16: [9], 17: [10], 19: [11]}
        FILLS = {0: [0, 1, 2], 1: [3, 4, 5], 2: [6, 7]}
        block = ctx.enter_context(nc.Block())

        def loops(eng, body, prolog=None, epilog=None):
            body(None, batch(0), batch(1))
            with eng.Fori(0, (B - 2) // 2) as it:
                for j in range(2):
                    now = Batch(it * 2 + (1 + j), it + j, 1 - j)
                    prev = Batch(it * 2 + j, it, j)
                    nxt = Batch(it * 2 + (2 + j), it + 1, j)
                    body(prev, now, nxt)
            body(batch(B - 2), batch(B - 1), None)

        @block.sync
        def _(sp):
            start_counts(sp, "SP")
            bc = lambda ap, n: ap.rearrange("(o d) -> o d", o=1).to_broadcast([P, n])
            sp.dma_start(xt[:], x[0].rearrange("(t p) d -> p t d", p=P)).then_inc(x_ld[0], 16)
            sp.dma_start(cin, c[:, :]).then_inc(s_par, 16)
            sp.dma_start(wm, wmod.rearrange("(c p) n -> p c n", p=P)).then_inc(s_par2, 16)
            sp.dma_start(wqkv[:], w_qkv.rearrange("(c p) n -> p c n", p=P)).then_inc(s_par, 16)
            sp.dma_start(bqk[:], b_qkv[0:4 * P].rearrange("(c p) -> p c", p=P),
                         allow_slow_non_contiguous=True).then_inc(s_par, 16)
            sp.dma_start(bv[:], bc(b_qkv[2 * D:3 * D], D)).then_inc(s_par, 16)
            sp.dma_start(bo[:], bc(b_out, D)).then_inc(s_par, 16)
            sp.dma_start(gb[:], bc(gate_bias, E)).then_inc(s_par, 16)
            sp.dma_start(gw, gate_w[:, :]).then_inc(s_par, 16)
            sp.dma_start(wo[:], w_out.rearrange("(c p) n -> p c n", p=P)).then_inc(s_par, 16)
            sp.wait_ge(s_const, NCONST)
            for i in range(2):
                sp.dma_start(Ks[i][MROW:KROWS, :, :].rearrange("a h (r n) -> a (h r) n", n=P),
                             onesb[0:2, :].unsqueeze(1).to_broadcast([2, H * KW // P, P])).then_inc(s_ones, 16)
            sp.wait_ge(s_v0, 9)
            sp.dma_start(mod_d[:, 0:4:3, :], gates[:, 0, :, :]).then_inc(s_mod_st, 16)
            sp.dma_start(mod_d[:, 1:3, :], gates[:, 1, :, :]).then_inc(s_mod_st, 16)
            def zero_acc(bt):
                i = bass.ds(bt.b, 1) if not isinstance(bt.b, int) else slice(bt.b, bt.b + 1)
                for acc in acc_d:
                    for h in range(2):
                        dst = acc.rearrange("r d -> (r d)").rearrange("(b h p n) -> b h p n", b=B, h=2, p=P)[i, h]
                        sp.dma_start(dst.rearrange("o p n -> p (o n)"), zero[:]).then_inc(s_zero, 16)

            def load_x(bt):
                after(sp, "xn", bt, 0)
                row = x[bass.ds(bt.b, 1)] if not isinstance(bt.b, int) else x[bt.b:bt.b + 1]
                sp.dma_start(xt[:], row.rearrange("o (t p) d -> p (o t) d", p=P)).then_inc(x_ld[bt.par], 16)

            def load_c(bt):
                after(sp, "h2", bt, 0)
                after(sp, "x1", bt, 0)
                i = bass.ds(bt.b, 1) if not isinstance(bt.b, int) else slice(bt.b, bt.b + 1)
                sp.dma_start(xc[:], x[i].rearrange("o (t p) d -> p (o t) d", p=P)).then_inc(sems["c_ld"], 16)
                sp.dma_start(mr[:], mod_d[i, 0:3, :].rearrange("o k d -> o (k d)").to_broadcast([P, 3 * D])
                             ).then_inc(sems["c_ld"], 16)

            def store_parts(bt, j):
                after(sp, "lpart", bt, j + 1)
                after(sp, "mpart", bt, j + 1)
                after(sp, "hpart", bt, j + 1)
                if j % 2 == 0:
                    after(sp, "qk_ld", bt, 0)
                dst = parts_d[bt.par][j // 2, :, (j % 2) * P:(j % 2 + 1) * P, :]
                sp.dma_start(dst.rearrange("k p s -> p k s"), parts[:, j % 2, :, :]).then_inc(parts_st[j % 2], 16)

            def load_stack(bt, which):
                parts_stored(sp, bt, 0, which + 1)
                parts_stored(sp, bt, 1, which + 1)
                if not isinstance(bt.b, int) or bt.b >= 2:
                    after(sp, "STp", Batch(bt.b - 1, 0, 0), 0)
                dst = Qs[bt.par] if which == 0 else Ks[bt.par]
                lo = 0 if which == 0 else BAND
                for n, pair in enumerate(PAIRS):
                    src = parts_d[bt.par][which, pair[which]].rearrange("(h d) s -> d h s", d=HD)
                    sp.dma_start(dst[n * HD:(n + 1) * HD, :, lo:lo + S], src).then_inc(sems["qk_ld"], 16)

            def mrows(bt, g):
                after(sp, "mT", bt, g + 1)
                sp.dma_start(mt_d[:, :], MT[:]).then_inc(sems["mt_st"], 16)
                after(sp, "mt_st", bt, 16 * (g + 1))
                sp.dma_start(Qs[bt.par][MROW:KROWS, HQ * g:HQ * g + HQ, :].rearrange("a h q -> a (h q)"),
                             mt_d.rearrange("(a r) q -> a (r q)", a=2)).then_inc(sems["mrow_ld"], 16)

            def body(prev, now, nxt):
                for slot in range(SLOTS):
                    g, u = divmod(slot, U)
                    if slot == 0 and nxt:
                        load_x(nxt)
                    if slot == 0 and prev:
                        load_c(prev)
                    if u == 3 and (g < QUADS - 1 or nxt):
                        mrows(*((now, g + 1) if g < QUADS - 1 else (nxt, 0)))
                    if nxt and slot in STORE_SLOTS:
                        store_parts(nxt, STORE_SLOTS.index(slot))
                    if nxt and slot in (8, 11):
                        load_stack(nxt, (slot - 8) // 3)
                    if slot == 12:
                        zero_acc(now)
                    if prev and slot == 9:
                        store_c(prev, 0)
                    if prev and slot == 19:
                        store_c(prev, 1)

            def store_c(bt, which):
                i = bass.ds(bt.b, 1) if not isinstance(bt.b, int) else slice(bt.b, bt.b + 1)
                if which == 0:
                    after(sp, "x1", bt, 2)
                    sp.dma_start(x1_d[i].rearrange("o (t p) d -> p (o t) d", p=P), x1[:]).then_inc(sems["x1_st"], 16)
                else:
                    after(sp, "route", bt, PER["route"])
                    after(sp, "h2", bt, T)
                    sp.dma_start(htab.rearrange("(b t p) d -> b p t d", p=P, t=T)[i].rearrange("o p t d -> p (o t) d"),
                                 H2[:]).then_inc(sems["h_st"], 16)

            first = batch(0)
            for j in range(4):
                store_parts(first, j)
                if j % 2:
                    load_stack(first, j // 2)
            mrows(first, 0)
            sp.wait_ge(s_mod_st, 32)
            loops(sp, body)
            last = batch(B - 1)
            load_c(last)
            store_c(last, 0)
            store_c(last, 1)

            def load_w(e, half, n):
                sp.dma_start(wgu[n][:, 0], w_gate[e].rearrange("o (c p) i -> p (o c) i", p=P)).then_inc(mo["w_ld"][n], 16)
                sp.dma_start(wgu[n][:, 1], w_up[e].rearrange("o (c p) i -> p (o c) i", p=P)).then_inc(mo["w_ld"][n], 16)
                sp.dma_start(wd[n][:], w_down[e].rearrange("o i d -> i (o d)")).then_inc(mo["w_ld"][n], 16)

            for n in range(NW):
                load_w(slice(n, n + 1), 0, n)
            with sp.Fori(1, E // NW) as it:
                for n in range(NW):
                    hold(sp, mo["yp"], it * NW + (n - NW + 1))
                    load_w(bass.ds(it * NW + n, 1), it, n)

            sp.dma_start(fx[:], x1_d.rearrange("b (t p) d -> p (b t) d", p=P)).then_inc(s_fx, 16)
            sp.dma_start(fg[:], mod_d[:, 3, :].unsqueeze(0).to_broadcast([P, B, D])).then_inc(s_fx, 16)
            for n in range(NY):
                sp.wait_ge(mo["y_st"][n], 32 * E // NY)

            def load_f(i, n):
                for k in range(2):
                    sp.dma_start(fa[n][:, k], acc_d[k][0:N, :].rearrange("(b t p) d -> b p t d", b=B, p=P)[i]
                                 .rearrange("o p t d -> p (o t) d")).then_inc(mo["f_ld"][n], 16)

            def store_f(i, n):
                sp.dma_start(out[i].rearrange("o (t p) d -> p (o t) d", p=P), fa[n][:, 0]).then_inc(mo["f_st"], 16)

            for b in range(B):
                if b >= NF:
                    sp.wait_ge(mo["f_st"], 16 * (b - NF + 1))
                load_f(slice(b, b + 1), b % NF)
                if b >= NF - 1:
                    sp.wait_ge(mo["fout"], b - NF + 2)
                    store_f(slice(b - NF + 1, b - NF + 2), (b + 1) % NF)
            for b in range(B - NF + 1, B):
                sp.wait_ge(mo["fout"], b + 1)
                store_f(slice(b, b + 1), b % NF)
            sp.wait_ge(mo["f_st"], 16 * B)

        @block.gpsimd
        def _(pool):
            start_counts(pool, "Pool")
            gp = nc.gpsimd
            n = [0]
            nothing = pool.to_reg(0.0)
            last_row = pool.to_reg(N - 1)
            last_acc = pool.to_reg(ACCROWS - 1)

            def const(ins):
                ins.then_inc(s_const, 1)
                n[0] += 1
                pool.wait_ge(s_const, n[0])

            const(gp.memset(ident[:], 0.0))
            const(gp.affine_select(out=ident[:], in_=ident[:], compare_op=ALU.not_equal, fill=1.0, base=0,
                                   pattern=[[-1, P]], channel_multiplier=1))
            const(gp.tensor_copy(identb[:], ident[:]))
            const(gp.memset(onesb[:], 1.0))
            const(gp.affine_select(out=before[:], in_=onesb[:], compare_op=ALU.is_gt, fill=0.0, base=0,
                                   pattern=[[1, P]], channel_multiplier=-1))
            const(gp.memset(mask[:], 0.0))
            const(gp.affine_select(out=mask[:], in_=mask[:], compare_op=ALU.is_ge, fill=NEG, base=0,
                                   pattern=[[0, 3], [1, 2 * P]], channel_multiplier=-1))
            const(gp.affine_select(out=mask[:], in_=mask[:], compare_op=ALU.is_ge, fill=NEG, base=2 * BAND,
                                   pattern=[[0, 3], [-1, 2 * P]], channel_multiplier=1))
            const(gp.memset(mask[:, 0, 0:BAND], NEG))
            const(gp.memset(mask[:, 2, 2 * P - BAND:2 * P], NEG))
            const(gp.iota(digits[:], pattern=[[1, LO], [0, EG]], base=0, channel_multiplier=0))
            const(gp.memset(lowerg[:], 1.0))
            const(gp.affine_select(out=lowerg[:], in_=lowerg[:], compare_op=ALU.is_gt, fill=0.0, base=0,
                                   pattern=[[1, G], [-1, G]], channel_multiplier=0))
            half = N // P // 2
            const(gp.iota(valt[:, 0:half], pattern=[[P, half]], base=1, channel_multiplier=1,
                          allow_small_or_imprecise_dtypes=True))
            const(gp.iota(valt[:, half:], pattern=[[-P, half]], base=-1, channel_multiplier=-1,
                          allow_small_or_imprecise_dtypes=True))
            const(gp.memset(half_c[:], -0.5))
            const(gp.iota(bits_e, pattern=[[-1, EG], [0, LO]], base=P, channel_multiplier=1))
            const(gp.iota(bits_k, pattern=[[-EG, P // LO], [0, LO]], base=P, channel_multiplier=1))
            const(gp.iota(bits_eh, pattern=[[-1, EG], [-P // 2, 2]], base=P, channel_multiplier=1))
            const(gp.iota(high, pattern=[[0, G], [0, LO]], base=0, channel_multiplier=LO // EG))
            const(gp.iota(empty[:], pattern=[[0, G], [1, LO]], base=N + 1, channel_multiplier=0,
                          allow_small_or_imprecise_dtypes=True))
            const(gp.memset(zero[:], 0.0))
            assert n[0] == NCONST

            def a_rstd(bt):
                after(pool, "aggr", bt, T)
                after(pool, "xn", bt, 0)
                gp.tensor_scalar(ve[:], mv[:, :, 1], EPS, None, ALU.add).then_inc(sems["rstd"], 1)
                after(pool, "rstd", bt, 1)
                gp.tensor_tensor(rs[:], ve[:], half_c[:], ALU.pow).then_inc(sems["rstd"], 1)
                gp.tensor_scalar(nmean[:], mv[:, :, 0], -1.0, None, ALU.mult).then_inc(sems["rstd"], 1)
                after(pool, "rstd", bt, 3)
                gp.tensor_tensor(nmean[:], nmean[:], rs[:], ALU.mult).then_inc(sems["rstd"], 1)

            def a_split(bt, n):
                j, k = divmod(n, 3)
                if k == 0:
                    after(pool, "hpart", bt, j + 1)
                    parts_stored(pool, bt, j, j // 2)
                    after(pool, "lpart", bt, j)
                    gp.tensor_tensor(r32[:], p32[j % 2][:], parts[:, j % 2, 0, :], ALU.subtract
                                     ).then_inc(sems["r32"], 1)
                elif k == 1:
                    gp.tensor_tensor(parts[:, j % 2, 1, :], p32[j % 2][:], parts[:, j % 2, 0, :], ALU.subtract
                                     ).then_inc(sems["mpart"], 1)
                else:
                    after(pool, "r32", bt, j + 1)
                    after(pool, "mpart", bt, j + 1)
                    gp.tensor_tensor(parts[:, j % 2, 2, :], r32[:], parts[:, j % 2, 1, :], ALU.subtract
                                     ).then_inc(sems["lpart"], 1)

            def cuts(bt, g, u, p):
                if True:
                    m = 10 * g + 2 * u + p
                    pt = PT[m % NPT]
                    after(pool, "exp", bt, m + 1)
                    if u > 0:
                        v = pt[:, :, 0:P]
                        gp.affine_select(out=v, in_=v, compare_op=ALU.is_ge, fill=nothing, base=0,
                                         pattern=[[0, 2], [1, P]], channel_multiplier=-1).then_inc(sems["cut"], 1)
                    if u < U - 1:
                        v = pt[:, :, 0:P] if u == 0 else pt[:, :, P:2 * P]
                        gp.affine_select(out=v, in_=v, compare_op=ALU.is_ge, fill=nothing, base=0,
                                         pattern=[[0, 2], [-1, P]], channel_multiplier=1).then_inc(sems["cut"], 1)

            def c_xb(bt):
                after(pool, "c_ld", bt, 32)
                after(pool, "xb", bt, 0)
                gp.tensor_tensor(gbo[:], mr[:, 0, :], bo[:], ALU.mult).then_inc(sems["xb"], 1)
                after(pool, "xb", bt, 1)
                gp.tensor_tensor(xc[:], xc[:], gbo[:, :].unsqueeze(1).to_broadcast([P, T, D]), ALU.add
                                 ).then_inc(sems["xb"], 1)

            def c_rstd(bt):
                after(pool, "aggr2", bt, T)
                after(pool, "xn2", bt, 0)
                gp.tensor_scalar(ve2[:], mv2[:, :, 1], EPS, None, ALU.add).then_inc(sems["rstd2"], 1)
                after(pool, "rstd2", bt, 1)
                gp.tensor_tensor(rs2[:], ve2[:], half_c[:], ALU.pow).then_inc(sems["rstd2"], 1)

            def body(prev, now, nxt):
                for slot in range(SLOTS):
                    g, u = divmod(slot, U)
                    for p in range(2):
                        cuts(now, g, u, p)
                        if nxt and p < SPLITS.get(slot, 0):
                            a_split(nxt, sum(n for at, n in SPLITS.items() if at < slot) + p)
                    if nxt and slot == 1:
                        a_rstd(nxt)
                    if prev and slot == 2:
                        c_xb(prev)
                    if prev and slot == 8:
                        c_rstd(prev)

            pool.wait_ge(s_par, 16 * 8)
            a_rstd(batch(0))
            for n in range(12):
                a_split(batch(0), n)
            pool.wait_ge(s_pe0, 7)
            gp.memset(oneh[:, 0:2 * T], 0.0).then_inc(s_cleared, 1)
            loops(pool, body)
            last = batch(B - 1)
            c_xb(last)
            c_rstd(last)

            done = Batch(B, 0, 0)
            def gather(n4, count_half):
                for h in range(2):
                    pool.indirect_dma_start(
                        out=xg[n4][:, h, :], out_offset=None, in_=htab[:, :],
                        in_offset=bass.IndirectOffsetOnAxis(ap=gstage[:, n4, h:h + 1], axis=0),
                        bounds_check=last_row, oob_is_err=False).then_inc(mo["x_ld"][n4], 16)

            def scatter(n4):
                for h in range(2):
                    pool.indirect_dma_start(
                        out=acc_d[n4 % 2][:, :], in_=ys[n4][:, h, :], in_offset=None,
                        out_offset=bass.IndirectOffsetOnAxis(ap=sstage[:, n4, h:h + 1], axis=0),
                        bounds_check=last_acc, oob_is_err=True, compute_op=ALU.add).then_inc(mo["y_st"][n4], 16)

            after(pool, "h_st", done, 0)
            pool.wait_ge(s_zero, 16 * 4 * B)
            pool.wait_ge(mo["gst"], NX)
            for n4 in range(3):
                gather(n4, 0)
            def four(it):
                for n4 in range(4):
                    m4 = (n4 + 3) % 4
                    hold(pool, mo["gst"], it * 4 + (n4 + 4))
                    if not isinstance(it, int) or n4 > 0:
                        hold(pool, mo["gp"], it * 4 + n4)
                        hold(pool, mo["wc"], it * 4 + n4)
                    gather(m4, 0)
                    hold(pool, mo["sst"], it * 4 + (n4 + 1))
                    hold(pool, mo["yc"], it * 8 + (2 * n4 + 2))
                    if n4 >= 2:
                        hold(pool, mo["y_st"][n4 - 2], it * 32 + 32)
                    elif not isinstance(it, int):
                        hold(pool, mo["y_st"][n4 + 2], it * 32)
                    scatter(n4)

            four(0)
            with pool.Fori(1, E // 4 - 1) as it:
                four(it)
            for n4 in range(4):
                e = E - 4 + n4
                if n4 == 0:
                    pool.wait_ge(mo["gst"], E)
                    pool.wait_ge(mo["gp"], e)
                    pool.wait_ge(mo["wc"], e)
                    gather(3, 0)
                pool.wait_ge(mo["sst"], e + 1)
                pool.wait_ge(mo["yc"], 2 * e + 2)
                pool.wait_ge(mo["y_st"][(n4 + 2) % 4], 32 * (E // 4 - (n4 < 2)))
                scatter(n4)

            pool.wait_ge(s_fx, 32)
            for b in range(B):
                a = fa[b % NF]
                pool.wait_ge(mo["fsum"], 2 * b + 2)
                gp.tensor_tensor(a[:, 0], a[:, 0], fx[:, b * T:(b + 1) * T, :], ALU.add).then_inc(mo["fout"], 1)

        @block.scalar
        def _(act):
            start_counts(act, "Act")
            sc_ = nc.scalar
            act.wait_ge(s_par, 16 * 8)
            sc_.activation(sil[:, 0, :], cin, ACT.Exp, scale=-1.0).then_inc(s_a0, 1)
            act.wait_ge(s_v0, 1)

            def a_norm(bt):
                after(act, "rstd", bt, 4)
                after(act, "hTp", bt, 0)
                for t in range(T):
                    sc_.activation(xn[:, t, :], xt[:, t, :], ACT.Identity, scale=rs[:, t:t + 1], bias=nmean[:, t:t + 1]
                                   ).then_inc(sems["xn"], 1)

            def a_hT(bt, k):
                after(act, "hTp", bt, k + 1)
                after(act, "mcol", bt, 1)
                after(act, "vp", bt, 0)
                sc_.activation(hT[:, k, BAND:BAND + S], bA[:, :], ACT.Identity, scale=mcol[:, 2 + k:3 + k],
                               bias=mcol[:, k:k + 1]).then_inc(sems["hT"], 1)

            def a_p32(bt, j):
                after(act, "proj", bt, j + 1)
                if j >= 2:
                    after(act, "lpart", bt, j - 1)
                else:
                    after(act, "lpart", bt, 0)
                sc_.activation(p32[j % 2][:], bA[:, :], ACT.Identity, scale=SCALE if j < 2 else 1.0,
                               bias=bqk[:, j:j + 1]).then_inc(sems["p32"], 1)
                after(act, "p32", bt, j + 1)
                parts_stored(act, bt, j, j // 2)
                sc_.activation(parts[:, j % 2, 0, :], p32[j % 2][:], ACT.Copy).then_inc(sems["hpart"], 1)

            def exps(bt, g, u):
                for p in range(2):
                    m = 10 * g + 2 * u + p
                    after(act, "STp", bt, m + 1)
                    after(act, "pv", bt, m - NPT + 1)
                    w = P if u in (0, U - 1) else 2 * P
                    src = bST[m % 2][:, 0:2 * w].rearrange("p (h q) -> p h q", h=2)
                    sc_.activation(PT[m % NPT][:, :, 0:w], src, ACT.Exp).then_inc(sems["exp"], 1)

            def take_mT(bt, g):
                after(act, "mTp", bt, g + 1)
                after(act, "mrow_ld", bt, 16 * g)
                sc_.activation(MT[:], bT[0:32, 0:P // 2].bitcast(BF16), ACT.Copy).then_inc(sems["mT"], 1)

            def take_oT(bt, g):
                after(act, "pv", bt, 10 * g + 10)
                after(act, "oTp", bt, g)
                sc_.activation(OTs[:], bO[:, :], ACT.Copy).then_inc(sems["oTs"], 1)

            def c_onT(bt, k):
                after(act, "onTp", bt, k + 1)
                after(act, "op", bt, 0)
                sc_.activation(onT[:, k, :], bC[:, :], ACT.Copy).then_inc(sems["onT"], 1)

            def c_h2T(bt, k):
                after(act, "h2Tp", bt, k + 1)
                after(act, "lg", bt, 0)
                sc_.activation(h2T[:, k, :], bC[:, :], ACT.Copy).then_inc(sems["h2T"], 1)

            def c_ex(bt):
                after(act, "lg", bt, 1)
                after(act, "pos", bt, 0)
                sc_.activation(ex[:], bC[:, 0:T * E], ACT.Exp, scale=-1.0).then_inc(sems["ex"], 1)

            def body(prev, now, nxt):
                for slot in range(SLOTS):
                    g, u = divmod(slot, U)
                    exps(now, g, u)
                    if u == 0 and (g > 0 or prev):
                        take_oT(*((now, g - 1) if g > 0 else (prev, QUADS - 1)))
                    if u == 3 and (g < QUADS - 1 or nxt):
                        take_mT(*((now, g + 1) if g < QUADS - 1 else (nxt, 0)))
                    if nxt and slot == 1:
                        a_norm(nxt)
                    if nxt and slot in (2, 3):
                        a_hT(nxt, slot - 2)
                    if nxt and slot in PROJ_SLOTS:
                        a_p32(nxt, PROJ_SLOTS.index(slot))
                    if prev and slot in (3, 4):
                        c_onT(prev, slot - 3)
                    if prev and slot in (10, 11):
                        c_h2T(prev, slot - 10)
                    if prev and slot == 12:
                        c_ex(prev)

            a_norm(batch(0))
            a_hT(batch(0), 0)
            a_hT(batch(0), 1)
            for j in range(4):
                a_p32(batch(0), j)
            take_mT(batch(0), 0)
            loops(act, body)
            last = batch(B - 1)
            take_oT(last, QUADS - 1)
            for k in range(C):
                c_onT(last, k)
            for k in range(C):
                c_h2T(last, k)
            c_ex(last)

            def take_x(it, n):
                need(act, mo["xTp"], it * 8 + (2 * n + 1))
                need(act, mo["gp"], it * 4 + (n - 1))
                sc_.activation(xgT[n % 2][:, 0, :], bS[n % 2][:, 0:CAP], ACT.Copy).then_inc(mo["xTc"], 1)

            def silu(it, n):
                need(act, mo["gp"], it * 4 + (n + 1))
                need(act, mo["hm"], it * 4 + (n - 1))
                sc_.activation(sg[n % 2][:], bST[n % 2][:, 0:CAP], ACT.Silu).then_inc(mo["sg"], 1)

            def scale_y(it, n):
                need(act, mo["yp"], it * 4 + (n + 1))
                need(act, mo["wc"], it * 4 + (n + 1))
                need(act, mo["y_st"][n % 4], (it + n // 4) * 32)
                yb = bO if n % 2 == 0 else bT
                for h in range(2):
                    sc_.activation(ys[n % 4][:, h, :], yb[:, h * D:(h + 1) * D], ACT.Copy,
                                   scale=wcol[n % 4][:, h:h + 1]).then_inc(mo["yc"], 1)

            def four(it, first=False, final=False):
                for n in range(4):
                    silu(it, n)
                    if not (final and n == 3):
                        take_x(it, n + 1)
                    if not (first and n == 0):
                        scale_y(it, n - 1)

            take_x(0, 0)
            four(0, first=True)
            with act.Fori(1, E // 4 - 1) as it:
                four(it)
            four(E // 4 - 1, final=True)
            scale_y(E // 4 - 1, 3)

        @block.tensor
        def _(pe):
            start_counts(pe, "PE")
            mm = nc.tensor.matmul
            pe.wait_ge(s_const, NCONST)
            pe.wait_ge(s_v0, 3)
            for k in range(C):
                nc.tensor.transpose(bA[:, k * B:(k + 1) * B], sil[:, 2, k * P:(k + 1) * P], ident[0:B, 0:B]
                                    ).then_inc(s_pe0, 1)
            for k in range(C):
                nc.tensor.transpose(bC[:, k * E:(k + 1) * E], gw[:, k * P:(k + 1) * P], ident[0:E, 0:E]
                                    ).then_inc(s_pe0, 1)
            pe.wait_ge(s_v0, 5)
            pe.wait_ge(s_par2, 16)
            for n in range(4):
                col = (n // 2) * D + (n % 2) * P
                for k in range(C):
                    last = mm(bT[:, n * B:(n + 1) * B], wm[:, k, col:col + P], silT[:, k, :], start=(k == 0), stop=(k == C - 1))
            last.then_inc(s_pe0, 1)
            for n, bank in enumerate((bS[0], bS[1])):
                for q, col in enumerate(((2, 5), (3, 4))[n]):
                    for k in range(C):
                        last = mm(bank[0:B, q * D:(q + 1) * D], silT[:, k, :], wm[:, k, col * D:(col + 1) * D],
                                  start=(k == 0), stop=(k == C - 1))
                last.then_inc(s_pe0, 1)

            def a_hT(bt, k):
                after(pe, "xn", bt, T)
                if k == 0:
                    after(pe, "v", bt, 0)
                else:
                    after(pe, "hT", bt, k)
                for t in range(T):
                    last = nc.tensor.transpose(bA[:, t * P:(t + 1) * P], xn[:, t, k * P:(k + 1) * P], ident[:])
                last.then_inc(sems["hTp"], 1)

            def a_proj(bt, j):
                if j == 0:
                    after(pe, "hT", bt, C)
                else:
                    after(pe, "p32", bt, j)
                for k in range(C):
                    last = mm(bA[:, :], wqkv[:, k, j * P:(j + 1) * P], hT[:, k, BAND:BAND + S], start=(k == 0), stop=(k == C - 1))
                last.then_inc(sems["proj"], 1)

            def a_v(bt, j):
                if j == 0:
                    after(pe, "p32", bt, 4)
                else:
                    after(pe, "v", bt, j)
                for i, u in enumerate(range(2 * j, min(2 * j + 2, U))):
                    for k in range(C):
                        last = mm(bA[:, i * D:(i + 1) * D], hT[:, k, u * P:(u + 1) * P], wqkv[:, k, 2 * D:3 * D],
                                  start=(k == 0), stop=(k == C - 1))
                last.then_inc(sems["vp"], 1)

            def fills(bt, g, ks):
                if not ks:
                    return
                if g == 0 and ks[0] == 0:
                    after(pe, "qk_ld", bt, 192)
                q, kk = Qs[bt.par], Ks[bt.par]
                for n in ks:
                    t, pr = divmod(n, 2)
                    after(pe, "smax", bt, 2 * (8 * g + n - 1))
                    for i in range(2):
                        h = HQ * g + 2 * pr + i
                        last = mm(bS[n % 2][:, i * 2 * P:(i + 1) * 2 * P], q[0:MROW, h, t * P:(t + 1) * P],
                                  kk[0:MROW, h, t * P:(t + 2) * P], start=True, stop=True)
                    last.then_inc(sems["Sp"], 1)

            def turn_m(bt, g):
                after(pe, "m2", bt, 2 * g + 2)
                after(pe, "on", bt, g - 1)
                nc.tensor.transpose(bT[:, 0:P // 2].bitcast(BF16), M2[:], identb[:]).then_inc(sems["mTp"], 1)

            def qrange(u):
                return max(u - 1, 0) * P, min(u + 1, T) * P

            def scoresT(bt, g, u, p):
                if u == 0 and p == 0:
                    after(pe, "mrow_ld", bt, 16 * (g + 1))
                q, kk = Qs[bt.par], Ks[bt.par]
                lo, hi = qrange(u)
                if True:
                    m = 10 * g + 2 * u + p
                    after(pe, "exp", bt, m - 1)
                    for i in range(2):
                        h = HQ * g + 2 * p + i
                        last = mm(bST[m % 2][:, i * (hi - lo):(i + 1) * (hi - lo)], kk[0:KROWS, h, u * P:(u + 1) * P],
                                  q[0:KROWS, h, lo:hi], start=True, stop=True)
                    last.then_inc(sems["STp"], 1)

            def values(bt, g, u, p):
                if g == 0 and u == 0 and p == 0:
                    after(pe, "v", bt, 3)
                if u == 0 and p == 0:
                    after(pe, "oTs", bt, g)
                lo, hi = qrange(u)
                rows = slice(BAND, P) if u == 0 else slice(0, BAND) if u == U - 1 else slice(0, P)
                if True:
                    m = 10 * g + 2 * u + p
                    after(pe, "cut", bt, 16 * g + 2 * SEL_BEFORE[u] + SEL_OF[u] * (p + 1), apart=True)
                    for i in range(2):
                        j = 2 * p + i
                        last = mm(bO[32 * j:32 * j + 32, lo:hi], Va[bt.par][rows, u, HQ * g + j, :],
                                  PT[m % NPT][rows, i, 0:hi - lo], start=(u == 0), stop=(u == U - 1),
                                  skip_group_check=True)
                    last.then_inc(sems["pv"], 1)

            def turn_o(bt, g):
                after(pe, "oTs", bt, g + 1)
                after(pe, "mT", *((bt, g + 2) if g < QUADS - 1 else (Batch(bt.b + 1, 0, 0), 1))) if True else None
                for t in range(T):
                    last = nc.tensor.transpose(bT[:, t * P:(t + 1) * P], OTs[:, t * P:(t + 1) * P], ident[:])
                last.then_inc(sems["oTp"], 1)

            def turn_o_last(bt):
                after(pe, "oTs", bt, QUADS)
                after(pe, "on", bt, QUADS - 1)
                for t in range(T):
                    last = nc.tensor.transpose(bT[:, t * P:(t + 1) * P], OTs[:, t * P:(t + 1) * P], ident[:])
                last.then_inc(sems["oTp"], 1)

            def c_onT(bt, k):
                after(pe, "on", bt, QUADS)
                if k == 0:
                    after(pe, "idx", bt, 2)
                else:
                    after(pe, "onT", bt, k)
                for t in range(T):
                    last = nc.tensor.transpose(bC[:, t * P:(t + 1) * P], on[:, t, k * P:(k + 1) * P], ident[:])
                last.then_inc(sems["onTp"], 1)

            def c_op(bt, n):
                after(pe, "onT", bt, C)
                after(pe, "t1", bt, n)
                for i in range(2):
                    t = 2 * n + i
                    for k in range(C):
                        last = mm(bC[:, i * D:(i + 1) * D], onT[:, k, t * P:(t + 1) * P], wo[:, k, :],
                                  start=(k == 0), stop=(k == C - 1))
                last.then_inc(sems["op"], 1)

            def c_h2T(bt, k):
                after(pe, "h2", bt, T)
                if k == 0:
                    after(pe, "t1", bt, 2)
                else:
                    after(pe, "h2T", bt, k)
                for t in range(T):
                    last = nc.tensor.transpose(bC[:, t * P:(t + 1) * P], H2[:, t, k * P:(k + 1) * P], ident[:])
                last.then_inc(sems["h2Tp"], 1)

            def c_lg(bt):
                after(pe, "h2T", bt, C)
                for t in range(T):
                    for k in range(C):
                        last = mm(bC[:, t * E:(t + 1) * E], h2T[:, k, t * P:(t + 1) * P], gwT[:, k, :],
                                  start=(k == 0), stop=(k == C - 1))
                last.then_inc(sems["lg"], 1)

            def c_cnt(bt):
                after(pe, "ex", bt, 1)
                after(pe, "pre", bt, T + 1)
                mm(bC[:, 0:T * E], before[:], selb[:], start=True, stop=False)
                mm(bC[:, 0:T * E], onesb[:], Spre[:, 0:T, :].rearrange("p t e -> p (t e)"), start=False, stop=True
                   ).then_inc(sems["cntp"], 1)

            def c_idx(bt, half):
                if half == 0:
                    after(pe, "pos", bt, 0)
                    after(pe, "oneh", bt, 0)
                else:
                    after(pe, "idx", bt, 1)
                for i in range(G // 2):
                    g = half * (G // 2) + i
                    for t in range(T):
                        last = mm(bC[:, i * P:(i + 1) * P], oneh[:, t, g].rearrange("p a e -> p (a e)"),
                                  oneh[:, T + t, g].rearrange("p b e -> p e b"), start=(t == 0), stop=(t == T - 1))
                last.then_inc(sems["idxp"], 1)

            def body(prev, now, nxt):
                for slot in range(SLOTS):
                    g, u = divmod(slot, U)
                    ahead = (now, g + 1) if g < QUADS - 1 else (nxt, 0)
                    ks = FILLS.get(u, []) if ahead[0] else []
                    last = (now, *divmod(slot - 1, U)) if slot else (prev, QUADS - 1, U - 1)
                    for p in range(2):
                        scoresT(now, g, u, p)
                        fills(*ahead, ks[p:p + 1])
                    for p in range(2):
                        if last[0]:
                            values(*last, p)
                        fills(*ahead, ks[2 + p:3 + p])
                    if u == 1 and (g > 0 or prev):
                        turn_o(*((now, g - 1) if g > 0 else (prev, QUADS - 1)))
                    if u == 3 and ahead[0]:
                        turn_m(*ahead)
                    if nxt:
                        if slot in (2, 3):
                            a_hT(nxt, slot - 2)
                        if slot in PROJ_SLOTS:
                            a_proj(nxt, PROJ_SLOTS.index(slot))
                        if 9 <= slot <= 11:
                            a_v(nxt, slot - 9)
                    if prev:
                        if slot in (3, 4):
                            c_onT(prev, slot - 3)
                        if slot in (5, 6):
                            c_op(prev, slot - 5)
                        if slot in (10, 11):
                            c_h2T(prev, slot - 10)
                        if slot == 12:
                            c_lg(prev)
                        if slot == 17:
                            c_cnt(prev)
                        if slot < 2:
                            c_idx(prev, slot)

            first = batch(0)
            pe.wait_ge(s_v0, 9)
            pe.wait_ge(s_par, 16 * 8)
            pe.wait_ge(s_ones, 32)
            pe.wait_ge(s_ix2, NSET)
            a_hT(first, 0)
            a_hT(first, 1)
            for j in range(4):
                a_proj(first, j)
            for j in range(3):
                a_v(first, j)
            fills(first, 0, list(range(8)))
            turn_m(first, 0)
            pe.wait_ge(s_cleared, 1)
            loops(pe, body)
            last = batch(B - 1)
            for p in range(2):
                values(last, QUADS - 1, U - 1, p)
            turn_o_last(last)
            c_idx(last, 0)
            c_idx(last, 1)
            for k in range(C):
                c_onT(last, k)
            for n in range(2):
                c_op(last, n)
            for k in range(C):
                c_h2T(last, k)
            c_lg(last)
            c_cnt(last)
            c_idx(batch(B), 0)
            c_idx(batch(B), 1)

            for k in range(2):
                pe.wait_ge(s_ix, 4 + k)
                for g in range(G):
                    last_t = mm(bC[:, k * P + g * 2 * EG:k * P + (g + 1) * 2 * EG],
                                spread[:, k, g].rearrange("p k b -> p (k b)"),
                                own_eh[:, :, :].rearrange("p e h -> p (e h)"), start=True, stop=True)
            last_t.then_inc(s_tabT, 1)

            def turn_x(it, n):
                par = n % 2
                pe.wait_ge(mo["x_ld"][n % 4], (it + n // 4) * 32 + 32)
                need(pe, mo["xTc"], it * 4 + (n - 1))
                need(pe, mo["xTd"], it * 4 + (n - 1))
                if isinstance(it, int) and it == 0 and n == 1:
                    pe.wait_ge(s_ix, 7)
                for k, bank in ((0, bS[par]), (1, bA if par == 0 else bC)):
                    for h in range(2):
                        last = nc.tensor.transpose(bank[:, h * P:(h + 1) * P], xg[n % 4][:, h, k * P:(k + 1) * P], ident[:])
                    last.then_inc(mo["xTp"], 1)

            def expert(it, n):
                par = n % 2
                need(pe, mo["xTc"], it * 4 + (n + 1))
                need(pe, mo["xTd"], it * 4 + (n + 1))
                need(pe, mo["w_ld"][n], it * 48 + 48)
                need(pe, mo["hm"], it * 4 + (n - 1))
                for a in range(2):
                    for k in range(C):
                        last = mm(bST[par][:, a * CAP:(a + 1) * CAP], wgu[n][:, a, k, :], xgT[par][:, k, :],
                                  start=(k == 0), stop=(k == C - 1))
                last.then_inc(mo["gp"], 1)

            def expert_out(it, n):
                par = n % 2
                need(pe, mo["hm"], it * 4 + (n + 1))
                need(pe, mo["yc"], it * 8 + (2 * n - 2))
                yb = bO if par == 0 else bT
                for h in range(2):
                    last = mm(yb[:, h * D:(h + 1) * D], hm[par][:, h * P:(h + 1) * P], wd[n % 4][:], start=True, stop=True)
                last.then_inc(mo["yp"], 1)

            def four(it, first=False, final=False):
                for n in range(4):
                    expert(it, n)
                    if not (final and n == 3):
                        turn_x(it, n + 1)
                    if not (first and n == 0):
                        expert_out(it, n - 1)

            turn_x(0, 0)
            four(0, first=True)
            with pe.Fori(1, E // 4 - 1) as it:
                four(it)
            four(E // 4 - 1, final=True)
            expert_out(E // 4 - 1, 3)

        @block.vector
        def _(dve):
            start_counts(dve, "DVE")
            v = nc.vector

            def a_stats(bt, half):
                ts = range(2 * half, 2 * half + 2)
                if half == 0:
                    dve.wait_ge(x_ld[bt.par], bt.half * 16 + 16)
                for t in ts:
                    v.bn_stats(stats[:, t, :], xt[:, t, :]).then_inc(sems["stats"], 1)
                after(dve, "rstd", bt, 0, apart=True)
                for t in ts:
                    after(dve, "stats", bt, t + 1, apart=True)
                    v.bn_aggr(mv[:, t, :], stats[:, t, :]).then_inc(sems["aggr"], 1)

            def a_mod(bt):
                after(dve, "hT", bt, 0)
                i = bt.b if isinstance(bt.b, int) else None
                src = modT[:, i, :] if i is not None else modT[:, bass.ds(bt.b, 1), :].rearrange("p o n -> p (o n)")
                v.tensor_copy(mcol[:], src).then_inc(sems["mcol"], 1)

            def a_v(bt, j):
                after(dve, "vp", bt, j + 1)
                if not isinstance(bt.b, int) or bt.b >= 2:
                    after(dve, "pv", Batch(bt.b - 1, 0, 0), 0)
                us = slice(2 * j, min(2 * j + 2, U))
                nu = us.stop - us.start
                v.tensor_tensor(Va[bt.par][:, us, :, 0:HD],
                                bA[:, 0:nu * D].rearrange("p (u h d) -> p u h d", u=nu, d=HD),
                                bv[:, :].rearrange("p (h d) -> p h d", d=HD).unsqueeze(1).to_broadcast([P, nu, H, HD]),
                                ALU.add).then_inc(sems["v"], 1)

            def maxima(bt, g, ks):
                for n in ks:
                    t, pr = divmod(n, 2)
                    after(dve, "Sp", bt, 8 * g + n + 1)
                    if n == 0:
                        after(dve, "m2", bt, 2 * g)
                    edge = 0 if t == 0 else 2 if t == T - 1 else 1
                    for i in range(2):
                        at = 2 * (8 * g + n) + i
                        after(dve, "smax", bt, at - 1, apart=True)
                        h = 2 * pr + i
                        ins = v.tensor_tensor_reduce(out=junk[:, i, :], in0=bS[n % 2][:, i * 2 * P:(i + 1) * 2 * P],
                                                     in1=mask[:, edge, :], scale=1.0, scalar=TAKEN, op0=ALU.add,
                                                     op1=ALU.max, accum_out=mrowmax[:, h, t:t + 1])
                        ins.then_inc(sems["smax"], 1)

            def split_m(bt, g):
                after(dve, "mTp", bt, g)
                after(dve, "smax", bt, 16 * (g + 1))
                flat = mrowmax[:, :, :].rearrange("p h t -> p (h t)")
                v.tensor_scalar(M2[:, 0:16], flat, -1.0, None, ALU.mult).then_inc(sems["m2"], 1)
                after(dve, "m2", bt, 2 * g + 1)
                v.scalar_tensor_tensor(M2[:, 16:32], flat, -1.0, M2[:, 0:16], ALU.mult, ALU.subtract
                                       ).then_inc(sems["m2"], 1)

            def norm_o(bt, g):
                after(dve, "oTp", bt, g + 1)
                if g == 0:
                    after(dve, "onTp", bt, 0)
                after(dve, "on", bt, g)
                src = bT[:, :].rearrange("p (t h d) -> p t h d", t=T, d=32)
                v.reciprocal(rec[:], src[:, :, :, HD]).then_inc(sems["rec"], 1)
                after(dve, "rec", bt, g + 1)
                v.tensor_tensor(on[:, :, g * 64:(g + 1) * 64].rearrange("p t (h d) -> p t h d", d=HD), src[:, :, :, 0:HD],
                                rec[:, :, :].unsqueeze(3).to_broadcast([P, T, HQ, HD]), ALU.mult).then_inc(sems["on"], 1)

            def c_x1(bt, n):
                after(dve, "op", bt, n + 1)
                after(dve, "x1_st", bt, 0)
                after(dve, "stats2", bt, 0)
                after(dve, "xb", bt, 2)
                dst = x1[:, 2 * n:2 * n + 2, :]
                v.tensor_tensor(dst, bC[:, :].rearrange("p (t d) -> p t d", t=2),
                                mr[:, 0, :].unsqueeze(1).to_broadcast([P, 2, D]), ALU.mult).then_inc(sems["t1"], 1)
                after(dve, "t1", bt, n + 1)
                v.tensor_tensor(dst, dst, xc[:, 2 * n:2 * n + 2, :], ALU.add).then_inc(sems["x1"], 1)

            def c_stats(bt, half):
                ts = range(2 * half, 2 * half + 2)
                after(dve, "x1", bt, half + 1)
                for t in ts:
                    v.bn_stats(stats2[:, t, :], x1[:, t, :]).then_inc(sems["stats2"], 1)
                after(dve, "rstd2", bt, 0, apart=True)
                for t in ts:
                    after(dve, "stats2", bt, t + 1, apart=True)
                    v.bn_aggr(mv2[:, t, :], stats2[:, t, :]).then_inc(sems["aggr2"], 1)

            def c_norm(bt, k):
                if k == 0:
                    after(dve, "h_st", bt, 0)
                    after(dve, "h2Tp", bt, 0)
                    after(dve, "aggr2", bt, T)
                    for t in range(T):
                        v.scalar_tensor_tensor(xn2[:, t, :], x1[:, t, :], mv2[:, t, 0:1], mr[:, 2, :], ALU.subtract,
                                               ALU.mult).then_inc(sems["xn2"], 1)
                else:
                    after(dve, "rstd2", bt, 2)
                    for t in range(T):
                        after(dve, "xn2", bt, t + 1)
                        v.scalar_tensor_tensor(xn2[:, t, :], xn2[:, t, :], rs2[:, t:t + 1], mr[:, 1, :], ALU.mult,
                                               ALU.add).then_inc(sems["h2"], 1)

            def c_route(bt, part):
                done = [ROUTE_PARTS[part]]

                def step(op, *args, **kw):
                    after(dve, "route", bt, done[0], apart=op in (v.max, v.match_replace))
                    op(*args, **kw).then_inc(sems["route"], 1)
                    done[0] += 1

                hi4, lo4, hi2, q2, r2, lo2 = (pairs[:, i] for i in range(6))
                g4 = gs[:, 3, :].rearrange("p (t g) -> p t g", t=T)
                other = g4.unsqueeze(2).to_broadcast([P, T, G, G])
                own = g4.unsqueeze(3).to_broadcast([P, T, G, G])
                wide = lambda n: gs[:, n, :].unsqueeze(2).to_broadcast([P, T * G, EG])
                per_t = lambda ap: ap.rearrange("p (t e) -> p t e", t=T)

                def pick(t):
                    tt = tmp[:, t * G:(t + 1) * G, :].rearrange("p g e -> p (g e)")
                    rr = rep[:, t * G:(t + 1) * G, :].rearrange("p g e -> p (g e)")
                    step(v.max, top8[:, t, :], tt)
                    step(v.match_replace, rr, top8[:, t, :], tt, TAKEN)

                if part == 0:
                    after(dve, "ex", bt, 1)
                    step(v.tensor_scalar, ex[:], ex[:], 1.0, None, ALU.add)
                    step(v.reciprocal, sc[:], ex[:])
                    step(v.tensor_tensor, sfc[:, :, :].rearrange("p (t g) e -> p t (g e)", t=T), per_t(sc[:, :]),
                         gb[:, :].unsqueeze(1).to_broadcast([P, T, E]), ALU.add)
                elif part == 1:
                    step(v.tensor_tensor, hi4, sfc[:, :, 0:4], sfc[:, :, 4:8], ALU.max)
                    step(v.tensor_tensor, lo4, sfc[:, :, 0:4], sfc[:, :, 4:8], ALU.min)
                    step(v.tensor_tensor, hi2[:, :, 0:2], hi4[:, :, 0:2], hi4[:, :, 2:4], ALU.max)
                    step(v.tensor_tensor, q2[:, :, 0:2], hi4[:, :, 0:2], hi4[:, :, 2:4], ALU.min)
                elif part == 2:
                    step(v.tensor_tensor, r2[:, :, 0:2], lo4[:, :, 0:2], lo4[:, :, 2:4], ALU.max)
                    step(v.tensor_tensor, lo2[:, :, 0:2], q2[:, :, 0:2], r2[:, :, 0:2], ALU.max)
                    step(v.tensor_tensor, gs[:, 0, :], hi2[:, :, 0], hi2[:, :, 1], ALU.max)
                    step(v.tensor_tensor, gs[:, 1, :], hi2[:, :, 0], hi2[:, :, 1], ALU.min)
                elif part == 3:
                    step(v.tensor_tensor, gs[:, 2, :], lo2[:, :, 0], lo2[:, :, 1], ALU.max)
                    step(v.tensor_tensor, gs[:, 1, :], gs[:, 1, :], gs[:, 2, :], ALU.max)
                    step(v.tensor_tensor, gs[:, 3, :], gs[:, 0, :], gs[:, 1, :], ALU.add)
                elif part == 4:
                    step(v.tensor_tensor, cmp1[:], other, own, ALU.is_gt)
                    step(v.tensor_tensor, cmp2[:], other, own, ALU.is_equal)
                    step(v.tensor_tensor, cmp2[:], cmp2[:], lowerg[:, :, :].unsqueeze(1).to_broadcast([P, T, G, G]),
                         ALU.mult)
                elif part == 5:
                    step(v.tensor_tensor, cmp1[:], cmp1[:], cmp2[:], ALU.add)
                    step(v.tensor_reduce, gs[:, 0, :], cmp1[:, :, :, :].rearrange("p t g h -> p (t g) h"), AX_X, ALU.add)
                    step(v.tensor_scalar, gs[:, 1, :], gs[:, 0, :], TG - 0.5, None, ALU.is_lt)
                elif part == 6:
                    step(v.tensor_scalar, gs[:, 2, :], gs[:, 1, :], 1.0, -NEG, ALU.subtract, ALU.mult)
                    step(v.tensor_tensor, tmp[:], sfc[:], wide(1), ALU.mult)
                    step(v.tensor_tensor, tmp[:], tmp[:], wide(2), ALU.add)
                elif part == 7:
                    pick(0)
                    pick(1)
                elif part == 8:
                    pick(2)
                    pick(3)
                elif part == 9:
                    after(dve, "cntp", bt, 0)
                    step(v.tensor_scalar, selb[:], rep[:, :, :].rearrange("p g e -> p (g e)"), TAKEN / 1.5, None, ALU.is_lt)
                    v.tensor_copy(Spre[:, 0, :], Spre[:, T, :]).then_inc(sems["pre"], 1)
                    after(dve, "route", bt, done[0])
                    for t in range(T):
                        after(dve, "pre", bt, t + 1)
                        v.tensor_tensor(Spre[:, t + 1, :], Spre[:, t, :], selb[:, t * E:(t + 1) * E], ALU.add
                                        ).then_inc(sems["pre"], 1)
                elif part == 10:
                    step(v.tensor_tensor, sc[:], sc[:], selb[:], ALU.mult)
                    step(v.tensor_reduce, wsum[:, 0, :], per_t(sc[:, :]), AX_X, ALU.add)
                    step(v.tensor_scalar, wsum[:, 1, :], wsum[:, 0, :], 1e-20, None, ALU.add)
                    step(v.reciprocal, wsum[:, 2, :], wsum[:, 1, :])
                else:
                    step(v.tensor_tensor, per_t(sc[:, :]), per_t(sc[:, :]),
                         wsum[:, 2, :].unsqueeze(2).to_broadcast([P, T, E]), ALU.mult)
                    after(dve, "h_st", bt, 0)
                    step(v.tensor_scalar, H2[:, :, D:HW], per_t(sc[:, :]), ROUTE_SCALE, None, ALU.mult)
                assert done[0] == ROUTE_PARTS[part + 1], (part, done[0])

            def c_pos(bt):
                after(dve, "cntp", bt, 1)
                v.scalar_tensor_tensor(posf[:], selb[:], -FAR, bC[:, 0:T * E], ALU.mult, ALU.add).then_inc(sems["pos"], 1)
                after(dve, "pos", bt, 1)
                v.tensor_scalar(posi[:, 0, :], posf[:], FAR, None, ALU.add).then_inc(sems["pos"], 1)
                after(dve, "pos", bt, 2)
                v.tensor_scalar(posi[:, 1, :], posi[:, 0, :], 4, None, ALU.logical_shift_right).then_inc(sems["pos"], 1)
                v.tensor_scalar(posi[:, 2, :], posi[:, 0, :], LO - 1, None, ALU.bitwise_and).then_inc(sems["pos"], 1)
                i = bt.b * T
                src = valt[:, bass.ds(i, T)] if not isinstance(i, int) else valt[:, i:i + T]
                v.tensor_copy(vt[:], src).then_inc(sems["vt"], 1)

            def c_onehot(bt, t):
                after(dve, "pos", bt, 4)
                after(dve, "vt", bt, 1)
                after(dve, "idxp", bt, 2)
                es = slice(t * E, (t + 1) * E)
                digit_of = lambda k: posi[:, k, es].rearrange("p (g e) -> p g e", e=EG).unsqueeze(2).to_broadcast([P, G, LO, EG])
                every = digits[:, :, :].unsqueeze(1).to_broadcast([P, G, LO, EG])
                low = oneh[:, 2 * T]
                after(dve, "oneh", bt, 3 * t)
                v.tensor_tensor(oneh[:, t], digit_of(1), every, ALU.is_equal
                                ).then_inc(sems["oneh"], 1)
                v.tensor_tensor(low, digit_of(2), every, ALU.is_equal
                                ).then_inc(sems["oneh"], 1)
                after(dve, "oneh", bt, 3 * t + 2)
                v.tensor_scalar(oneh[:, T + t], low, vt[:, t:t + 1], None, ALU.mult).then_inc(sems["oneh"], 1)

            def c_idx(bt, half):
                after(dve, "idxp", bt, half + 1)
                dst = iacc[:, half * 4:half * 4 + 4].rearrange("p g e b -> p (g e b)")
                v.tensor_tensor(dst, dst, bC[:, :], ALU.add).then_inc(sems["idx"], 1)

            def body(prev, now, nxt):
                for slot in range(SLOTS):
                    g, u = divmod(slot, U)
                    ahead = (now, g + 1) if g < QUADS - 1 else (nxt, 0)
                    ks = FILLS.get(u, []) if ahead[0] else []
                    parts = ROUTE_SLOTS.get(slot, []) if prev else []
                    for k in range(4):
                        maxima(*ahead, ks[k:k + 1])
                        for part in parts[k:k + 1]:
                            c_route(prev, part)
                    if u == 2 and ahead[0]:
                        split_m(*ahead)
                    if u == 2 and (g > 0 or prev):
                        norm_o(*((now, g - 1) if g > 0 else (prev, QUADS - 1)))
                    if nxt:
                        if slot in (0, 1):
                            a_stats(nxt, slot)
                        if slot == 2:
                            a_mod(nxt)
                        if 9 <= slot <= 11:
                            a_v(nxt, slot - 9)
                    if prev:
                        if slot in (5, 6):
                            c_x1(prev, slot - 5)
                        if slot in (6, 7):
                            c_stats(prev, slot - 6)
                        if slot in (8, 9):
                            c_norm(prev, slot - 8)
                        if slot == 18:
                            c_pos(prev)
                        if slot in (18, 19):
                            c_onehot(prev, 2 * (slot - 18))
                            c_onehot(prev, 2 * (slot - 18) + 1)
                        if slot < 2:
                            c_idx(prev, slot)

            nset = [0]

            def setup(ins):
                ins.then_inc(s_ix2, 1)
                nset[0] += 1

            a_stats(batch(0), 0)
            a_stats(batch(0), 1)
            for i in range(2):
                setup(v.memset(Ks[i][0:MROW, :, 0:BAND], 0.0))
                setup(v.memset(Ks[i][0:MROW, :, BAND + S:KW], 0.0))
                setup(v.memset(Va[i][:, :, :, HD:HD + 1], 1.0))
                setup(v.memset(Va[i][:, :, :, HD + 1:], 0.0))
            setup(v.memset(hT[:, :, 0:BAND], 0.0))
            setup(v.memset(hT[:, :, BAND + S:KW], 0.0))
            setup(v.memset(M2[:], 0.0))
            setup(v.memset(Spre[:, T, :], 0.0))
            setup(v.memset(iacc[:], 0.0))
            dve.wait_ge(s_const, NCONST)
            setup(v.tensor_scalar(bits_e, bits_e, EG - 1, None, ALU.bitwise_and))
            setup(v.tensor_scalar(bits_k, bits_k, P // 2 - EG, None, ALU.bitwise_and))
            setup(v.tensor_scalar(bits_eh, bits_eh, P // 2 + EG - 1, None, ALU.bitwise_and))
            setup(v.tensor_scalar(high, high, CAP - LO, None, ALU.bitwise_and))
            dve.wait_ge(s_ix2, nset[0])
            setup(v.tensor_scalar(own_e[:], bits_e, 0.0, None, ALU.is_equal))
            setup(v.tensor_scalar(own_k[:], bits_k, 0.0, None, ALU.is_equal))
            setup(v.tensor_scalar(own_eh[:], bits_eh, 0.0, None, ALU.is_equal))
            setup(v.tensor_tensor(empty[:], empty[:], high, ALU.add))
            assert nset[0] == NSET
            dve.wait_ge(s_par, 16 * 8)
            dve.wait_ge(s_a0, 1)
            v.tensor_scalar(sil[:, 1, :], sil[:, 0, :], 1.0, None, ALU.add).then_inc(s_v0, 1)
            dve.wait_ge(s_v0, 1)
            v.reciprocal(sil[:, 0, :], sil[:, 1, :]).then_inc(s_v0, 1)
            dve.wait_ge(s_v0, 2)
            dve.wait_ge(s_ix2, nset[0])
            v.tensor_tensor(sil[:, 2, :], cin, sil[:, 0, :], ALU.mult).then_inc(s_v0, 1)
            dve.wait_ge(s_pe0, 4)
            v.tensor_copy(silT[:], bA[:, 0:C * B].rearrange("p (c b) -> p c b", c=C)).then_inc(s_v0, 1)
            v.tensor_copy(gwT[:], bC[:, 0:C * E].rearrange("p (c e) -> p c e", c=C)).then_inc(s_v0, 1)
            dve.wait_ge(s_pe0, 7)
            cols = bT[:, 0:4 * B].rearrange("p (n b) -> p b n", n=4)
            v.tensor_copy(modT[:, :, 0:2], cols[:, :, 0:2]).then_inc(s_v0, 1)
            v.tensor_scalar(modT[:, :, 2:4], cols[:, :, 2:4], 1.0, None, ALU.add).then_inc(s_v0, 1)
            v.tensor_copy(gates[:, 1, 0, :], bS[1][0:B, 0:D]).then_inc(s_v1, 1)
            v.tensor_scalar(gates[:, 1, 1, :], bS[1][0:B, D:2 * D], 1.0, None, ALU.add).then_inc(s_v1, 1)
            gg = gates[:, 0].rearrange("b k d -> b (k d)")
            sgn = sil[:, 0:2, :].rearrange("b k d -> b (k d)")
            v.tensor_copy(gg, bS[0][0:B, :]).then_inc(s_v1, 1)
            dve.wait_ge(s_v1, 3)
            v.tensor_scalar(sgn, gg, 0.0, 2.0, ALU.is_ge, ALU.mult).then_inc(s_v1, 1)
            dve.wait_ge(s_v1, 4)
            v.scalar_tensor_tensor(gg, gg, -1.0, gg, ALU.mult, ALU.max).then_inc(s_v1, 1)
            v.tensor_scalar(sgn, sgn, 1.0, None, ALU.subtract).then_inc(s_v1, 1)
            dve.wait_ge(s_v1, 6)
            v.tensor_scalar(gg, gg, 0.25, None, ALU.max).then_inc(s_v1, 1)
            dve.wait_ge(s_v1, 7)
            v.tensor_tensor(gg, gg, sgn, ALU.mult).then_inc(s_v0, 1)
            v.tensor_scalar(bqk[:, 0:2], bqk[:, 0:2], SCALE, None, ALU.mult).then_inc(s_v0, 1)
            dve.wait_ge(s_v0, 9)
            a_mod(batch(0))
            for j in range(3):
                a_v(batch(0), j)
            maxima(batch(0), 0, list(range(8)))
            split_m(batch(0), 0)
            loops(dve, body)
            last = batch(B - 1)
            norm_o(last, QUADS - 1)
            c_idx(last, 0)
            c_idx(last, 1)
            c_x1(last, 0)
            c_x1(last, 1)
            c_stats(last, 0)
            c_stats(last, 1)
            c_norm(last, 0)
            c_norm(last, 1)
            for k in range(12):
                c_route(last, k)
            c_pos(last)
            for t in range(T):
                c_onehot(last, t)
            c_idx(batch(B), 0)
            c_idx(batch(B), 1)

            k = [0]

            def step(ins):
                ins.then_inc(s_ix, 1)
                k[0] += 1
                dve.wait_ge(s_ix, k[0])

            after(dve, "idx", batch(B), 2)
            dve.wait_ge(s_zero, 16 * 4 * B)
            dm = own_e[:, :, :].rearrange("p e b -> p (e b)").unsqueeze(1).to_broadcast([P, G, P])
            flat = iacc[:, :, :, :].rearrange("p g e b -> p g (e b)")
            v.tensor_tensor(flat, flat, dm, ALU.mult).then_inc(s_i2, 1)
            dve.wait_ge(s_i2, 1)
            v.tensor_reduce(iv[:, 0], iacc[:, :, :, :].rearrange("p g e b -> p g b e"), AX_X, ALU.add).then_inc(s_i2, 1)
            dve.wait_ge(s_i2, 2)
            v.tensor_scalar(iv[:, 1], iv[:, 0], 0.0, None, ALU.is_lt).then_inc(s_i2, 1)
            dve.wait_ge(s_i2, 3)
            v.tensor_scalar(iv[:, 2], iv[:, 1], -2.0, 1.0, ALU.mult, ALU.add).then_inc(s_i2, 1)
            v.tensor_scalar(iv[:, 1], iv[:, 1], N / 2.0, -1.0, ALU.mult, ALU.add).then_inc(s_i2, 1)
            dve.wait_ge(s_i2, 5)
            v.tensor_tensor(iv[:, 2], iv[:, 2], iv[:, 0], ALU.mult).then_inc(s_i2, 1)
            dve.wait_ge(s_i2, 6)
            v.tensor_tensor(iv[:, 2], iv[:, 2], iv[:, 1], ALU.add).then_inc(s_i2, 1)
            dve.wait_ge(s_i2, 7)
            step(v.tensor_scalar(iv[:, 4], iv[:, 2], 0.0, None, ALU.max))
            v.tensor_scalar(iv[:, 1], iv[:, 2], 0.0, None, ALU.is_lt).then_inc(s_i2, 1)
            dve.wait_ge(s_i2, 8)
            step(v.tensor_tensor(iv[:, 3], empty[:], iv[:, 1], ALU.mult))
            step(v.tensor_tensor(iv[:, 5], iv[:, 3], iv[:, 2], ALU.add))
            for i in range(2):
                step(v.tensor_tensor(spread[:, i], iv[:, 4 + i].unsqueeze(2).to_broadcast([P, G, P // LO, LO]),
                                     own_k[:, :, :].unsqueeze(1).to_broadcast([P, G, P // LO, LO]), ALU.mult))
            dve.wait_ge(s_tabT, 1)
            step(v.tensor_copy(gidx[:], bC[:, 0:P]))
            step(v.tensor_copy(sidx[:], bC[:, P:2 * P]))

            def stage(dst, table, it, n):
                at = it * 8 + 2 * n
                src = table[:, bass.ds(at, 2)] if not isinstance(at, int) else table[:, at:at + 2]
                return v.tensor_copy(dst[:, n % 4, :], src)

            def take_x(it, n):
                need(dve, mo["xTp"], it * 8 + (2 * n + 2))
                need(dve, mo["gp"], it * 4 + (n - 1))
                bank = bA if n % 2 == 0 else bC
                v.tensor_copy(xgT[n % 2][:, 1, :], bank[:, 0:CAP]).then_inc(mo["xTd"], 1)
                need(dve, mo["y_st"][n % 4], (it + n // 4) * 32)
                stage(sstage, sidx, it, n).then_inc(mo["sst"], 1)
                need(dve, mo["yc"], it * 8 + (2 * n - 6))
                need(dve, mo["x_ld"][n % 4], (it + n // 4) * 32 + 32)
                at = it * 4 + (D + n)
                col = bass.ds(at, 1) if not isinstance(at, int) else slice(at, at + 1)
                v.tensor_copy(wcol[n % 4][:, :].unsqueeze(2), xg[n % 4][:, :, col]).then_inc(mo["wc"], 1)

            def hidden(it, n):
                need(dve, mo["sg"], it * 4 + (n + 1))
                need(dve, mo["yp"], it * 4 + (n - 1))
                v.tensor_tensor(hm[n % 2][:], bST[n % 2][:, CAP:2 * CAP], sg[n % 2][:], ALU.mult).then_inc(mo["hm"], 1)

            for n in range(4):
                stage(gstage, gidx, 0, n).then_inc(mo["gst"], 1)
            def four(it, final=False):
                for n in range(4):
                    if not (final and n == 3):
                        take_x(it, n + 1)
                    if not final:
                        stage(gstage, gidx, it, n + 4).then_inc(mo["gst"], 1)
                    hidden(it, n)

            take_x(0, 0)
            four(0)
            with dve.Fori(1, E // 4 - 1) as it:
                four(it)
            four(E // 4 - 1, final=True)

            dve.wait_ge(s_fx, 32)
            for b in range(B):
                a = fa[b % NF]
                dve.wait_ge(mo["f_ld"][b % NF], 32 * (b // NF + 1))
                v.tensor_tensor(a[:, 0], a[:, 0], a[:, 1], ALU.add).then_inc(mo["fsum"], 1)
                dve.wait_ge(mo["fsum"], 2 * b + 1)
                v.tensor_tensor(a[:, 0], a[:, 0], fg[:, b, :].unsqueeze(1).to_broadcast([P, T, D]), ALU.mult
                                ).then_inc(mo["fsum"], 1)


_INS = ["L0_attn_x", "L0_attn_w_qkv", "L0_attn_b_qkv", "L0_attn_w_out", "L0_attn_b_out", "L0_ffn_gate_w",
        "L0_ffn_gate_bias", "L0_ffn_w_gate", "L0_ffn_w_up", "L0_ffn_w_down", "L0_c", "L0_wmod"]


def kernel(**inputs):
    import numpy as np
    import concourse.bacc as bacc
    from concourse.bass_utils import run_bass_kernel_spmd

    nc = bacc.Bacc("TRN2", target_bir_lowering=False, num_devices=1)
    arrays, args = {}, []
    for name in _INS:
        a = np.ascontiguousarray(inputs[name])
        arrays[name + "_dram"] = a
        args.append(nc.dram_tensor(name + "_dram", a.shape, mybir.dt.from_np(a.dtype), kind="ExternalInput").ap())
    out = nc.dram_tensor("out_dram", (B, S, D), F32, kind="ExternalOutput").ap()
    build(nc, *args, out)
    r = run_bass_kernel_spmd(nc, [arrays], core_ids=[0])
    return r.results[0]["out_dram"]
```

```python
from contextlib import ExitStack

import concourse.bass as bass
from concourse import mybir

F32 = mybir.dt.float32
BF16 = mybir.dt.bfloat16
F16 = mybir.dt.float16
I32 = mybir.dt.int32
I16 = mybir.dt.int16
U32 = mybir.dt.uint32
ALU = mybir.AluOpType
ACT = mybir.ActivationFunctionType
AX_X = mybir.AxisListType.X

P = 128
B, S, D = 8, 512, 256
H, HD, BAND = 16, 16, 64
E, K, G, TG = 64, 8, 8, 4
CAP, I = 256, 128
N = B * S
T = S // P
C = D // P
U = T + 1
KW = S + 2 * BAND
QUADS, HQ = H // 4, 4
SLOTS = QUADS * U
EG = E // G
SCALE = float(HD) ** -0.5
EPS = 1e-5
ROUTE_SCALE = 2.5
HW = D + E
LO, HI = 16, CAP // 16
FAR = 16.0 * 256
NEG = -1e30
TAKEN = -3e38
PAIRS = [(0, 0), (0, 1), (1, 0), (1, 1), (0, 2), (2, 0)]
MROW = len(PAIRS) * HD
KROWS = MROW + 2
NPT = 4
SEL_BEFORE = [0, 1, 3, 5, 7]
SEL_OF = [1, 2, 2, 2, 1]

PER = dict(
    xn=T, mcol=1, stats=T, aggr=T, rstd=4, hTp=C, hT=C, proj=4, p32=4, hpart=4, r32=4, mpart=4,
    lpart=4, vp=3, v=3, Sp=8 * QUADS, smax=2 * 8 * QUADS, m2=2 * QUADS, mTp=QUADS, mT=QUADS, STp=10 * QUADS,
    exp=10 * QUADS, cut=16 * QUADS, pv=10 * QUADS, oTs=QUADS, oTp=QUADS, rec=QUADS, on=QUADS,
    onTp=C, onT=C, op=2, t1=2, xb=2, x1=2, stats2=T, aggr2=T, rstd2=2, xn2=T, h2=T, h2Tp=C, h2T=C,
    lg=1, ex=1, route=38, pre=T + 1, vt=1, cntp=1, pos=4, oneh=3 * T, idxp=2, idx=2,
    qk_ld=192, mrow_ld=64, c_ld=32, x1_st=16, h_st=16,
)

FROM_ONE = dict(
    SP=["h_st", "x1_st"], Pool=["xb", "rstd2"], Act=["t1", "ex"], PE=["op", "h2Tp", "lg", "cntp", "idxp"],
    DVE=["x1", "stats2", "xn2", "h2", "route", "pre", "vt", "pos", "oneh", "idx"],
)
STARTS = {name: 1 for names in FROM_ONE.values() for name in names}


ROUTE_PARTS = [0, 3, 7, 11, 14, 17, 20, 23, 27, 31, 32, 36, 38]


class Batch:

    def __init__(self, b, half, par):
        self.b, self.half, self.par = b, half, par


def batch(b):
    return Batch(b, b // 2, b % 2)


def build(nc, x, w_qkv, b_qkv, w_out, b_out, gate_w, gate_bias, w_gate, w_up, w_down, c, wmod, out):
    with ExitStack() as ctx:
        sems = {name: ctx.enter_context(nc.semaphore("s_" + name)) for name in PER}

        def sem(name):
            return ctx.enter_context(nc.semaphore(name))

        def ps(name, n=512):
            return ctx.enter_context(nc.psum_tensor(name, [P, n], F32))

        def dram(name, shape, dt=F32):
            return nc.dram_tensor(name, shape, dt, kind="Internal").ap()

        def hold(eng, s, v):
            if not isinstance(v, int):
                eng.compute_val(v)
                eng.wait_ge(s_const, NCONST)
            eng.wait_ge(s, v)

        def need(eng, s, v):
            if not isinstance(v, int) or v > 0:
                eng.wait_ge(s, v)

        def after(eng, name, bt, k, apart=False):
            v = bt.b * PER[name] + k
            if isinstance(v, int) and v <= 0:
                return
            v = v + STARTS.get(name, 0)
            assert isinstance(v, int) or v.min_val > 0, name
            if apart or eng is nc.sync or eng is nc.gpsimd:
                hold(eng, sems[name], v)
            else:
                eng.wait_ge(sems[name], v)

        def start_counts(eng, which):
            for name in FROM_ONE[which]:
                eng.sem_inc(sems[name], 1)

        def parts_stored(eng, bt, j, k):
            v = bt.b * 32 + 16 * k
            if isinstance(v, int) and v <= 0:
                return
            hold(eng, parts_st[j % 2], v)

        s_par = sem("params_loaded")
        s_cin = sem("c_loaded")
        s_wm1 = sem("wmod_of_first_norm_loaded")
        s_wm2 = sem("rest_of_wmod_loaded")
        s_wq = sem("projection_weights_loaded")
        s_const = sem("constants_made")
        s_pe0 = sem("start_products")
        s_v0 = sem("start_vector_steps")
        s_a0 = sem("start_scalar_steps")
        s_late = sem("one_hots_of_last_but_one_used")
        s_ones = sem("rows_of_ones_loaded")
        s_mod_st = sem("mod_rows_stored")
        s_zero = sem("accumulators_zeroed")
        parts_st = [sem("parts_stored_even"), sem("parts_stored_odd")]
        x_ld = [sem("x_loaded_even"), sem("x_loaded_odd")]
        s_ix = sem("index_steps")
        s_i2 = sem("index_sums")
        s_ix2 = sem("operand_constants")
        s_v1 = sem("gate_steps")
        s_tabT = sem("tables_turned")
        s_fx = sem("residual_loaded")

        def sbt(stack, name, shape, dt=F32):
            return stack.enter_context(nc.sbuf_tensor(name, shape, dt))

        ident = sbt(ctx, "ident", [P, P])
        iacc = sbt(ctx, "iacc", [P, G, EG, LO])
        own_e = sbt(ctx, "own_e", [P, EG, LO])
        own_k = sbt(ctx, "own_k", [P, P // LO, LO])
        own_eh = sbt(ctx, "own_eh", [P, EG, 2], F16)
        empty = sbt(ctx, "empty", [P, E, 2])
        ACCROWS = N + CAP
        ZCOLS = ACCROWS * D // B // P // 2

        bS = [ps("scores0"), ps("scores1")]
        bST = [ps("scoresT0"), ps("scoresT1")]
        bO = ps("outT")
        bT = ps("turns")
        bA = ps("stageA")
        bC = ps("stageC")

        parts_d = [dram(f"parts_d{i}", [2, 3, D, S], BF16) for i in range(2)]
        mod_d = dram("mod_d", [B, 4, D])
        x1_d = dram("x1_d", [B, S, D])
        htab = dram("htab", [N, HW])
        acc_d = [dram(f"acc_d{i}", [ACCROWS, D]) for i in range(2)]

        att = ExitStack()
        sb = lambda name, shape, dt=F32: sbt(att, name, shape, dt)
        zero = sb("zero", [P, ZCOLS])
        identb = sb("identb", [P, P], BF16)
        onesb = sb("onesb", [P, P], BF16)
        before = sb("before", [P, P], BF16)
        mask = sb("mask", [P, 3, 2 * P], BF16)
        digits = sb("digits", [P, LO, EG], I16)
        lowerg = sb("lowerg", [P, G, G])
        valt = sb("valt", [P, N // P])
        half_c = sb("half_c", [P, T])
        wqkv = sb("wqkv", [P, C, 3 * D])
        wo = sb("wo", [P, C, D])
        bqk = sb("bqk", [P, 4])
        bv = sb("bv", [P, D])
        bo = sb("bo", [P, D])
        gwT = sb("gwT", [P, C, E])
        gb = sb("gbias", [P, E])
        silT = sb("silT", [P, C, B])
        modT = sb("modT", [P, B, 4])
        xt = sb("xt", [P, T, D])
        xn = sb("xn", [P, T, D])
        stats = sb("stats", [P, T, 6])
        mv = sb("mv", [P, T, 2])
        ve = sb("ve", [P, T])
        rs = sb("rs", [P, T])
        nmean = sb("nmean", [P, T])
        mcol = sb("mcol", [P, 4])
        hT = sb("hT", [P, C, KW])
        p32 = [sb(f"p32_{i}", [P, S]) for i in range(2)]
        r32 = sb("r32", [P, S])
        parts = sb("parts", [P, 2, 3, S], BF16)
        Qs = [sb(f"Qs{i}", [P, H, S], BF16) for i in range(2)]
        Ks = [sb(f"Ks{i}", [P, H, KW], BF16) for i in range(2)]
        Va = [sb(f"Va{i}", [P, U, H, 32]) for i in range(2)]
        junk = sb("junk", [P, 2, 2 * P], BF16)
        mrowmax = sb("mrowmax", [P, HQ, T])
        M2 = sb("M2", [P, P], BF16)
        MT = sb("MT", [32, P], BF16)
        PT = [sb(f"PT{i}", [P, 2, 2 * P]) for i in range(NPT)]
        OTs = sb("OTs", [P, S])
        rec = sb("rec", [P, T, HQ])
        on = sb("on", [P, T, D])
        onT = sb("onT", [P, C, S])
        xc = sb("xc", [P, T, D])
        mr = sb("mr", [P, 3, D])
        gbo = sb("gbo", [P, D])
        x1 = sb("x1", [P, T, D])
        stats2 = sb("stats2", [P, T, 6])
        mv2 = sb("mv2", [P, T, 2])
        ve2 = sb("ve2", [P, T])
        rs2 = sb("rs2", [P, T])
        H2 = sb("H2", [P, T, HW])
        xn2 = H2[:, :, 0:D]
        h2T = onT
        ex = sb("ex", [P, T * E])
        sc = sb("sc", [P, T * E])
        sfc = sb("sfc", [P, T * G, EG])
        tmp = sb("tmp", [P, T * G, EG])
        rep = sb("rep", [P, T * G, EG])
        pairs = sb("pairs", [P, 6, T * G, 4])
        gs = sb("gs", [P, 4, T * G])
        cmp1 = sb("cmp1", [P, T, G, G])
        cmp2 = sb("cmp2", [P, T, G, G])
        top8 = sb("top8", [P, T, 8])
        selb = sb("selb", [P, T * E], BF16)
        wsum = sb("wsum", [P, 3, T])
        Spre = sb("Spre", [P, T + 1, E], BF16)
        posf = ex
        posi = sb("posi", [P, 3, T * E], I16)
        vt = sb("vt", [P, T])
        oneh = sb("oneh", [P, T + T + 1, G, LO, EG], F16)
        wm = oneh[:, 0:6].rearrange("p t g b e -> p (t g b e)").bitcast(F32).rearrange("p (c n) -> p c n", c=C)
        bits_e = tmp[:, 0:16, :].rearrange("p g e -> p (g e)").bitcast(I32).rearrange("p (e b) -> p e b", b=LO)
        bits_k = rep[:, 0:16, :].rearrange("p g e -> p (g e)").bitcast(I32).rearrange("p (k b) -> p k b", b=LO)
        bits_eh = tmp[:, 16:18, :].rearrange("p g e -> p (g e)").bitcast(I32).rearrange("p (e h) -> p e h", h=2)
        gw = on[0:E, 0, :]
        cin = xc[0:B, 0, :]
        sil = x1[0:B, 0:3, :]
        gates = onT[0:B, :, :].rearrange("b i (k d) -> b i k d", k=2)
        att.close()

        moe = ExitStack()
        sb = lambda name, shape, dt=F32: sbt(moe, name, shape, dt)
        NW, NX, NY = 4, 4, 4
        coded = sb("coded", [P, G, LO])
        iv = sb("iv", [P, 4, 2 * E])
        spread = sb("spread", [P, G, P // LO, LO], F16)
        gidx = sb("gidx", [P, 2 * E], U32)
        sidx = sb("sidx", [P, 2 * E], U32)
        gstage = sb("gstage", [P, 4, 2], U32)
        sstage = sb("sstage", [P, 4, 2], U32)
        wcol = [sb(f"wcol{i}", [P, 2]) for i in range(4)]
        sb("beyond_parameters", [P, 7552])
        wgu = [sb(f"wgu{i}", [P, 2, C, I]) for i in range(NW)]
        wd = [sb(f"wd{i}", [P, D]) for i in range(NW)]
        xg = [sb(f"xg{i}", [P, 2, HW]) for i in range(NX)]
        xgT = [sb(f"xgT{i}", [P, C, CAP]) for i in range(2)]
        sg = [sb(f"sg{i}", [P, CAP]) for i in range(2)]
        hm = [sb(f"hm{i}", [P, CAP]) for i in range(2)]
        ys = [sb(f"ys{i}", [P, 2, D]) for i in range(NY)]
        NF = 8
        fx = sb("fx", [P, B * T, D])
        fg = sb("fg", [P, B, D])
        fa = [sb(f"fa{i}", [P, 2, T, D]) for i in range(NF)]
        moe.close()
        eng_moe = dict(
            w_ld=[sem(f"weights_loaded{i}") for i in range(NW)],
            x_ld=[sem(f"rows_gathered{i}") for i in range(NX)],
            y_st=[sem(f"rows_added{i}") for i in range(NY)],
            gst=sem("gather_indices_staged"), sst=sem("scatter_indices_staged"),
            xTp=sem("rows_turned"), xTc=sem("first_features_kept"), xTd=sem("second_features_kept"), gp=sem("gate_up_made"),
            sg=sem("silu_done"), wc=sem("slot_weights_staged"),
            hm=sem("hidden_done"), yp=sem("expert_out_made"), yc=sem("expert_out_scaled"),
            f_ld=[sem(f"sums_loaded{i}") for i in range(NF)], fsum=sem("last_sums"), fout=sem("out_made"),
            f_st=sem("out_stored"),
        )
        mo = eng_moe

        NCONST = 32
        NSET = 10
        PROJ_SLOTS = (5, 6, 7, 8)
        STORE_SLOTS = (6, 7, 9, 10)
        SPLITS = {5: 2, 6: 2, 7: 2, 8: 2, 9: 2, 10: 2}
        ROUTE_SLOTS = {12: [0], 13: [1, 2, 3], 14: [4], 15: [5], 16: [6, 7], 17: [8], 18: [9, 10], 19: [11]}
        FILLS = {4: [0, 1], 0: [2, 3], 1: [4, 5], 2: [6, 7], 3: []}
        LATE = dict(onT=(bA, bST[0]), op=(bST[1], bO), h2T=(bA, bST[0]), cnt=bT, idx=(bS[0], bS[1]))
        block = ctx.enter_context(nc.Block())

        def ahead_of(now, nxt, g, u):
            q = g + 1 + (u == U - 1)
            return (now, q) if q < QUADS else (nxt, q - QUADS)

        def loops(eng, body, prolog=None, epilog=None):
            body(None, batch(0), batch(1))
            with eng.Fori(0, (B - 2) // 2) as it:
                for j in range(2):
                    now = Batch(it * 2 + (1 + j), it + j, 1 - j)
                    prev = Batch(it * 2 + j, it, j)
                    nxt = Batch(it * 2 + (2 + j), it + 1, j)
                    body(prev, now, nxt)
            body(batch(B - 2), batch(B - 1), None)

        @block.sync
        def _(sp):
            start_counts(sp, "SP")
            bc = lambda ap, n: ap.rearrange("(o d) -> o d", o=1).to_broadcast([P, n])
            sp.dma_start(cin, c[:, :]).then_inc(s_cin, 16)
            sp.dma_start(xt[:], x[0].rearrange("(t p) d -> p t d", p=P)).then_inc(x_ld[0], 16)
            sp.dma_start(wm[:, :, 0:2 * D], wmod.rearrange("(c p) n -> p c n", p=P)[:, :, 0:2 * D]).then_inc(s_wm1, 16)
            sp.dma_start(wqkv[:], w_qkv.rearrange("(c p) n -> p c n", p=P)).then_inc(s_wq, 16)
            sp.dma_start(bqk[:], b_qkv[0:4 * P].rearrange("(c p) -> p c", p=P),
                         allow_slow_non_contiguous=True).then_inc(s_wq, 16)
            sp.dma_start(wm[:, :, 2 * D:6 * D], wmod.rearrange("(c p) n -> p c n", p=P)[:, :, 2 * D:6 * D]
                         ).then_inc(s_wm2, 16)
            sp.dma_start(bv[:], bc(b_qkv[2 * D:3 * D], D)).then_inc(s_par, 16)
            sp.dma_start(bo[:], bc(b_out, D)).then_inc(s_par, 16)
            sp.dma_start(gb[:], bc(gate_bias, E)).then_inc(s_par, 16)
            sp.dma_start(gw, gate_w[:, :]).then_inc(s_par, 16)
            sp.dma_start(wo[:], w_out.rearrange("(c p) n -> p c n", p=P)).then_inc(s_par, 16)
            sp.wait_ge(s_const, NCONST)
            for i in range(2):
                sp.dma_start(Ks[i][MROW:KROWS, :, :].rearrange("a h (r n) -> a (h r) n", n=P),
                             onesb[0:2, :].unsqueeze(1).to_broadcast([2, H * KW // P, P])).then_inc(s_ones, 16)
            def zero_acc(bt):
                i = bass.ds(bt.b, 1) if not isinstance(bt.b, int) else slice(bt.b, bt.b + 1)
                for acc in acc_d:
                    for h in range(2):
                        dst = acc.rearrange("r d -> (r d)").rearrange("(b h p n) -> b h p n", b=B, h=2, p=P)[i, h]
                        sp.dma_start(dst.rearrange("o p n -> p (o n)"), zero[:]).then_inc(s_zero, 16)

            def load_x(bt):
                after(sp, "xn", bt, 0)
                row = x[bass.ds(bt.b, 1)] if not isinstance(bt.b, int) else x[bt.b:bt.b + 1]
                sp.dma_start(xt[:], row.rearrange("o (t p) d -> p (o t) d", p=P)).then_inc(x_ld[bt.par], 16)

            def load_c(bt):
                after(sp, "h2", bt, 0)
                after(sp, "x1", bt, 0)
                i = bass.ds(bt.b, 1) if not isinstance(bt.b, int) else slice(bt.b, bt.b + 1)
                sp.dma_start(xc[:], x[i].rearrange("o (t p) d -> p (o t) d", p=P)).then_inc(sems["c_ld"], 16)
                sp.dma_start(mr[:], mod_d[i, 0:3, :].rearrange("o k d -> o (k d)").to_broadcast([P, 3 * D])
                             ).then_inc(sems["c_ld"], 16)

            def store_parts(bt, j):
                after(sp, "lpart", bt, j + 1)
                after(sp, "mpart", bt, j + 1)
                after(sp, "hpart", bt, j + 1)
                if j % 2 == 0:
                    after(sp, "qk_ld", bt, 0)
                dst = parts_d[bt.par][j // 2, :, (j % 2) * P:(j % 2 + 1) * P, :]
                sp.dma_start(dst.rearrange("k p s -> p k s"), parts[:, j % 2, :, :]).then_inc(parts_st[j % 2], 16)

            def load_stack(bt, which):
                parts_stored(sp, bt, 0, which + 1)
                parts_stored(sp, bt, 1, which + 1)
                if not isinstance(bt.b, int) or bt.b >= 2:
                    after(sp, "STp", Batch(bt.b - 1, 0, 0), 0)
                dst = Qs[bt.par] if which == 0 else Ks[bt.par]
                lo = 0 if which == 0 else BAND
                for n, pair in enumerate(PAIRS):
                    src = parts_d[bt.par][which, pair[which]].rearrange("(h d) s -> d h s", d=HD)
                    sp.dma_start(dst[n * HD:(n + 1) * HD, :, lo:lo + S], src).then_inc(sems["qk_ld"], 16)

            def mrows(bt, g):
                after(sp, "mT", bt, g + 1)
                sp.dma_start(Qs[bt.par][MROW:KROWS, HQ * g:HQ * g + HQ, :].rearrange("a h q -> a (h q)"),
                             MT[:]).then_inc(sems["mrow_ld"], 16)

            def body(prev, now, nxt):
                for slot in range(SLOTS):
                    g, u = divmod(slot, U)
                    if slot == 0 and nxt:
                        load_x(nxt)
                    if slot == 0 and prev:
                        load_c(prev)
                    if u == 3 and (g < QUADS - 1 or nxt):
                        mrows(*((now, g + 1) if g < QUADS - 1 else (nxt, 0)))
                    if nxt and slot in STORE_SLOTS:
                        store_parts(nxt, STORE_SLOTS.index(slot))
                    if nxt and slot in (8, 11):
                        load_stack(nxt, (slot - 8) // 3)
                    if slot == 12:
                        zero_acc(now)
                    if prev and slot == 9:
                        store_x1(prev)

            def store_x1(bt):
                after(sp, "x1", bt, 2)
                i = bass.ds(bt.b, 1) if not isinstance(bt.b, int) else slice(bt.b, bt.b + 1)
                sp.dma_start(x1_d[i].rearrange("o (t p) d -> p (o t) d", p=P), x1[:]).then_inc(sems["x1_st"], 16)

            first = batch(0)
            for j in range(4):
                store_parts(first, j)
                if j % 2:
                    load_stack(first, j // 2)
            sp.wait_ge(s_v0, 9)
            sp.dma_start(mod_d[:, 0:4:3, :], gates[:, 0, :, :]).then_inc(s_mod_st, 16)
            sp.dma_start(mod_d[:, 1:3, :], gates[:, 1, :, :]).then_inc(s_mod_st, 16)
            mrows(first, 0)
            sp.wait_ge(s_mod_st, 32)
            loops(sp, body)
            last = batch(B - 1)
            load_c(last)
            store_x1(last)

            def load_w(e, half, n):
                sp.dma_start(wgu[n][:, 0], w_gate[e].rearrange("o (c p) i -> p (o c) i", p=P)).then_inc(mo["w_ld"][n], 16)
                sp.dma_start(wgu[n][:, 1], w_up[e].rearrange("o (c p) i -> p (o c) i", p=P)).then_inc(mo["w_ld"][n], 16)
                sp.dma_start(wd[n][:], w_down[e].rearrange("o i d -> i (o d)")).then_inc(mo["w_ld"][n], 16)

            after(sp, "pv", batch(B), 0)
            for n in range(NW):
                load_w(slice(n, n + 1), 0, n)
            with sp.Fori(1, E // NW) as it:
                for n in range(NW):
                    hold(sp, mo["yp"], it * NW + (n - NW + 1))
                    load_w(bass.ds(it * NW + n, 1), it, n)

            sp.dma_start(fx[:], x1_d.rearrange("b (t p) d -> p (b t) d", p=P)).then_inc(s_fx, 16)
            sp.dma_start(fg[:], mod_d[:, 3, :].unsqueeze(0).to_broadcast([P, B, D])).then_inc(s_fx, 16)
            for n in range(NY):
                sp.wait_ge(mo["y_st"][n], 32 * E // NY)

            def load_f(i, n):
                for k in range(2):
                    sp.dma_start(fa[n][:, k], acc_d[k][0:N, :].rearrange("(b t p) d -> b p t d", b=B, p=P)[i]
                                 .rearrange("o p t d -> p (o t) d")).then_inc(mo["f_ld"][n], 16)

            def store_f(i, n):
                sp.dma_start(out[i].rearrange("o (t p) d -> p (o t) d", p=P), fa[n][:, 0]).then_inc(mo["f_st"], 16)

            for b in range(B):
                if b >= NF:
                    sp.wait_ge(mo["f_st"], 16 * (b - NF + 1))
                load_f(slice(b, b + 1), b % NF)
                if b >= NF - 1:
                    sp.wait_ge(mo["fout"], b - NF + 2)
                    store_f(slice(b - NF + 1, b - NF + 2), (b + 1) % NF)
            for b in range(B - NF + 1, B):
                sp.wait_ge(mo["fout"], b + 1)
                store_f(slice(b, b + 1), b % NF)
            sp.wait_ge(mo["f_st"], 16 * B)

        @block.gpsimd
        def _(pool):
            start_counts(pool, "Pool")
            gp = nc.gpsimd
            n = [0]
            nothing = pool.to_reg(0.0)
            last_row = pool.to_reg(N - 1)
            last_acc = pool.to_reg(ACCROWS - 1)

            def const(ins):
                ins.then_inc(s_const, 1)
                n[0] += 1
                pool.wait_ge(s_const, n[0])

            const(gp.memset(half_c[:], -0.5))
            const(gp.memset(ident[:], 0.0))
            const(gp.affine_select(out=ident[:], in_=ident[:], compare_op=ALU.not_equal, fill=1.0, base=0,
                                   pattern=[[-1, P]], channel_multiplier=1))
            const(gp.tensor_copy(identb[:], ident[:]))

            def a_rstd(bt):
                after(pool, "aggr", bt, T)
                after(pool, "xn", bt, 0)
                gp.tensor_scalar(ve[:], mv[:, :, 1], EPS, None, ALU.add).then_inc(sems["rstd"], 1)
                after(pool, "rstd", bt, 1)
                gp.tensor_tensor(rs[:], ve[:], half_c[:], ALU.pow).then_inc(sems["rstd"], 1)
                gp.tensor_scalar(nmean[:], mv[:, :, 0], -1.0, None, ALU.mult).then_inc(sems["rstd"], 1)
                after(pool, "rstd", bt, 3)
                gp.tensor_tensor(nmean[:], nmean[:], rs[:], ALU.mult).then_inc(sems["rstd"], 1)

            def a_split(bt, n):
                j, k = divmod(n, 3)
                if k == 0:
                    after(pool, "hpart", bt, j + 1)
                    parts_stored(pool, bt, j, j // 2)
                    after(pool, "lpart", bt, j)
                    gp.tensor_tensor(r32[:], p32[j % 2][:], parts[:, j % 2, 0, :], ALU.subtract
                                     ).then_inc(sems["r32"], 1)
                elif k == 1:
                    gp.tensor_tensor(parts[:, j % 2, 1, :], p32[j % 2][:], parts[:, j % 2, 0, :], ALU.subtract
                                     ).then_inc(sems["mpart"], 1)
                else:
                    after(pool, "r32", bt, j + 1)
                    after(pool, "mpart", bt, j + 1)
                    gp.tensor_tensor(parts[:, j % 2, 2, :], r32[:], parts[:, j % 2, 1, :], ALU.subtract
                                     ).then_inc(sems["lpart"], 1)

            def cuts(bt, g, u, p):
                if True:
                    m = 10 * g + 2 * u + p
                    pt = PT[m % NPT]
                    after(pool, "exp", bt, m + 1)
                    if u > 0:
                        v = pt[:, :, 0:P]
                        gp.affine_select(out=v, in_=v, compare_op=ALU.is_ge, fill=nothing, base=0,
                                         pattern=[[0, 2], [1, P]], channel_multiplier=-1).then_inc(sems["cut"], 1)
                    if u < U - 1:
                        v = pt[:, :, 0:P] if u == 0 else pt[:, :, P:2 * P]
                        gp.affine_select(out=v, in_=v, compare_op=ALU.is_ge, fill=nothing, base=0,
                                         pattern=[[0, 2], [-1, P]], channel_multiplier=1).then_inc(sems["cut"], 1)

            def c_xb(bt):
                after(pool, "c_ld", bt, 32)
                after(pool, "xb", bt, 0)
                gp.tensor_tensor(gbo[:], mr[:, 0, :], bo[:], ALU.mult).then_inc(sems["xb"], 1)
                after(pool, "xb", bt, 1)
                gp.tensor_tensor(xc[:], xc[:], gbo[:, :].unsqueeze(1).to_broadcast([P, T, D]), ALU.add
                                 ).then_inc(sems["xb"], 1)

            def c_rstd(bt):
                after(pool, "aggr2", bt, T)
                after(pool, "xn2", bt, 0)
                gp.tensor_scalar(ve2[:], mv2[:, :, 1], EPS, None, ALU.add).then_inc(sems["rstd2"], 1)
                after(pool, "rstd2", bt, 1)
                gp.tensor_tensor(rs2[:], ve2[:], half_c[:], ALU.pow).then_inc(sems["rstd2"], 1)

            def body(prev, now, nxt):
                for slot in range(SLOTS):
                    g, u = divmod(slot, U)
                    for p in range(2):
                        cuts(now, g, u, p)
                        if nxt and p < SPLITS.get(slot, 0):
                            a_split(nxt, sum(n for at, n in SPLITS.items() if at < slot) + p)
                    if nxt and slot == 1:
                        a_rstd(nxt)
                    if prev and slot == 2:
                        c_xb(prev)
                    if prev and slot == 6:
                        c_rstd(prev)

            a_rstd(batch(0))
            const(gp.memset(onesb[:], 1.0))
            const(gp.affine_select(out=before[:], in_=onesb[:], compare_op=ALU.is_gt, fill=0.0, base=0,
                                   pattern=[[1, P]], channel_multiplier=-1))
            const(gp.memset(mask[:], 0.0))
            const(gp.affine_select(out=mask[:], in_=mask[:], compare_op=ALU.is_ge, fill=NEG, base=0,
                                   pattern=[[0, 3], [1, 2 * P]], channel_multiplier=-1))
            const(gp.affine_select(out=mask[:], in_=mask[:], compare_op=ALU.is_ge, fill=NEG, base=2 * BAND,
                                   pattern=[[0, 3], [-1, 2 * P]], channel_multiplier=1))
            const(gp.memset(mask[:, 0, 0:BAND], NEG))
            const(gp.memset(mask[:, 2, 2 * P - BAND:2 * P], NEG))
            const(gp.iota(digits[:], pattern=[[1, LO], [0, EG]], base=0, channel_multiplier=0))
            const(gp.memset(lowerg[:], 1.0))
            const(gp.affine_select(out=lowerg[:], in_=lowerg[:], compare_op=ALU.is_gt, fill=0.0, base=0,
                                   pattern=[[1, G], [-1, G]], channel_multiplier=0))
            half = N // P // 2
            const(gp.iota(valt[:, 0:half], pattern=[[P, half]], base=1, channel_multiplier=1,
                          allow_small_or_imprecise_dtypes=True))
            const(gp.iota(valt[:, half:], pattern=[[-P, half]], base=-1, channel_multiplier=-1,
                          allow_small_or_imprecise_dtypes=True))
            const(gp.iota(bits_e, pattern=[[-1, EG], [0, LO]], base=P, channel_multiplier=1))
            const(gp.iota(bits_k, pattern=[[-EG, P // LO], [0, LO]], base=P, channel_multiplier=1))
            const(gp.iota(bits_eh, pattern=[[-1, EG], [-P // 2, 2]], base=P, channel_multiplier=1))
            const(gp.iota(empty[:], pattern=[[0, E], [P, 2]], base=N + 1, channel_multiplier=1,
                          allow_small_or_imprecise_dtypes=True))
            const(gp.memset(zero[:], 0.0))
            for i in range(2):
                const(gp.memset(Va[i][:, :, :, HD:HD + 1], 1.0))
                const(gp.memset(Va[i][:, :, :, HD + 1:], 0.0))
            const(gp.memset(hT[:, :, 0:BAND], 0.0))
            const(gp.memset(hT[:, :, BAND + S:KW], 0.0))
            const(gp.memset(M2[:], 0.0))
            const(gp.memset(Spre[:], 0.0))
            const(gp.memset(selb[:], 0.0))
            const(gp.memset(vt[:], 0.0))
            const(gp.memset(iacc[:], 0.0))
            assert n[0] == NCONST
            for j in range(4):
                a_split(batch(0), 3 * j)
            loops(pool, body)
            last = batch(B - 1)
            c_xb(last)
            c_rstd(last)

            done = Batch(B, 0, 0)
            def gather(n4, count_half):
                for h in range(2):
                    pool.indirect_dma_start(
                        out=xg[n4][:, h, :], out_offset=None, in_=htab[:, :],
                        in_offset=bass.IndirectOffsetOnAxis(ap=gstage[:, n4, h:h + 1], axis=0),
                        bounds_check=last_row, oob_is_err=False).then_inc(mo["x_ld"][n4], 16)

            def scatter(n4):
                for h in range(2):
                    pool.indirect_dma_start(
                        out=acc_d[n4 % 2][:, :], in_=ys[n4][:, h, :], in_offset=None,
                        out_offset=bass.IndirectOffsetOnAxis(ap=sstage[:, n4, h:h + 1], axis=0),
                        bounds_check=last_acc, oob_is_err=True, compute_op=ALU.add).then_inc(mo["y_st"][n4], 16)

            after(pool, "h_st", done, 0)
            pool.wait_ge(s_zero, 16 * 4 * B)
            pool.wait_ge(mo["gst"], NX)
            for n4 in range(3):
                gather(n4, 0)
            def four(it):
                for n4 in range(4):
                    m4 = (n4 + 3) % 4
                    hold(pool, mo["gst"], it * 4 + (n4 + 4))
                    if not isinstance(it, int) or n4 > 0:
                        hold(pool, mo["gp"], it * 4 + n4)
                        hold(pool, mo["wc"], it * 4 + n4)
                    gather(m4, 0)
                    hold(pool, mo["sst"], it * 4 + (n4 + 1))
                    hold(pool, mo["yc"], it * 8 + (2 * n4 + 2))
                    if n4 >= 2:
                        hold(pool, mo["y_st"][n4 - 2], it * 32 + 32)
                    elif not isinstance(it, int):
                        hold(pool, mo["y_st"][n4 + 2], it * 32)
                    scatter(n4)

            four(0)
            with pool.Fori(1, E // 4 - 1) as it:
                four(it)
            for n4 in range(4):
                e = E - 4 + n4
                if n4 == 0:
                    pool.wait_ge(mo["gst"], E)
                    pool.wait_ge(mo["gp"], e)
                    pool.wait_ge(mo["wc"], e)
                    gather(3, 0)
                pool.wait_ge(mo["sst"], e + 1)
                pool.wait_ge(mo["yc"], 2 * e + 2)
                pool.wait_ge(mo["y_st"][(n4 + 2) % 4], 32 * (E // 4 - (n4 < 2)))
                scatter(n4)

            pool.wait_ge(s_fx, 32)
            for b in range(B):
                a = fa[b % NF]
                pool.wait_ge(mo["fsum"], 2 * b + 2)
                gp.tensor_tensor(a[:, 0], a[:, 0], fx[:, b * T:(b + 1) * T, :], ALU.add).then_inc(mo["fout"], 1)

        @block.scalar
        def _(act):
            start_counts(act, "Act")
            sc_ = nc.scalar
            act.wait_ge(s_cin, 16)
            sc_.activation(sil[:, 0, :], cin, ACT.Exp, scale=-1.0).then_inc(s_a0, 1)
            def a_norm(bt):
                after(act, "rstd", bt, 4)
                after(act, "hTp", bt, 0)
                for t in range(T):
                    sc_.activation(xn[:, t, :], xt[:, t, :], ACT.Identity, scale=rs[:, t:t + 1], bias=nmean[:, t:t + 1]
                                   ).then_inc(sems["xn"], 1)

            def a_hT(bt, k):
                after(act, "hTp", bt, k + 1)
                after(act, "mcol", bt, 1)
                after(act, "vp", bt, 0)
                sc_.activation(hT[:, k, BAND:BAND + S], bA[:, :], ACT.Identity, scale=mcol[:, 2 + k:3 + k],
                               bias=mcol[:, k:k + 1]).then_inc(sems["hT"], 1)

            def a_p32(bt, j):
                after(act, "proj", bt, j + 1)
                if j >= 2:
                    after(act, "lpart", bt, j - 1)
                else:
                    after(act, "lpart", bt, 0)
                sc_.activation(p32[j % 2][:], bA[:, :], ACT.Identity, scale=SCALE if j < 2 else 1.0,
                               bias=bqk[:, j:j + 1]).then_inc(sems["p32"], 1)
                after(act, "p32", bt, j + 1)
                parts_stored(act, bt, j, j // 2)
                sc_.activation(parts[:, j % 2, 0, :], p32[j % 2][:], ACT.Copy).then_inc(sems["hpart"], 1)

            def exps(bt, g, u, p):
                m = 10 * g + 2 * u + p
                after(act, "STp", bt, m + 1)
                after(act, "pv", bt, m - NPT + 1)
                w = P if u in (0, U - 1) else 2 * P
                src = bST[m % 2][:, 0:2 * w].rearrange("p (h q) -> p h q", h=2)
                sc_.activation(PT[m % NPT][:, :, 0:w], src, ACT.Exp).then_inc(sems["exp"], 1)

            def take_mT(bt, g):
                after(act, "mTp", bt, g + 1)
                after(act, "mrow_ld", bt, 16 * g)
                sc_.activation(MT[:], bT[0:32, 0:P // 2].bitcast(BF16), ACT.Copy).then_inc(sems["mT"], 1)

            def take_oT(bt, g):
                after(act, "pv", bt, 10 * g + 10)
                after(act, "oTp", bt, g)
                sc_.activation(OTs[:], bO[:, :], ACT.Copy).then_inc(sems["oTs"], 1)

            def c_onT(bt, k, bank=bC):
                after(act, "onTp", bt, k + 1)
                after(act, "op", bt, 0)
                sc_.activation(onT[:, k, :], bank[:, :], ACT.Copy).then_inc(sems["onT"], 1)

            def c_h2T(bt, k, bank=bC):
                after(act, "h2Tp", bt, k + 1)
                after(act, "lg", bt, 0)
                sc_.activation(h2T[:, k, :], bank[:, :], ACT.Copy).then_inc(sems["h2T"], 1)

            def c_ex(bt):
                after(act, "lg", bt, 1)
                after(act, "pos", bt, 4)
                sc_.activation(ex[:], bC[:, 0:T * E], ACT.Exp, scale=-1.0).then_inc(sems["ex"], 1)

            def store_h(bt):
                after(act, "route", bt, PER["route"], apart=True)
                after(act, "h2", bt, T, apart=True)
                i = bass.ds(bt.b, 1) if not isinstance(bt.b, int) else slice(bt.b, bt.b + 1)
                act.dma_start(htab.rearrange("(b t p) d -> b p t d", p=P, t=T)[i].rearrange("o p t d -> p (o t) d"),
                              H2[:]).then_inc(sems["h_st"], 16)

            def body(prev, now, nxt):
                for slot in range(SLOTS):
                    g, u = divmod(slot, U)
                    exps(now, g, u, 0)
                    if u == 3 and (g < QUADS - 1 or nxt):
                        take_mT(*((now, g + 1) if g < QUADS - 1 else (nxt, 0)))
                    exps(now, g, u, 1)
                    if u == 0 and (g > 0 or prev):
                        take_oT(*((now, g - 1) if g > 0 else (prev, QUADS - 1)))
                    if nxt and slot == 2:
                        a_norm(nxt)
                    if nxt and slot in (3, 4):
                        a_hT(nxt, slot - 3)
                    if nxt and slot in PROJ_SLOTS:
                        a_p32(nxt, PROJ_SLOTS.index(slot))
                    if prev and slot in (2, 3):
                        c_onT(prev, slot - 2)
                    if prev and slot in (9, 10):
                        c_h2T(prev, slot - 9)
                    if prev and slot == 11:
                        c_ex(prev)
                    if prev and slot == 19:
                        store_h(prev)

            a_norm(batch(0))
            a_hT(batch(0), 0)
            a_hT(batch(0), 1)
            act.wait_ge(s_v0, 7)
            for j in range(4):
                a_p32(batch(0), j)
            take_mT(batch(0), 0)
            loops(act, body)
            last = batch(B - 1)
            take_oT(last, QUADS - 1)
            for k in range(C):
                c_onT(last, k, LATE["onT"][k])
            for k in range(C):
                c_h2T(last, k, LATE["h2T"][k])
            c_ex(last)
            store_h(last)

            def take_x(it, n):
                need(act, mo["xTp"], it * 8 + (2 * n + 1))
                need(act, mo["gp"], it * 4 + (n - 1))
                sc_.activation(xgT[n % 2][:, 0, :], bS[n % 2][:, 0:CAP], ACT.Copy).then_inc(mo["xTc"], 1)

            def silu(it, n):
                need(act, mo["gp"], it * 4 + (n + 1))
                need(act, mo["hm"], it * 4 + (n - 1))
                sc_.activation(sg[n % 2][:], bST[n % 2][:, 0:CAP], ACT.Silu).then_inc(mo["sg"], 1)

            def scale_y(it, n):
                need(act, mo["yp"], it * 4 + (n + 1))
                need(act, mo["wc"], it * 4 + (n + 1))
                need(act, mo["y_st"][n % 4], (it + n // 4) * 32)
                yb = bO if n % 2 == 0 else bT
                for h in range(2):
                    sc_.activation(ys[n % 4][:, h, :], yb[:, h * D:(h + 1) * D], ACT.Copy,
                                   scale=wcol[n % 4][:, h:h + 1]).then_inc(mo["yc"], 1)

            def four(it, first=False, final=False):
                for n in range(4):
                    silu(it, n)
                    if not (final and n == 3):
                        take_x(it, n + 1)
                    if not (first and n == 0):
                        scale_y(it, n - 1)

            take_x(0, 0)
            four(0, first=True)
            with act.Fori(1, E // 4 - 1) as it:
                four(it)
            four(E // 4 - 1, final=True)
            scale_y(E // 4 - 1, 3)

        @block.tensor
        def _(pe):
            start_counts(pe, "PE")
            mm = nc.tensor.matmul
            pe.wait_ge(s_const, 3)
            pe.wait_ge(s_v0, 3)
            for k in range(C):
                nc.tensor.transpose(bA[:, k * B:(k + 1) * B], sil[:, 2, k * P:(k + 1) * P], ident[0:B, 0:B]
                                    ).then_inc(s_pe0, 1)
            pe.wait_ge(s_v0, 4)
            pe.wait_ge(s_wm1, 16)
            for n in range(4):
                col = (n // 2) * D + (n % 2) * P
                for k in range(C):
                    last = mm(bT[:, n * B:(n + 1) * B], wm[:, k, col:col + P], silT[:, k, :], start=(k == 0), stop=(k == C - 1))
            last.then_inc(s_pe0, 1)

            def gate_sums():
                for k in range(C):
                    last = nc.tensor.transpose(bC[:, k * E:(k + 1) * E], gw[:, k * P:(k + 1) * P], ident[0:E, 0:E])
                last.then_inc(s_pe0, 1)
                for n, bank in enumerate((bS[0], bS[1])):
                    for q, col in enumerate(((2, 5), (3, 4))[n]):
                        for k in range(C):
                            last = mm(bank[0:B, q * D:(q + 1) * D], silT[:, k, :], wm[:, k, col * D:(col + 1) * D],
                                      start=(k == 0), stop=(k == C - 1))
                    last.then_inc(s_pe0, 1)

            def a_hT(bt, k):
                after(pe, "xn", bt, T)
                if k == 0:
                    after(pe, "v", bt, 0)
                else:
                    after(pe, "hT", bt, k)
                for t in range(T):
                    last = nc.tensor.transpose(bA[:, t * P:(t + 1) * P], xn[:, t, k * P:(k + 1) * P], ident[:])
                last.then_inc(sems["hTp"], 1)

            def a_proj(bt, j):
                if j == 0:
                    after(pe, "hT", bt, C)
                else:
                    after(pe, "p32", bt, j)
                for k in range(C):
                    last = mm(bA[:, :], wqkv[:, k, j * P:(j + 1) * P], hT[:, k, BAND:BAND + S], start=(k == 0), stop=(k == C - 1))
                last.then_inc(sems["proj"], 1)

            def a_v(bt, j):
                if j == 0:
                    after(pe, "p32", bt, 4)
                else:
                    after(pe, "v", bt, j)
                for i, u in enumerate(range(2 * j, min(2 * j + 2, U))):
                    for k in range(C):
                        last = mm(bA[:, i * D:(i + 1) * D], hT[:, k, u * P:(u + 1) * P], wqkv[:, k, 2 * D:3 * D],
                                  start=(k == 0), stop=(k == C - 1))
                last.then_inc(sems["vp"], 1)

            def fills(bt, g, ks):
                if not ks:
                    return
                if g == 0 and ks[0] == 0:
                    after(pe, "qk_ld", bt, 192)
                q, kk = Qs[bt.par], Ks[bt.par]
                for n in ks:
                    t, pr = divmod(n, 2)
                    after(pe, "smax", bt, 2 * (8 * g + n - 1))
                    for i in range(2):
                        h = HQ * g + 2 * pr + i
                        last = mm(bS[n % 2][:, i * 2 * P:(i + 1) * 2 * P], q[0:MROW, h, t * P:(t + 1) * P],
                                  kk[0:MROW, h, t * P:(t + 2) * P], start=True, stop=True)
                    last.then_inc(sems["Sp"], 1)

            def turn_m(bt, g):
                after(pe, "m2", bt, 2 * g + 2)
                after(pe, "on", bt, g - 1)
                nc.tensor.transpose(bT[:, 0:P // 2].bitcast(BF16), M2[:], identb[:]).then_inc(sems["mTp"], 1)

            def qrange(u):
                return max(u - 1, 0) * P, min(u + 1, T) * P

            def scoresT(bt, g, u, p):
                if u == 0 and p == 0:
                    after(pe, "mrow_ld", bt, 16 * (g + 1))
                q, kk = Qs[bt.par], Ks[bt.par]
                lo, hi = qrange(u)
                if True:
                    m = 10 * g + 2 * u + p
                    after(pe, "exp", bt, m - 1)
                    for i in range(2):
                        h = HQ * g + 2 * p + i
                        last = mm(bST[m % 2][:, i * (hi - lo):(i + 1) * (hi - lo)], kk[0:KROWS, h, u * P:(u + 1) * P],
                                  q[0:KROWS, h, lo:hi], start=True, stop=True)
                    last.then_inc(sems["STp"], 1)

            def values(bt, g, u, p):
                if g == 0 and u == 0 and p == 0:
                    after(pe, "v", bt, 3)
                if u == 0 and p == 0:
                    after(pe, "oTs", bt, g)
                lo, hi = qrange(u)
                rows = slice(BAND, P) if u == 0 else slice(0, BAND) if u == U - 1 else slice(0, P)
                if True:
                    m = 10 * g + 2 * u + p
                    after(pe, "cut", bt, 16 * g + 2 * SEL_BEFORE[u] + SEL_OF[u] * (p + 1), apart=True)
                    for i in range(2):
                        j = 2 * p + i
                        last = mm(bO[32 * j:32 * j + 32, lo:hi], Va[bt.par][rows, u, HQ * g + j, :],
                                  PT[m % NPT][rows, i, 0:hi - lo], start=(u == 0), stop=(u == U - 1),
                                  skip_group_check=True)
                    last.then_inc(sems["pv"], 1)

            def turn_o(bt, g):
                after(pe, "oTs", bt, g + 1)
                after(pe, "mT", *((bt, g + 2) if g < QUADS - 1 else (Batch(bt.b + 1, 0, 0), 1))) if True else None
                for t in range(T):
                    last = nc.tensor.transpose(bT[:, t * P:(t + 1) * P], OTs[:, t * P:(t + 1) * P], ident[:])
                last.then_inc(sems["oTp"], 1)

            def turn_o_last(bt):
                after(pe, "oTs", bt, QUADS)
                after(pe, "on", bt, QUADS - 1)
                for t in range(T):
                    last = nc.tensor.transpose(bT[:, t * P:(t + 1) * P], OTs[:, t * P:(t + 1) * P], ident[:])
                last.then_inc(sems["oTp"], 1)

            def c_onT(bt, k, bank=bC):
                after(pe, "on", bt, QUADS)
                if bank is not bC:
                    pass
                elif k == 0:
                    after(pe, "pos", bt, 1)
                else:
                    after(pe, "onT", bt, k)
                for t in range(T):
                    last = nc.tensor.transpose(bank[:, t * P:(t + 1) * P], on[:, t, k * P:(k + 1) * P], ident[:])
                last.then_inc(sems["onTp"], 1)

            def c_op(bt, n, bank=bC):
                after(pe, "onT", bt, C)
                if bank is bC:
                    after(pe, "t1", bt, n)
                for i in range(2):
                    t = 2 * n + i
                    for k in range(C):
                        last = mm(bank[:, i * D:(i + 1) * D], onT[:, k, t * P:(t + 1) * P], wo[:, k, :],
                                  start=(k == 0), stop=(k == C - 1))
                last.then_inc(sems["op"], 1)

            def c_h2T(bt, k, bank=bC):
                after(pe, "h2", bt, T)
                if bank is not bC:
                    pass
                elif k == 0:
                    after(pe, "idx", bt, 2)
                else:
                    after(pe, "h2T", bt, k)
                for t in range(T):
                    last = nc.tensor.transpose(bank[:, t * P:(t + 1) * P], H2[:, t, k * P:(k + 1) * P], ident[:])
                last.then_inc(sems["h2Tp"], 1)

            def c_lg(bt):
                after(pe, "h2T", bt, C)
                for t in range(T):
                    for k in range(C):
                        last = mm(bC[:, t * E:(t + 1) * E], h2T[:, k, t * P:(t + 1) * P], gwT[:, k, :],
                                  start=(k == 0), stop=(k == C - 1))
                last.then_inc(sems["lg"], 1)

            def e_cnt(bt, bank=bC):
                after(pe, "ex", bt, 0)
                after(pe, "pre", bt, 0)
                mm(bank[:, 0:T * E], before[:], selb[:], start=True, stop=False)
                mm(bank[:, 0:T * E], onesb[:], Spre[:, 0:T, :].rearrange("p t e -> p (t e)"), start=False, stop=True
                   ).then_inc(sems["cntp"], 1)

            def e_idx(bt, half):
                if half == 0:
                    after(pe, "pos", bt, 1)
                    after(pe, "oneh", bt, 3 * T)
                    after(pe, "t1", bt, 2)
                else:
                    after(pe, "idx", bt, 1)
                for i in range(G // 2):
                    g = half * (G // 2) + i
                    for t in range(T):
                        last = mm(bC[:, i * P:(i + 1) * P], oneh[:, t, g].rearrange("p a e -> p (a e)"),
                                  oneh[:, T + t, g].rearrange("p b e -> p e b"), start=(t == 0), stop=(t == T - 1))
                last.then_inc(sems["idxp"], 1)

            def e_idx_late(bt, t):
                after(pe, "oneh", bt, 3 * (t + 1))
                for g in range(G):
                    first_mm, last_mm = bt.b == B - 1 and t == 0 and g % 4 == 0, bt.b == B and t == T - 1
                    last = mm(LATE["idx"][g // 4][:, g % 4 * P:(g % 4 + 1) * P], oneh[:, t, g].rearrange("p a e -> p (a e)"),
                              oneh[:, T + t, g].rearrange("p b e -> p e b"), start=first_mm, stop=last_mm,
                              skip_group_check=True)
                    if last_mm and g % 4 == 3:
                        last.then_inc(sems["idxp"], 1)
                if t == T - 1 and bt.b == B - 1:
                    last.then_inc(s_late, 1)

            def body(prev, now, nxt):
                for slot in range(SLOTS):
                    g, u = divmod(slot, U)
                    ahead = ahead_of(now, nxt, g, u)
                    ks = FILLS[u] if ahead[0] else []
                    last = (now, *divmod(slot - 1, U)) if slot else (prev, QUADS - 1, U - 1)
                    for p in range(2):
                        scoresT(now, g, u, p)
                        fills(*ahead, ks[p:p + 1])
                        if p == 0 and u == 3 and ahead[0]:
                            turn_m(*ahead)
                        if p == 0 and u == 1 and (g > 0 or prev):
                            turn_o(*((now, g - 1) if g > 0 else (prev, QUADS - 1)))
                    for p in range(2):
                        if last[0]:
                            values(*last, p)
                    if nxt:
                        if slot in (3, 4):
                            a_hT(nxt, slot - 3)
                        if slot in PROJ_SLOTS:
                            a_proj(nxt, PROJ_SLOTS.index(slot))
                        if 12 <= slot <= 14:
                            a_v(nxt, slot - 12)
                    if prev:
                        if slot == 0:
                            e_cnt(prev)
                        if slot in (7, 8):
                            e_idx(prev, slot - 7)
                        if slot in (2, 3):
                            c_onT(prev, slot - 2)
                        if slot in (4, 5):
                            c_op(prev, slot - 4)
                        if slot in (9, 10):
                            c_h2T(prev, slot - 9)
                        if slot == 11:
                            c_lg(prev)

            first = batch(0)
            a_hT(first, 0)
            a_hT(first, 1)
            pe.wait_ge(s_wq, 32)
            for j in range(4):
                a_proj(first, j)
            pe.wait_ge(s_par, 16 * 5)
            pe.wait_ge(s_const, NCONST)
            for j in range(3):
                a_v(first, j)
            pe.wait_ge(s_wm2, 16)
            gate_sums()
            pe.wait_ge(s_v0, 9)
            pe.wait_ge(s_ones, 32)
            pe.wait_ge(s_ix2, NSET)
            fills(first, 0, list(range(8)))
            turn_m(first, 0)
            fills(first, 1, FILLS[U - 1])
            loops(pe, body)
            last = batch(B - 1)
            for p in range(2):
                values(last, QUADS - 1, U - 1, p)
            turn_o_last(last)
            e_cnt(last)
            for k in range(C):
                c_onT(last, k, LATE["onT"][k])
            for n in range(2):
                c_op(last, n, LATE["op"][n])
            for k in range(C):
                c_h2T(last, k, LATE["h2T"][k])
            after(pe, "pos", last, 1)
            c_lg(last)
            for t in range(T):
                e_idx_late(last, t)
            e_cnt(batch(B), LATE["cnt"])
            for t in range(T):
                e_idx_late(batch(B), t)
            after(pe, "idx", batch(B), 0)

            pe.wait_ge(s_ix, 1)
            for g in range(G):
                last_t = mm(bC[:, g * 2 * EG:(g + 1) * 2 * EG], spread[:, g].rearrange("p k b -> p (k b)"),
                            own_eh[:, :, :].rearrange("p e h -> p (e h)"), start=True, stop=True)
            last_t.then_inc(s_tabT, 1)

            def turn_x(it, n):
                par = n % 2
                pe.wait_ge(mo["x_ld"][n % 4], (it + n // 4) * 32 + 32)
                need(pe, mo["xTc"], it * 4 + (n - 1))
                need(pe, mo["xTd"], it * 4 + (n - 1))
                if isinstance(it, int) and it == 0 and n == 1:
                    pe.wait_ge(s_ix, 2)
                for k, bank in ((0, bS[par]), (1, bA if par == 0 else bC)):
                    for h in range(2):
                        last = nc.tensor.transpose(bank[:, h * P:(h + 1) * P], xg[n % 4][:, h, k * P:(k + 1) * P], ident[:])
                    last.then_inc(mo["xTp"], 1)

            def expert(it, n):
                par = n % 2
                need(pe, mo["xTc"], it * 4 + (n + 1))
                need(pe, mo["xTd"], it * 4 + (n + 1))
                need(pe, mo["w_ld"][n], it * 48 + 48)
                need(pe, mo["hm"], it * 4 + (n - 1))
                for a in range(2):
                    for k in range(C):
                        last = mm(bST[par][:, a * CAP:(a + 1) * CAP], wgu[n][:, a, k, :], xgT[par][:, k, :],
                                  start=(k == 0), stop=(k == C - 1))
                last.then_inc(mo["gp"], 1)

            def expert_out(it, n):
                par = n % 2
                need(pe, mo["hm"], it * 4 + (n + 1))
                need(pe, mo["yc"], it * 8 + (2 * n - 2))
                yb = bO if par == 0 else bT
                for h in range(2):
                    last = mm(yb[:, h * D:(h + 1) * D], hm[par][:, h * P:(h + 1) * P], wd[n % 4][:], start=True, stop=True)
                last.then_inc(mo["yp"], 1)

            def four(it, first=False, final=False):
                for n in range(4):
                    expert(it, n)
                    if not (final and n == 3):
                        turn_x(it, n + 1)
                    if not (first and n == 0):
                        expert_out(it, n - 1)

            turn_x(0, 0)
            four(0, first=True)
            with pe.Fori(1, E // 4 - 1) as it:
                four(it)
            four(E // 4 - 1, final=True)
            expert_out(E // 4 - 1, 3)

        @block.vector
        def _(dve):
            start_counts(dve, "DVE")
            v = nc.vector

            def a_stats(bt, half):
                ts = range(2 * half, 2 * half + 2)
                if half == 0:
                    dve.wait_ge(x_ld[bt.par], bt.half * 16 + 16)
                for t in ts:
                    v.bn_stats(stats[:, t, :], xt[:, t, :]).then_inc(sems["stats"], 1)
                after(dve, "rstd", bt, 0, apart=True)
                for t in ts:
                    after(dve, "stats", bt, t + 1, apart=True)
                    v.bn_aggr(mv[:, t, :], stats[:, t, :]).then_inc(sems["aggr"], 1)

            def a_mod(bt):
                after(dve, "hT", bt, 0)
                i = bt.b if isinstance(bt.b, int) else None
                src = modT[:, i, :] if i is not None else modT[:, bass.ds(bt.b, 1), :].rearrange("p o n -> p (o n)")
                v.tensor_copy(mcol[:], src).then_inc(sems["mcol"], 1)

            def a_v(bt, j):
                after(dve, "vp", bt, j + 1)
                if not isinstance(bt.b, int) or bt.b >= 2:
                    after(dve, "pv", Batch(bt.b - 1, 0, 0), 0)
                us = slice(2 * j, min(2 * j + 2, U))
                nu = us.stop - us.start
                v.tensor_tensor(Va[bt.par][:, us, :, 0:HD],
                                bA[:, 0:nu * D].rearrange("p (u h d) -> p u h d", u=nu, d=HD),
                                bv[:, :].rearrange("p (h d) -> p h d", d=HD).unsqueeze(1).to_broadcast([P, nu, H, HD]),
                                ALU.add).then_inc(sems["v"], 1)

            def maxima(bt, g, ks):
                for n in ks:
                    t, pr = divmod(n, 2)
                    after(dve, "Sp", bt, 8 * g + n + 1)
                    if n == 0:
                        after(dve, "m2", bt, 2 * g)
                    edge = 0 if t == 0 else 2 if t == T - 1 else 1
                    for i in range(2):
                        at = 2 * (8 * g + n) + i
                        after(dve, "smax", bt, at - 1, apart=True)
                        h = 2 * pr + i
                        ins = v.tensor_tensor_reduce(out=junk[:, i, :], in0=bS[n % 2][:, i * 2 * P:(i + 1) * 2 * P],
                                                     in1=mask[:, edge, :], scale=1.0, scalar=TAKEN, op0=ALU.add,
                                                     op1=ALU.max, accum_out=mrowmax[:, h, t:t + 1])
                        ins.then_inc(sems["smax"], 1)

            def split_m(bt, g):
                after(dve, "mTp", bt, g)
                after(dve, "smax", bt, 16 * (g + 1))
                flat = mrowmax[:, :, :].rearrange("p h t -> p (h t)")
                v.tensor_scalar(M2[:, 0:16], flat, -1.0, None, ALU.mult).then_inc(sems["m2"], 1)
                after(dve, "m2", bt, 2 * g + 1)
                v.scalar_tensor_tensor(M2[:, 16:32], flat, -1.0, M2[:, 0:16], ALU.mult, ALU.subtract
                                       ).then_inc(sems["m2"], 1)

            def norm_o(bt, g):
                after(dve, "oTp", bt, g + 1)
                if g == 0:
                    after(dve, "onTp", bt, 0)
                after(dve, "on", bt, g)
                src = bT[:, :].rearrange("p (t h d) -> p t h d", t=T, d=32)
                v.reciprocal(rec[:], src[:, :, :, HD]).then_inc(sems["rec"], 1)
                after(dve, "rec", bt, g + 1)
                v.tensor_tensor(on[:, :, g * 64:(g + 1) * 64].rearrange("p t (h d) -> p t h d", d=HD), src[:, :, :, 0:HD],
                                rec[:, :, :].unsqueeze(3).to_broadcast([P, T, HQ, HD]), ALU.mult).then_inc(sems["on"], 1)

            def c_x1(bt, n, bank=bC):
                after(dve, "op", bt, n + 1)
                after(dve, "x1_st", bt, 0)
                after(dve, "stats2", bt, 0)
                after(dve, "xb", bt, 2)
                dst = x1[:, 2 * n:2 * n + 2, :]
                v.tensor_tensor(dst, bank[:, :].rearrange("p (t d) -> p t d", t=2),
                                mr[:, 0, :].unsqueeze(1).to_broadcast([P, 2, D]), ALU.mult).then_inc(sems["t1"], 1)
                after(dve, "t1", bt, n + 1)
                v.tensor_tensor(dst, dst, xc[:, 2 * n:2 * n + 2, :], ALU.add).then_inc(sems["x1"], 1)

            def c_stats(bt, half):
                ts = range(2 * half, 2 * half + 2)
                after(dve, "x1", bt, half + 1)
                for t in ts:
                    v.bn_stats(stats2[:, t, :], x1[:, t, :]).then_inc(sems["stats2"], 1)
                after(dve, "rstd2", bt, 0, apart=True)
                for t in ts:
                    after(dve, "stats2", bt, t + 1, apart=True)
                    v.bn_aggr(mv2[:, t, :], stats2[:, t, :]).then_inc(sems["aggr2"], 1)

            def c_norm(bt, k):
                if k == 0:
                    after(dve, "h_st", bt, 0)
                    after(dve, "h2Tp", bt, 0)
                    after(dve, "aggr2", bt, T)
                    for t in range(T):
                        v.scalar_tensor_tensor(xn2[:, t, :], x1[:, t, :], mv2[:, t, 0:1], mr[:, 2, :], ALU.subtract,
                                               ALU.mult).then_inc(sems["xn2"], 1)
                else:
                    after(dve, "rstd2", bt, 2)
                    for t in range(T):
                        after(dve, "xn2", bt, t + 1)
                        v.scalar_tensor_tensor(xn2[:, t, :], xn2[:, t, :], rs2[:, t:t + 1], mr[:, 1, :], ALU.mult,
                                               ALU.add).then_inc(sems["h2"], 1)

            def c_route(bt, part):
                done = [ROUTE_PARTS[part]]

                def step(op, *args, **kw):
                    after(dve, "route", bt, done[0], apart=op in (v.max, v.match_replace))
                    op(*args, **kw).then_inc(sems["route"], 1)
                    done[0] += 1

                hi4, lo4, hi2, q2, r2, lo2 = (pairs[:, i] for i in range(6))
                g4 = gs[:, 3, :].rearrange("p (t g) -> p t g", t=T)
                other = g4.unsqueeze(2).to_broadcast([P, T, G, G])
                own = g4.unsqueeze(3).to_broadcast([P, T, G, G])
                wide = lambda n: gs[:, n, :].unsqueeze(2).to_broadcast([P, T * G, EG])
                per_t = lambda ap: ap.rearrange("p (t e) -> p t e", t=T)

                def pick(t):
                    tt = tmp[:, t * G:(t + 1) * G, :].rearrange("p g e -> p (g e)")
                    rr = rep[:, t * G:(t + 1) * G, :].rearrange("p g e -> p (g e)")
                    step(v.max, top8[:, t, :], tt)
                    step(v.match_replace, rr, top8[:, t, :], tt, TAKEN)

                if part == 0:
                    after(dve, "ex", bt, 1)
                    step(v.tensor_scalar, ex[:], ex[:], 1.0, None, ALU.add)
                    step(v.reciprocal, sc[:], ex[:])
                    step(v.tensor_tensor, sfc[:, :, :].rearrange("p (t g) e -> p t (g e)", t=T), per_t(sc[:, :]),
                         gb[:, :].unsqueeze(1).to_broadcast([P, T, E]), ALU.add)
                elif part == 1:
                    step(v.tensor_tensor, hi4, sfc[:, :, 0:4], sfc[:, :, 4:8], ALU.max)
                    step(v.tensor_tensor, lo4, sfc[:, :, 0:4], sfc[:, :, 4:8], ALU.min)
                    step(v.tensor_tensor, hi2[:, :, 0:2], hi4[:, :, 0:2], hi4[:, :, 2:4], ALU.max)
                    step(v.tensor_tensor, q2[:, :, 0:2], hi4[:, :, 0:2], hi4[:, :, 2:4], ALU.min)
                elif part == 2:
                    step(v.tensor_tensor, r2[:, :, 0:2], lo4[:, :, 0:2], lo4[:, :, 2:4], ALU.max)
                    step(v.tensor_tensor, lo2[:, :, 0:2], q2[:, :, 0:2], r2[:, :, 0:2], ALU.max)
                    step(v.tensor_tensor, gs[:, 0, :], hi2[:, :, 0], hi2[:, :, 1], ALU.max)
                    step(v.tensor_tensor, gs[:, 1, :], hi2[:, :, 0], hi2[:, :, 1], ALU.min)
                elif part == 3:
                    step(v.tensor_tensor, gs[:, 2, :], lo2[:, :, 0], lo2[:, :, 1], ALU.max)
                    step(v.tensor_tensor, gs[:, 1, :], gs[:, 1, :], gs[:, 2, :], ALU.max)
                    step(v.tensor_tensor, gs[:, 3, :], gs[:, 0, :], gs[:, 1, :], ALU.add)
                elif part == 4:
                    step(v.tensor_tensor, cmp1[:], other, own, ALU.is_gt)
                    step(v.tensor_tensor, cmp2[:], other, own, ALU.is_equal)
                    step(v.tensor_tensor, cmp2[:], cmp2[:], lowerg[:, :, :].unsqueeze(1).to_broadcast([P, T, G, G]),
                         ALU.mult)
                elif part == 5:
                    step(v.tensor_tensor, cmp1[:], cmp1[:], cmp2[:], ALU.add)
                    step(v.tensor_reduce, gs[:, 0, :], cmp1[:, :, :, :].rearrange("p t g h -> p (t g) h"), AX_X, ALU.add)
                    step(v.tensor_scalar, gs[:, 1, :], gs[:, 0, :], TG - 0.5, None, ALU.is_lt)
                elif part == 6:
                    step(v.tensor_scalar, gs[:, 2, :], gs[:, 1, :], 1.0, -NEG, ALU.subtract, ALU.mult)
                    step(v.tensor_tensor, tmp[:], sfc[:], wide(1), ALU.mult)
                    step(v.tensor_tensor, tmp[:], tmp[:], wide(2), ALU.add)
                elif part == 7:
                    pick(0)
                    pick(1)
                elif part == 8:
                    pick(2)
                    pick(3)
                elif part == 9:
                    after(dve, "cntp", bt, 1)
                    step(v.tensor_scalar, selb[:], rep[:, :, :].rearrange("p g e -> p (g e)"), TAKEN / 1.5, None, ALU.is_lt)
                    v.tensor_copy(Spre[:, 0, :], Spre[:, T, :]).then_inc(sems["pre"], 1)
                    after(dve, "route", bt, done[0])
                    for t in range(T):
                        after(dve, "pre", bt, t + 1)
                        v.tensor_tensor(Spre[:, t + 1, :], Spre[:, t, :], selb[:, t * E:(t + 1) * E], ALU.add
                                        ).then_inc(sems["pre"], 1)
                elif part == 10:
                    step(v.tensor_tensor, sc[:], sc[:], selb[:], ALU.mult)
                    step(v.tensor_reduce, wsum[:, 0, :], per_t(sc[:, :]), AX_X, ALU.add)
                    step(v.tensor_scalar, wsum[:, 1, :], wsum[:, 0, :], 1e-20, None, ALU.add)
                    step(v.reciprocal, wsum[:, 2, :], wsum[:, 1, :])
                else:
                    step(v.tensor_tensor, per_t(sc[:, :]), per_t(sc[:, :]),
                         wsum[:, 2, :].unsqueeze(2).to_broadcast([P, T, E]), ALU.mult)
                    after(dve, "h_st", bt, 0)
                    step(v.tensor_scalar, H2[:, :, D:HW], per_t(sc[:, :]), ROUTE_SCALE, None, ALU.mult)
                    i = bt.b * T
                    src = valt[:, bass.ds(i, T)] if not isinstance(i, int) else valt[:, i:i + T]
                    v.tensor_copy(vt[:], src).then_inc(sems["vt"], 1)
                assert done[0] == ROUTE_PARTS[part + 1], (part, done[0])

            def e_pos(bt, bank=bC):
                after(dve, "cntp", bt, 1)
                v.scalar_tensor_tensor(posf[:], selb[:], -FAR, bank[:, 0:T * E], ALU.mult, ALU.add).then_inc(sems["pos"], 1)
                after(dve, "pos", bt, 1)
                v.tensor_scalar(posi[:, 0, :], posf[:], FAR, None, ALU.add).then_inc(sems["pos"], 1)
                after(dve, "pos", bt, 2)
                v.tensor_scalar(posi[:, 1, :], posi[:, 0, :], 4, None, ALU.logical_shift_right).then_inc(sems["pos"], 1)
                v.tensor_scalar(posi[:, 2, :], posi[:, 0, :], LO - 1, None, ALU.bitwise_and).then_inc(sems["pos"], 1)

            def e_onehot(bt, t):
                after(dve, "pos", bt, 4)
                after(dve, "vt", bt, 0)
                if isinstance(bt.b, int) and bt.b == B:
                    dve.wait_ge(s_late, 1)
                else:
                    after(dve, "idxp", bt, 0)
                es = slice(t * E, (t + 1) * E)
                digit_of = lambda k: posi[:, k, es].rearrange("p (g e) -> p g e", e=EG).unsqueeze(2).to_broadcast([P, G, LO, EG])
                every = digits[:, :, :].unsqueeze(1).to_broadcast([P, G, LO, EG])
                low = oneh[:, 2 * T]
                after(dve, "oneh", bt, 3 * t)
                v.tensor_tensor(oneh[:, t], digit_of(1), every, ALU.is_equal
                                ).then_inc(sems["oneh"], 1)
                v.tensor_tensor(low, digit_of(2), every, ALU.is_equal
                                ).then_inc(sems["oneh"], 1)
                after(dve, "oneh", bt, 3 * t + 2)
                v.tensor_scalar(oneh[:, T + t], low, vt[:, t:t + 1], None, ALU.mult).then_inc(sems["oneh"], 1)

            def e_idx(bt, half, bank=bC):
                after(dve, "idxp", bt, half + 1)
                dst = iacc[:, half * 4:half * 4 + 4].rearrange("p g e b -> p (g e b)")
                v.tensor_tensor(dst, dst, bank[:, :], ALU.add).then_inc(sems["idx"], 1)

            def body(prev, now, nxt):
                for slot in range(SLOTS):
                    g, u = divmod(slot, U)
                    ahead = ahead_of(now, nxt, g, u)
                    ks = FILLS[u] if ahead[0] else []
                    maxima(*ahead, ks)
                    if u == 2 and ahead[0]:
                        split_m(*ahead)
                    for part in ROUTE_SLOTS.get(slot, []) if prev else []:
                        c_route(prev, part)
                    if u == 1 and (g > 0 or prev):
                        norm_o(*((now, g - 1) if g > 0 else (prev, QUADS - 1)))
                    if nxt:
                        if slot in (0, 1):
                            a_stats(nxt, slot)
                        if slot == 2:
                            a_mod(nxt)
                        if 12 <= slot <= 14:
                            a_v(nxt, slot - 12)
                    if prev:
                        if slot == 1:
                            e_pos(prev)
                        for t in {2: [0], 3: [1, 2], 6: [3]}.get(slot, []):
                            e_onehot(prev, t)
                        if slot in (4, 5):
                            c_x1(prev, slot - 4)
                        if slot in (5, 6):
                            c_stats(prev, slot - 5)
                        if slot in (7, 8):
                            c_norm(prev, slot - 7)
                            e_idx(prev, slot - 7)

            nset = [0]

            def setup(ins):
                ins.then_inc(s_ix2, 1)
                nset[0] += 1

            a_stats(batch(0), 0)
            a_stats(batch(0), 1)
            dve.wait_ge(s_a0, 1)
            v.tensor_scalar(sil[:, 1, :], sil[:, 0, :], 1.0, None, ALU.add).then_inc(s_v0, 1)
            dve.wait_ge(s_v0, 1)
            v.reciprocal(sil[:, 0, :], sil[:, 1, :]).then_inc(s_v0, 1)
            dve.wait_ge(s_v0, 2)
            dve.wait_ge(s_cin, 16)
            v.tensor_tensor(sil[:, 2, :], cin, sil[:, 0, :], ALU.mult).then_inc(s_v0, 1)
            dve.wait_ge(s_pe0, 2)
            v.tensor_copy(silT[:], bA[:, 0:C * B].rearrange("p (c b) -> p c b", c=C)).then_inc(s_v0, 1)
            dve.wait_ge(s_pe0, 3)
            cols = bT[:, 0:4 * B].rearrange("p (n b) -> p b n", n=4)
            v.tensor_copy(modT[:, :, 0:2], cols[:, :, 0:2]).then_inc(s_v0, 1)
            v.tensor_scalar(modT[:, :, 2:4], cols[:, :, 2:4], 1.0, None, ALU.add).then_inc(s_v0, 1)
            dve.wait_ge(s_wq, 32)
            v.tensor_scalar(bqk[:, 0:2], bqk[:, 0:2], SCALE, None, ALU.mult).then_inc(s_v0, 1)
            dve.wait_ge(s_v0, 6)
            a_mod(batch(0))
            for i in range(2):
                setup(v.memset(Ks[i][0:MROW, :, 0:BAND], 0.0))
                setup(v.memset(Ks[i][0:MROW, :, BAND + S:KW], 0.0))
            for j in range(4):
                after(dve, "hpart", batch(0), j + 1)
                if j >= 2:
                    dve.wait_ge(parts_st[j % 2], 16)
                v.tensor_tensor(parts[:, j % 2, 1, :], p32[j % 2][:], parts[:, j % 2, 0, :], ALU.subtract
                                ).then_inc(sems["mpart"], 1)
                after(dve, "r32", batch(0), j + 1)
                after(dve, "mpart", batch(0), j + 1)
                v.tensor_tensor(parts[:, j % 2, 2, :], r32[:], parts[:, j % 2, 1, :], ALU.subtract
                                ).then_inc(sems["lpart"], 1)
            dve.wait_ge(s_par, 16 * 5)
            for j in range(3):
                a_v(batch(0), j)
            dve.wait_ge(s_const, NCONST)
            setup(v.tensor_scalar(bits_e, bits_e, EG - 1, None, ALU.bitwise_and))
            setup(v.tensor_scalar(bits_k, bits_k, P // 2 - EG, None, ALU.bitwise_and))
            setup(v.tensor_scalar(bits_eh, bits_eh, P // 2 + EG - 1, None, ALU.bitwise_and))
            dve.wait_ge(s_ix2, nset[0])
            setup(v.tensor_scalar(own_e[:], bits_e, 0.0, None, ALU.is_equal))
            setup(v.tensor_scalar(own_k[:], bits_k, 0.0, None, ALU.is_equal))
            setup(v.tensor_scalar(own_eh[:], bits_eh, 0.0, None, ALU.is_equal))
            assert nset[0] == NSET
            dve.wait_ge(s_pe0, 6)
            v.tensor_copy(gwT[:], bC[:, 0:C * E].rearrange("p (c e) -> p c e", c=C)).then_inc(s_v0, 1)
            v.tensor_copy(gates[:, 1, 0, :], bS[1][0:B, 0:D]).then_inc(s_v1, 1)
            v.tensor_scalar(gates[:, 1, 1, :], bS[1][0:B, D:2 * D], 1.0, None, ALU.add).then_inc(s_v1, 1)
            gg = gates[:, 0].rearrange("b k d -> b (k d)")
            sgn = sil[:, 0:2, :].rearrange("b k d -> b (k d)")
            v.tensor_copy(gg, bS[0][0:B, :]).then_inc(s_v1, 1)
            dve.wait_ge(s_v1, 3)
            v.tensor_scalar(sgn, gg, 0.0, 2.0, ALU.is_ge, ALU.mult).then_inc(s_v1, 1)
            dve.wait_ge(s_v1, 4)
            v.scalar_tensor_tensor(gg, gg, -1.0, gg, ALU.mult, ALU.max).then_inc(s_v1, 1)
            v.tensor_scalar(sgn, sgn, 1.0, None, ALU.subtract).then_inc(s_v1, 1)
            dve.wait_ge(s_v1, 6)
            v.tensor_scalar(gg, gg, 0.25, None, ALU.max).then_inc(s_v1, 1)
            dve.wait_ge(s_v1, 7)
            v.tensor_tensor(gg, gg, sgn, ALU.mult).then_inc(s_v0, 1)
            maxima(batch(0), 0, list(range(8)))
            split_m(batch(0), 0)
            maxima(batch(0), 1, FILLS[U - 1])
            loops(dve, body)
            last = batch(B - 1)
            norm_o(last, QUADS - 1)
            e_pos(last)
            e_onehot(last, 0)
            e_onehot(last, 1)
            for n in range(2):
                c_x1(last, n, LATE["op"][n])
                c_stats(last, n)
            c_norm(last, 0)
            c_norm(last, 1)
            e_onehot(last, 2)
            e_onehot(last, 3)
            for k in range(12):
                c_route(last, k)
            e_pos(batch(B), LATE["cnt"])
            for t in range(T):
                e_onehot(batch(B), t)
            e_idx(last, 0, LATE["idx"][0])
            e_idx(last, 1, LATE["idx"][1])

            k = [0]

            def step(ins):
                ins.then_inc(s_ix, 1)
                k[0] += 1
                dve.wait_ge(s_ix, k[0])

            after(dve, "idx", batch(B), 0)
            dve.wait_ge(s_zero, 16 * 4 * B)
            dm = own_e[:, :, :].rearrange("p e b -> p (e b)").unsqueeze(1).to_broadcast([P, G, P])
            flat = iacc[:, :, :, :].rearrange("p g e b -> p g (e b)")
            v.tensor_tensor(flat, flat, dm, ALU.mult).then_inc(s_i2, 1)
            dve.wait_ge(s_i2, 1)
            v.tensor_reduce(coded[:], iacc[:, :, :, :].rearrange("p g e b -> p g b e"), AX_X, ALU.add).then_inc(s_i2, 1)
            dve.wait_ge(s_i2, 2)
            step(v.tensor_tensor(spread[:], coded[:, :, :].unsqueeze(2).to_broadcast([P, G, P // LO, LO]),
                                 own_k[:, :, :].unsqueeze(1).to_broadcast([P, G, P // LO, LO]), ALU.mult))
            dve.wait_ge(s_tabT, 1)
            code = bC[:, 0:2 * E]
            v.tensor_scalar(iv[:, 0], code, 0.0, None, ALU.is_lt).then_inc(s_i2, 1)
            dve.wait_ge(s_i2, 3)
            v.tensor_scalar(iv[:, 1], iv[:, 0], -2.0, 1.0, ALU.mult, ALU.add).then_inc(s_i2, 1)
            v.tensor_scalar(iv[:, 2], iv[:, 0], N / 2.0, -1.0, ALU.mult, ALU.add).then_inc(s_i2, 1)
            dve.wait_ge(s_i2, 5)
            step(v.tensor_tensor(iv[:, 1], iv[:, 1], code, ALU.mult))
            v.tensor_tensor(iv[:, 1], iv[:, 1], iv[:, 2], ALU.add).then_inc(s_i2, 1)
            dve.wait_ge(s_i2, 6)
            step(v.tensor_scalar(gidx[:], iv[:, 1], 0.0, None, ALU.max))

            def stage(dst, table, it, n):
                at = it * 8 + 2 * n
                src = table[:, bass.ds(at, 2)] if not isinstance(at, int) else table[:, at:at + 2]
                return v.tensor_copy(dst[:, n % 4, :], src)

            def take_x(it, n):
                need(dve, mo["xTp"], it * 8 + (2 * n + 2))
                need(dve, mo["gp"], it * 4 + (n - 1))
                bank = bA if n % 2 == 0 else bC
                v.tensor_copy(xgT[n % 2][:, 1, :], bank[:, 0:CAP]).then_inc(mo["xTd"], 1)
                need(dve, mo["y_st"][n % 4], (it + n // 4) * 32)
                stage(sstage, sidx, it, n).then_inc(mo["sst"], 1)
                need(dve, mo["yc"], it * 8 + (2 * n - 6))
                need(dve, mo["x_ld"][n % 4], (it + n // 4) * 32 + 32)
                at = it * 4 + (D + n)
                col = bass.ds(at, 1) if not isinstance(at, int) else slice(at, at + 1)
                v.tensor_copy(wcol[n % 4][:, :].unsqueeze(2), xg[n % 4][:, :, col]).then_inc(mo["wc"], 1)

            def hidden(it, n):
                need(dve, mo["sg"], it * 4 + (n + 1))
                need(dve, mo["yp"], it * 4 + (n - 1))
                v.tensor_tensor(hm[n % 2][:], bST[n % 2][:, CAP:2 * CAP], sg[n % 2][:], ALU.mult).then_inc(mo["hm"], 1)

            for n in range(4):
                stage(gstage, gidx, 0, n).then_inc(mo["gst"], 1)
            v.tensor_scalar(iv[:, 0], iv[:, 1], 0.0, None, ALU.is_lt).then_inc(s_i2, 1)
            dve.wait_ge(s_i2, 7)
            v.tensor_tensor(iv[:, 3], iv[:, 0], empty[:, :, :].rearrange("p e h -> p (e h)"), ALU.mult).then_inc(s_i2, 1)
            dve.wait_ge(s_i2, 8)
            step(v.tensor_tensor(sidx[:], iv[:, 3], iv[:, 1], ALU.add))

            def four(it, final=False):
                for n in range(4):
                    if not (final and n == 3):
                        take_x(it, n + 1)
                    if not final:
                        stage(gstage, gidx, it, n + 4).then_inc(mo["gst"], 1)
                    hidden(it, n)

            take_x(0, 0)
            four(0)
            with dve.Fori(1, E // 4 - 1) as it:
                four(it)
            four(E // 4 - 1, final=True)

            dve.wait_ge(s_fx, 32)
            for b in range(B):
                a = fa[b % NF]
                dve.wait_ge(mo["f_ld"][b % NF], 32 * (b // NF + 1))
                v.tensor_tensor(a[:, 0], a[:, 0], a[:, 1], ALU.add).then_inc(mo["fsum"], 1)
                dve.wait_ge(mo["fsum"], 2 * b + 1)
                v.tensor_tensor(a[:, 0], a[:, 0], fg[:, b, :].unsqueeze(1).to_broadcast([P, T, D]), ALU.mult
                                ).then_inc(mo["fsum"], 1)


_INS = ["L0_attn_x", "L0_attn_w_qkv", "L0_attn_b_qkv", "L0_attn_w_out", "L0_attn_b_out", "L0_ffn_gate_w",
        "L0_ffn_gate_bias", "L0_ffn_w_gate", "L0_ffn_w_up", "L0_ffn_w_down", "L0_c", "L0_wmod"]


def kernel(**inputs):
    import numpy as np
    import concourse.bacc as bacc
    from concourse.bass_utils import run_bass_kernel_spmd

    nc = bacc.Bacc("TRN2", target_bir_lowering=False, num_devices=1)
    arrays, args = {}, []
    for name in _INS:
        a = np.ascontiguousarray(inputs[name])
        arrays[name + "_dram"] = a
        args.append(nc.dram_tensor(name + "_dram", a.shape, mybir.dt.from_np(a.dtype), kind="ExternalInput").ap())
    out = nc.dram_tensor("out_dram", (B, S, D), F32, kind="ExternalOutput").ap()
    build(nc, *args, out)
    r = run_bass_kernel_spmd(nc, [arrays], core_ids=[0])
    return r.results[0]["out_dram"]
```
